# Optimizing a Trainium2 kernel written in Bass

```python
import numpy as np
import jax
import jax.numpy as jnp

def _softmax(x, axis=-1):
    return jax.nn.softmax(x, axis=axis)

def _gelu(x):
    return jax.nn.gelu(x, approximate=True)

def _silu(x):
    return jax.nn.silu(x)

def _sigmoid(x):
    return jax.nn.sigmoid(x)

def _layernorm(x, axis=-1, eps=1e-05):
    m = jnp.mean(x, axis=axis, keepdims=True)
    v = jnp.var(x, axis=axis, keepdims=True)
    return (x - m) / jnp.sqrt(v + eps)

def _scatter_add(tgt, idx, src, axis=0):
    return tgt.at[idx].add(src)

def _segment_sum(src, seg, n):
    return jax.ops.segment_sum(src, seg, n)
kernel_name = 'mk_decoder_preln_d1_seqx_r4_d2fc28'

def setup_inputs(seed: int=0):
    np.random.seed(seed)
    _w = jnp.asarray

    def _rec_inputs():
        import jax
        import jax.numpy as jnp
        _rk = jax.random.key(seed)
        x = -0.000125 + 0.9999 * jax.random.normal(jax.random.fold_in(_rk, 1), (16, 256, 512), jnp.float32)
        _lenS = 256 - jax.random.randint(jax.random.fold_in(_rk, 7), (16,), 0, max(1, 256 // 4) + 1, jnp.int32)
        _lenS2 = 256 - jax.random.randint(jax.random.fold_in(_rk, 8), (16,), 0, max(1, 256 // 4) + 1, jnp.int32)
        _ctx_2048P = jax.random.normal(jax.random.fold_in(_rk, 11), (16, 16, 512), jnp.float32)
        _ctx_2048c = jax.random.dirichlet(jax.random.fold_in(_rk, 511), 0.3 * jnp.ones((16,), jnp.float32), (16, 256))
        _ctx_2048t = jnp.einsum('bsk,bkd->bsd', _ctx_2048c, _ctx_2048P)
        _ctx_2048t = _ctx_2048t * jax.lax.rsqrt(jnp.mean(jnp.square(_ctx_2048t)) + 1e-12) * 0.953939
        ctx_2048 = -1.52775e-05 + 0.999936 * (_ctx_2048t + 0.3 * jax.random.normal(jax.random.fold_in(_rk, 611), (16, 256, 512), jnp.float32))
        return (x, ctx_2048)
    x, ctx_2048 = _rec_inputs()

    def _L0_attn_setup():
        import jax, jax.numpy as jnp
        import numpy as np
        B, S, D = (2, 1024, 512)
        EPS = 1e-05

        def rmsnorm(h, scale, eps=EPS):
            hf = h.astype(jnp.float32)
            hf = hf * jax.lax.rsqrt(jnp.mean(hf * hf, axis=-1, keepdims=True) + eps)
            return hf.astype(h.dtype) * scale
        key = jax.random.key(seed)
        kx, kr, kf, kc, ko = jax.random.split(key, 5)
        sc = 1.0 / np.sqrt(D).astype(np.float32)
        return {'x': jax.random.normal(kx, (B, S, D), jnp.float32), 'Wr': jax.random.normal(kr, (D, D), jnp.float32) * sc, 'Wf': jax.random.normal(kf, (D, D), jnp.float32) * sc, 'Wc': jax.random.normal(kc, (D, D), jnp.float32) * sc, 'Wo': jax.random.normal(ko, (D, D), jnp.float32) * sc, 'ln_scale': jnp.ones((D,), jnp.float32)}
    _L0_attn_all = _L0_attn_setup()
    _L0_attn_in = {k: v for k, v in _L0_attn_all.items() if k in ('Wr', 'Wf', 'Wc', 'Wo', 'ln_scale')}
    del _L0_attn_all

    def _L0_xattn_setup():
        import jax, jax.numpy as jnp
        import numpy as np
        B, DIM1, DIM2, LATENT, T = (16, 256, 256, 128, 512)
        LN_EPS = 1e-05
        key = jax.random.key(seed)
        ks = jax.random.split(key, 8)

        def xavier(k, shape):
            fan_out, fan_in = shape
            std = float(np.sqrt(2.0 / (fan_in + fan_out)))
            return jax.random.normal(k, shape, dtype=jnp.float32) * std
        return {'input1': jax.random.normal(ks[0], (B, DIM1, T), dtype=jnp.float32), 'input2': jax.random.normal(ks[1], (B, DIM2, T), dtype=jnp.float32), 'theta_w': xavier(ks[2], (LATENT, DIM2)), 'theta_b': jnp.zeros((LATENT,), jnp.float32), 'phi_w': xavier(ks[3], (LATENT, DIM1)), 'phi_b': jnp.zeros((LATENT,), jnp.float32), 'g_w': xavier(ks[4], (LATENT, DIM1)), 'g_b': jnp.zeros((LATENT,), jnp.float32), 'ln_gamma': jnp.ones((LATENT, T), jnp.float32), 'ln_beta': jnp.zeros((LATENT, T), jnp.float32), 'out_w': xavier(ks[5], (DIM2, LATENT)), 'out_b': jnp.zeros((DIM2,), jnp.float32)}
    _L0_xattn_all = _L0_xattn_setup()
    _L0_xattn_in = {k: v for k, v in _L0_xattn_all.items() if k in ('theta_w', 'theta_b', 'phi_w', 'phi_b', 'g_w', 'g_b', 'ln_gamma', 'ln_beta', 'out_w', 'out_b')}
    del _L0_xattn_all

    def _L0_ffn_setup():
        import jax, jax.numpy as jnp
        import numpy as np
        LN_EPS = 1e-05
        Q_EPS = 1e-05

        def ternary_quantize(w):
            scale = jnp.mean(jnp.abs(w))
            return jnp.clip(jnp.round(w / (scale + Q_EPS)), -1.0, 1.0)

        def layernorm(x, gamma, beta):
            mu = jnp.mean(x, axis=-1, keepdims=True)
            var = jnp.mean(jnp.square(x - mu), axis=-1, keepdims=True)
            return (x - mu) * jax.lax.rsqrt(var + LN_EPS) * gamma + beta
        key = jax.random.key(seed)
        k_x, k_w = jax.random.split(key)
        B, S, D_IN, D_OUT = (4, 512, 512, 512)
        x = jax.random.normal(k_x, (B, S, D_IN), dtype=jnp.float32)
        std = np.sqrt(2.0 / D_OUT).astype(np.float32)
        weight = jax.random.normal(k_w, (D_OUT, D_IN), dtype=jnp.float32) * std
        bias = jnp.zeros((D_OUT,), dtype=jnp.float32)
        ln_gamma = jnp.ones((D_IN,), dtype=jnp.float32)
        ln_beta = jnp.zeros((D_IN,), dtype=jnp.float32)
        return {'x': x, 'weight': weight, 'bias': bias, 'ln_gamma': ln_gamma, 'ln_beta': ln_beta}
    _L0_ffn_all = _L0_ffn_setup()
    _L0_ffn_in = {k: v for k, v in _L0_ffn_all.items() if k in ('weight', 'bias', 'ln_gamma', 'ln_beta')}
    del _L0_ffn_all
    return {'x': x, 'ctx_2048': ctx_2048, 'L0_attn_Wr': _L0_attn_in['Wr'], 'L0_attn_Wf': _L0_attn_in['Wf'], 'L0_attn_Wc': _L0_attn_in['Wc'], 'L0_attn_Wo': _L0_attn_in['Wo'], 'L0_attn_ln_scale': _L0_attn_in['ln_scale'], 'L0_xattn_theta_w': _L0_xattn_in['theta_w'], 'L0_xattn_theta_b': _L0_xattn_in['theta_b'], 'L0_xattn_phi_w': _L0_xattn_in['phi_w'], 'L0_xattn_phi_b': _L0_xattn_in['phi_b'], 'L0_xattn_g_w': _L0_xattn_in['g_w'], 'L0_xattn_g_b': _L0_xattn_in['g_b'], 'L0_xattn_ln_gamma': _L0_xattn_in['ln_gamma'], 'L0_xattn_ln_beta': _L0_xattn_in['ln_beta'], 'L0_xattn_out_w': _L0_xattn_in['out_w'], 'L0_xattn_out_b': _L0_xattn_in['out_b'], 'L0_ffn_weight': _L0_ffn_in['weight'], 'L0_ffn_bias': _L0_ffn_in['bias'], 'L0_ffn_ln_gamma': _L0_ffn_in['ln_gamma'], 'L0_ffn_ln_beta': _L0_ffn_in['ln_beta']}

def reference(x, ctx_2048, L0_attn_Wr, L0_attn_Wf, L0_attn_Wc, L0_attn_Wo, L0_attn_ln_scale, L0_xattn_theta_w, L0_xattn_theta_b, L0_xattn_phi_w, L0_xattn_phi_b, L0_xattn_g_w, L0_xattn_g_b, L0_xattn_ln_gamma, L0_xattn_ln_beta, L0_xattn_out_w, L0_xattn_out_b, L0_ffn_weight, L0_ffn_bias, L0_ffn_ln_gamma, L0_ffn_ln_beta):
    import jax
    import jax.numpy as jnp

    def _L0_attn_ref(x, Wr, Wf, Wc, Wo, ln_scale):
        import jax, jax.numpy as jnp
        import numpy as np
        B, S, D = (2, 1024, 512)
        EPS = 1e-05

        def rmsnorm(h, scale, eps=EPS):
            hf = h.astype(jnp.float32)
            hf = hf * jax.lax.rsqrt(jnp.mean(hf * hf, axis=-1, keepdims=True) + eps)
            return hf.astype(h.dtype) * scale
        r = jax.nn.silu(x @ Wr)
        f = jax.nn.sigmoid(x @ Wf)
        c = jax.nn.silu(x @ Wc)

        def combine(a, b):
            fa, ca = a
            fb, cb = b
            return (fa * fb, fb * ca + (1.0 - fb) * cb)
        _, h = jax.lax.associative_scan(combine, (f, c), axis=1)
        y = r * rmsnorm(h, ln_scale) @ Wo
        return y

    def _L0_xattn_ref(input1, input2, theta_w, theta_b, phi_w, phi_b, g_w, g_b, ln_gamma, ln_beta, out_w, out_b):
        import jax, jax.numpy as jnp
        import numpy as np
        B, DIM1, DIM2, LATENT, T = (16, 256, 256, 128, 512)
        LN_EPS = 1e-05
        theta_x = jnp.einsum('ld,bdt->btl', theta_w, input2) + theta_b
        phi_x = jnp.einsum('ld,bdt->blt', phi_w, input1) + phi_b[:, None]
        scores = jnp.einsum('btl,bls->bts', theta_x, phi_x)
        p = jax.nn.softmax(scores, axis=-1)
        g_x = jnp.einsum('ld,bdt->btl', g_w, input1) + g_b
        t_x = jnp.einsum('bts,bsl->blt', p, g_x)
        mu = jnp.mean(t_x, axis=(1, 2), keepdims=True)
        var = jnp.var(t_x, axis=(1, 2), keepdims=True)
        h = (t_x - mu) * jax.lax.rsqrt(var + LN_EPS) * ln_gamma + ln_beta
        h = jax.nn.relu(h)
        w_t = jnp.einsum('ol,blt->bot', out_w, h) + out_b[None, :, None]
        return w_t + input2

    def _L0_ffn_ref(x, weight, bias, ln_gamma, ln_beta):
        import jax, jax.numpy as jnp
        import numpy as np
        LN_EPS = 1e-05
        Q_EPS = 1e-05

        def ternary_quantize(w):
            scale = jnp.mean(jnp.abs(w))
            return jnp.clip(jnp.round(w / (scale + Q_EPS)), -1.0, 1.0)

        def layernorm(x, gamma, beta):
            mu = jnp.mean(x, axis=-1, keepdims=True)
            var = jnp.mean(jnp.square(x - mu), axis=-1, keepdims=True)
            return (x - mu) * jax.lax.rsqrt(var + LN_EPS) * gamma + beta
        xn = layernorm(x, ln_gamma, ln_beta)
        w_q = ternary_quantize(weight)
        return jnp.einsum('bsi,oi->bso', xn, w_q) + bias
    x = x + _L0_attn_ref(_layernorm(x, axis=-1), L0_attn_Wr, L0_attn_Wf, L0_attn_Wc, L0_attn_Wo, L0_attn_ln_scale)
    x = x + _L0_xattn_ref(_layernorm(x, axis=-1), ctx_2048, L0_xattn_theta_w, L0_xattn_theta_b, L0_xattn_phi_w, L0_xattn_phi_b, L0_xattn_g_w, L0_xattn_g_b, L0_xattn_ln_gamma, L0_xattn_ln_beta, L0_xattn_out_w, L0_xattn_out_b)
    x = x + _L0_ffn_ref(_layernorm(x, axis=-1), L0_ffn_weight, L0_ffn_bias, L0_ffn_ln_gamma, L0_ffn_ln_beta)
    return x

_drawn_inputs = setup_inputs


def setup_inputs(seed=0):
    import zlib

    import numpy as np

    out = dict(_drawn_inputs(seed))
    spreads = {'L0_attn_ln_scale': (1.0, 0.2),
     'L0_xattn_theta_b': (0.0, 0.1),
     'L0_xattn_phi_b': (0.0, 0.8),
     'L0_xattn_g_b': (0.0, 0.338),
     'L0_xattn_ln_gamma': (1.0, 0.2),
     'L0_xattn_ln_beta': (0.0, 0.1),
     'L0_xattn_out_b': (0.0, 0.8),
     'L0_ffn_bias': (0.0, 0.8),
     'L0_ffn_ln_gamma': (1.0, 0.2),
     'L0_ffn_ln_beta': (0.0, 0.1)}
    factors = {}
    for name, (base, spread) in spreads.items():
        noise = np.random.default_rng([zlib.crc32(name.encode()), seed]).standard_normal(out[name].shape)
        drawn = base * np.exp(spread * noise) if base else spread * noise
        out[name] = jnp.asarray(drawn.astype(out[name].dtype))
    for name, factor in factors.items():
        out[name] = (out[name] * factor).astype(out[name].dtype)
    return out
```

```python
from contextlib import ExitStack

import concourse.bass as bass
from concourse import mybir

F32 = mybir.dt.float32
F32R = mybir.dt.float32r
ALU = mybir.AluOpType
ACT = mybir.ActivationFunctionType
AX = mybir.AxisListType

P = 128
EPS = 1e-5
Q_EPS = 1e-5


def need(eng, sem, value):
    if not isinstance(value, int) or value > 0:
        eng.wait_ge(sem, value)


def f32(ap):
    return ap.bitcast(F32)


def build(nc, x, ctx_in, wr, wf, wc, wo, ln_scale, theta_w, theta_b, phi_w, phi_b, g_w, g_b,
          ln_gamma, ln_beta, out_w, out_b, ffn_w, ffn_bias, ffn_gamma, ffn_beta, out):
    B, S, D = x.shape
    L = theta_w.shape[0]
    PAIRS = B // 2
    KT = D // P
    LEVELS = S.bit_length() - 1
    TREE = 1 + 4 * (LEVELS - 1) + 2 + 2 * (LEVELS - 1)
    assert S == 1 << LEVELS
    ST = S // P
    QT = 2 * ST
    assert L == P and D == 512 and S == 256 and B % 2 == 0 and PAIRS >= 3

    x_rows = x.rearrange("b (s p) d -> p (b s) d", p=P)
    ctx_rows = ctx_in.rearrange("b (s p) d -> p (b s) d", p=P)
    out_rows = out.rearrange("b (s p) d -> p (b s) d", p=P)

    stack = ExitStack()
    with stack:
        def sb(name, shape, dt=F32):
            return stack.enter_context(nc.sbuf_tensor(name, shape, dt))

        def sem(name):
            return stack.enter_context(nc.semaphore(name))

        ident = sb("ident", [P, P])
        avg = sb("avg", [P, P])
        ones = sb("ones", [P, P])
        minus_half = sb("minus_half", [P, 4])
        w_hi = [sb(f"w{m}_hi", [P, KT, D], F32R) for m in "rfc"]
        w_lo = [sb(f"w{m}_lo", [P, KT, D], F32R) for m in "rfc"]
        wo_hi = sb("wo_hi", [P, KT, D], F32R)
        wo_lo = sb("wo_lo", [P, KT, D], F32R)
        wq = sb("wq", [P, KT, D], F32R)
        pj_hi = sb("pj_hi", [P, 4, 2 * P], F32R)
        pj_lo = sb("pj_lo", [P, 4, 2 * P], F32R)
        gamma_lt = sb("gamma_lt", [P, D])
        beta_lt = sb("beta_lt", [P, D])
        gamma_bc = sb("gamma_bc", [P, D])
        bias_bc = sb("bias_bc", [P, D])
        cols = sb("cols", [P, 16])
        theta_bc, phi_bc, g_bc = cols[:, 0:1], cols[:, 1:2], cols[:, 2:3]
        out_bc, scale_bc, beta_c = cols[:, 3:5], cols[:, 5:9], cols[:, 9:13]
        thr, neg_thr, abs_sum = cols[:, 13:14], cols[:, 14:15], cols[:, 15:16]
        brow = sb("brow", [1, D])

        x_in = sb("x_in", [P, QT, D])
        xt_hi = sb("xt_hi", [P, KT, D], F32R)
        xt_lo = sb("xt_lo", [P, KT, D], F32R)
        tr = sb("tr", [P, D])
        tf = sb("tf", [P, D])
        tc = sb("tc", [P, D])
        fg = sb("fg", [P, D])
        gg = sb("gg", [P, D])
        tt = sb("tt", [P, 2, S // 2])
        hsq = sb("hsq", [P, D])
        rh_hi = sb("rh_hi", [P, KT, D], F32R)
        rh_lo = sb("rh_lo", [P, KT, D], F32R)
        res = sb("res", [P, QT, D])
        cx = sb("cx", [P, ST, D])
        fin = sb("fin", [P, ST, D])
        cz_hi = sb("cz_hi", [P, 2 * D], F32R)
        cz_lo = sb("cz_lo", [P, 2 * D], F32R)
        th_hi = sb("th_hi", [P, D], F32R)
        th_lo = sb("th_lo", [P, D], F32R)
        ph_hi = sb("ph_hi", [P, D], F32R)
        ph_lo = sb("ph_lo", [P, D], F32R)
        gt = sb("gt", [P, D])
        g_hi = sb("g_hi", [P, KT, P], F32R)
        g_lo = sb("g_lo", [P, KT, P], F32R)
        prob = sb("prob", [P, KT, D])
        fz = prob[:, 0:ST, :]
        pt_hi = sb("pt_hi", [P, KT, D], F32R)
        pt_lo = sb("pt_lo", [P, KT, D], F32R)
        beta_w = fin[:, 1, :]
        fx_hi, fx_lo = pt_hi[:, 0:ST, :], pt_lo[:, 0:ST, :]
        a_raw = sb("a_raw", [P, QT, 6])
        a_mv = sb("a_mv", [P, QT, 2])
        a_ve = sb("a_ve", [P, QT])
        a_rstd = sb("a_rstd", [P, QT])
        a_nb = sb("a_nb", [P, QT])
        m_ve = sb("m_ve", [P, QT])
        m_rstd = sb("m_rstd", [P, QT])
        b_raw = sb("b_raw", [P, ST, 6])
        b_mv = sb("b_mv", [P, ST, 2])
        b_ve = sb("b_ve", [P, ST])
        b_rstd = sb("b_rstd", [P, ST])
        b_nb = sb("b_nb", [P, ST])
        c_raw = sb("c_raw", [P, ST, 6])
        c_mv = sb("c_mv", [P, ST, 2])
        c_ve = sb("c_ve", [P, ST])
        c_rstd = sb("c_rstd", [P, ST])
        nmax = sb("nmax", [P, KT])
        rsum = sb("rsum", [P, KT])
        rinv = sb("rinv", [P, KT])
        t_raw = sb("t_raw", [P, 6])
        t_mv = sb("t_mv", [P, 2])
        t_s = sb("t_s", [P, 6])

        Z = [stack.enter_context(nc.psum_tensor(f"z{m}", [P, D], F32)) for m in "rfc"]
        W = [stack.enter_context(nc.psum_tensor(f"work{n}", [P, D], F32)) for n in range(5)]

        x_here = sem("x_here")
        res_here = [sem(f"res_here_{b}") for b in range(2)]
        ctx_here = sem("ctx_here")
        stored = sem("stored")
        w_here = [sem(f"w{m}_here") for m in "rfco"]
        q_here = sem("q_here")
        pj_here = sem("pj_here")
        small_here = sem("small_here")
        ident_zero = sem("ident_zero")
        const_done = sem("const_done")
        w_hi_done = sem("w_hi_done")
        w_lo_done = sem("w_lo_done")
        col_done = sem("col_done")
        abs_done = sem("abs_done")
        abs_mean = sem("abs_mean")
        thr_done = sem("thr_done")
        below_done = sem("below_done")
        q_done = sem("q_done")
        q_t = sem("q_t")
        wq_done = sem("wq_done")
        beta_done = sem("beta_done")
        bias_mm = sem("bias_mm")
        bias_done = sem("bias_done")
        pj_t = sem("pj_t")
        pj_hi_done = sem("pj_hi_done")
        pj_lo_done = sem("pj_lo_done")
        a_raw_done = sem("a_raw_done")
        a_mv_done = sem("a_mv_done")
        a_ve_done = sem("a_ve_done")
        a_rstd_done = sem("a_rstd_done")
        a_nb_done = sem("a_nb_done")
        xn_done = sem("xn_done")
        xt_mm = sem("xt_mm")
        xt_hi_done = sem("xt_hi_done")
        xt_lo_done = sem("xt_lo_done")
        z_mm = sem("z_mm")
        tr_done = sem("tr_done")
        tf_done = sem("tf_done")
        tc_done = sem("tc_done")
        r_done = sem("r_done")
        f_done = sem("f_done")
        c_done = sem("c_done")
        tree_done = sem("tree_done")
        sq_done = sem("sq_done")
        hsq_done = sem("hsq_done")
        rh_done = sem("rh_done")
        rh_hi_done = sem("rh_hi_done")
        rh_lo_done = sem("rh_lo_done")
        hsq_mm = sem("hsq_mm")
        m_ve_done = sem("m_ve_done")
        m_rstd_done = sem("m_rstd_done")
        wo_mm = sem("wo_mm")
        x1_done = sem("x1_done")
        b_raw_done = sem("b_raw_done")
        b_mv_done = sem("b_mv_done")
        b_ve_done = sem("b_ve_done")
        b_rstd_done = sem("b_rstd_done")
        b_nb_done = sem("b_nb_done")
        fn_done = sem("fn_done")
        fx_hi_done = sem("fx_hi_done")
        fx_lo_done = sem("fx_lo_done")
        ctx_hi_done = sem("ctx_hi_done")
        ctx_lo_done = sem("ctx_lo_done")
        cx_done = sem("cx_done")
        g_mm = sem("g_mm")
        ph_mm = sem("ph_mm")
        th_mm = sem("th_mm")
        gt_done = sem("gt_done")
        ph_hi_done = sem("ph_hi_done")
        ph_lo_done = sem("ph_lo_done")
        th_hi_done = sem("th_hi_done")
        th_lo_done = sem("th_lo_done")
        g_t = sem("g_t")
        g_hi_done = sem("g_hi_done")
        g_lo_done = sem("g_lo_done")
        score_mm = sem("score_mm")
        nmax_done = sem("nmax_done")
        exp_done = sem("exp_done")
        rinv_done = sem("rinv_done")
        prob_done = sem("prob_done")
        prob_t = sem("prob_t")
        pt_hi_done = sem("pt_hi_done")
        pt_lo_done = sem("pt_lo_done")
        av_mm = sem("av_mm")
        t_raw_done = sem("t_raw_done")
        t_mv_done = sem("t_mv_done")
        t_mean_done = sem("t_mean_done")
        mean_mm = sem("mean_mm")
        t_dist_done = sem("t_dist_done")
        t_sec_done = sem("t_sec_done")
        sec_mm = sem("sec_mm")
        t_ve_done = sem("t_ve_done")
        t_rstd_done = sem("t_rstd_done")
        t_gam_done = sem("t_gam_done")
        t_bet_done = sem("t_bet_done")
        relu_hi_done = sem("relu_hi_done")
        relu_lo_done = sem("relu_lo_done")
        out_mm = sem("out_mm")
        x2_done = sem("x2_done")
        c_raw_done = sem("c_raw_done")
        c_mv_done = sem("c_mv_done")
        c_ve_done = sem("c_ve_done")
        c_rstd_done = sem("c_rstd_done")
        zg_done = sem("zg_done")
        fin_done = sem("fin_done")
        zg_t = sem("zg_t")
        z_hi_done = sem("z_hi_done")
        z_lo_done = sem("z_lo_done")
        ffn_mm = sem("ffn_mm")
        x3_done = sem("x3_done")

        def level(tile, start, step):
            return tile[:, :].rearrange("p (b n) -> p b n", n=S)[:, :, start:S:step]

        def tree(t, e):
            return t * (KT * TREE) + e * TREE

        block = stack.enter_context(nc.Block())

        def store(eng, n):
            need(eng, x3_done, n * ST + ST)
            eng.dma_start(out_rows[:, bass.ds(n * ST, ST), :], fin[:, :, :]).then_inc(stored, 16)

        @block.sync
        def _(sp):
            def load_x(t):
                need(sp, xt_mm, t * KT)
                sp.dma_start(x_in[:, :, :], x_rows[:, bass.ds(t * QT, QT), :]).then_inc(x_here, 16)

            def load_res(t, b):
                n = t * 2 + (b - 2)
                if not isinstance(t, int) or t > 0:
                    need(sp, fin_done, n * ST + ST)
                    need(sp, zg_done, n * ST + ST)
                sp.dma_start(res[:, b * ST:(b + 1) * ST, :],
                             x_rows[:, bass.ds(t * QT + b * ST, ST), :]).then_inc(res_here[b], 16)

            def load_ctx(n):
                need(sp, x2_done, n * ST)
                sp.dma_start(cx[:, :, :], ctx_rows[:, bass.ds(n * ST, ST), :]).then_inc(ctx_here, 16)

            load_x(0)
            rows = lambda w: w.rearrange("(k p) n -> p k n", p=P)
            sp.dma_start(res[:, :, :], rows(wr)).then_inc(w_here[0], 16)
            sp.dma_start(prob[:, :, :], rows(wf)).then_inc(w_here[1], 16)
            sp.dma_start(cx[:, :, :], rows(wc)[:, 0:2, :]).then_inc(w_here[2], 16)
            sp.dma_start(fin[:, :, :], rows(wc)[:, 2:4, :]).then_inc(w_here[2], 16)
            sp.wait_ge(w_lo_done, 3 * KT)
            sp.dma_start(prob[:, :, :], rows(ffn_w)).then_inc(q_here, 16)
            for n, w in enumerate((theta_w, phi_w, g_w)):
                sp.dma_start(cx[:, 0, 0:256] if n == 0 else cx[:, n // 2, (n % 2) * 256:(n % 2) * 256 + 256],
                             w).then_inc(pj_here, 16)
            sp.dma_start(fin[:, 0, 0:256].rearrange("p (o l) -> p o l", o=2), rows(out_w)).then_inc(pj_here, 16)
            sp.dma_start(res[:, :, :], rows(wo)).then_inc(w_here[3], 16)
            sp.dma_start(gamma_bc[:, :], ffn_gamma.rearrange("(a d) -> a d", a=1).to_broadcast([P, D]))\
              .then_inc(small_here, 16)
            sp.dma_start(gamma_lt[:, :], ln_gamma).then_inc(small_here, 16)
            sp.dma_start(beta_lt[:, :], ln_beta).then_inc(small_here, 16)
            load_x(1)
            sp.wait_ge(w_lo_done, 4 * KT)
            load_res(0, 0)
            load_res(0, 1)
            sp.wait_ge(pj_lo_done, 2)
            load_ctx(0)

            def step(i, load_next):
                load_ctx(i * 2 - 1)
                if load_next:
                    load_x(i + 1)
                load_res(i, 0)
                store(sp, i * 2 - 2)
                load_ctx(i * 2)
                load_res(i, 1)
                store(sp, i * 2 - 1)

            with sp.Fori(1, PAIRS - 1) as i:
                step(i, True)
            step(PAIRS - 1, False)
            load_ctx(2 * PAIRS - 1)
            store(sp, 2 * PAIRS - 2)
            store(sp, 2 * PAIRS - 1)
            sp.wait_ge(stored, 16 * B)

        @block.gpsimd
        def _(pool):
            pool.memset(ident[:, :], 0.0).then_inc(ident_zero, 1)
            pool.memset(avg[:, :], 1.0 / P).then_inc(const_done, 1)
            pool.memset(ones[:, :], 1.0).then_inc(const_done, 1)
            pool.memset(minus_half[:, :], -0.5).then_inc(const_done, 1)
            pool.wait_ge(ident_zero, 1)
            pool.affine_select(out=ident[:, :], in_=ident[:, :], compare_op=ALU.not_equal, fill=1.0,
                               base=0, pattern=[[-1, P]], channel_multiplier=1).then_inc(const_done, 1)
            pool.wait_ge(const_done, 4)

            def rsqrt(out_ap, in_ap, width, done):
                pool.tensor_tensor(out_ap, in_ap, minus_half[:, 0:width], ALU.pow).then_inc(done, 1)

            def norm_x(t):
                pool.wait_ge(a_ve_done, t + 1)
                need(pool, xn_done, t * QT)
                rsqrt(a_rstd[:, :], a_ve[:, :], QT, a_rstd_done)

            def gate_rh(t, e):
                pool.wait_ge(tree_done, tree(t, e + 1))
                pool.wait_ge(r_done, t * KT + (e + 1))
                pool.tensor_tensor(tr[:, :], tr[:, :], tc[:, :], ALU.mult).then_inc(rh_done, 1)

            def sum_sq(t, e):
                pool.wait_ge(sq_done, t * KT + (e + 1))
                need(pool, hsq_done, t * (KT - 1) + (e - 1))
                pool.tensor_tensor(hsq[:, :], hsq[:, :], fg[:, :], ALU.add).then_inc(hsq_done, 1)

            def norm_m(t):
                pool.wait_ge(m_ve_done, t + 1)
                need(pool, x1_done, t * QT)
                rsqrt(m_rstd[:, :], m_ve[:, :], QT, m_rstd_done)

            def norm_b(n):
                pool.wait_ge(b_ve_done, n + 1)
                need(pool, fn_done, n * ST)
                rsqrt(b_rstd[:, :], b_ve[:, :], ST, b_rstd_done)

            def ctx_low(n):
                pool.wait_ge(ctx_hi_done, n + 1)
                pool.tensor_tensor(cz_lo[:, :].rearrange("p (s d) -> p s d", s=ST), cx[:, :, :],
                                   f32(cz_hi[:, :]).rearrange("p (s d) -> p s d", s=ST), ALU.subtract)\
                    .then_inc(ctx_lo_done, 1)

            def ctx_plus(n, b):
                pool.wait_ge(ctx_lo_done, n + 1)
                pool.wait_ge(x1_done, n * ST + ST)
                pool.tensor_tensor(cx[:, :, :], cx[:, :, :], res[:, b * ST:(b + 1) * ST, :], ALU.add)\
                    .then_inc(cx_done, 1)

            def norm_t(n):
                pool.wait_ge(t_ve_done, n + 1)
                rsqrt(t_s[:, 5:6], t_s[:, 4:5], 1, t_rstd_done)

            def norm_c(n):
                pool.wait_ge(c_ve_done, n + 1)
                need(pool, x3_done, n * ST)
                rsqrt(c_rstd[:, :], c_ve[:, :], ST, c_rstd_done)

            def fin_sum(n, b):
                pool.wait_ge(x2_done, n * ST + ST)
                need(pool, stored, n * 16)
                for s in range(ST):
                    pool.tensor_tensor(fin[:, s, :], res[:, b * ST + s, :], bias_bc[:, :], ALU.add)\
                        .then_inc(fin_done, 1)

            def e_tile(t, e):
                gate_rh(t, e)
                if e:
                    sum_sq(t, e)

            def back(i, b, gates):
                n = i * 2 + (b - 2)
                if b == 1:
                    norm_b(n)
                    ctx_low(n)
                    ctx_plus(n, b)
                else:
                    ctx_low(n)
                    ctx_plus(n, b)
                if gates and b == 0:
                    e_tile(i, 0)
                norm_t(n)
                if gates and b == 1:
                    e_tile(i, 2)
                norm_c(n)
                fin_sum(n, b)
                if gates:
                    e_tile(i, 2 * b + 1)

            norm_x(0)
            for e in range(KT - 1):
                e_tile(0, e)
            norm_x(1)
            e_tile(0, KT - 1)
            norm_m(0)
            pool.wait_ge(bias_done, 1)
            norm_b(0)

            def step(i, load_next):
                back(i, 0, True)
                if load_next:
                    norm_x(i + 1)
                back(i, 1, True)
                norm_m(i)
                norm_b(i * 2)

            with pool.Fori(1, PAIRS - 1) as i:
                step(i, True)
            step(PAIRS - 1, False)
            back(PAIRS, 0, False)
            back(PAIRS, 1, False)

        @block.scalar
        def _(act):
            col = lambda v: v.rearrange("(k p) -> p k", p=P)
            with nc.allow_non_contiguous_dma(reason="vectors of a few hundred elements, once"):
                for dst, src in ((theta_bc, theta_b), (phi_bc, phi_b), (g_bc, g_b), (out_bc, out_b),
                                 (scale_bc, ln_scale), (beta_c, ffn_beta)):
                    act.dma_start(dst, col(src)).then_inc(small_here, 16)
            act.dma_start(brow[:, :], ffn_bias.rearrange("(a d) -> a d", a=1)).then_inc(small_here, 16)

            def norm_x(t):
                act.wait_ge(a_nb_done, t + 1)
                for q in range(QT):
                    act.activation(x_in[:, q, :], x_in[:, q, :], ACT.Identity, bias=a_nb[:, q:q + 1],
                                   scale=a_rstd[:, q:q + 1]).then_inc(xn_done, 1)

            def xt_high(t):
                need(act, z_mm, t * 3 * KT)
                for k in range(KT):
                    act.wait_ge(xt_mm, t * KT + (k + 1))
                    act.activation(xt_hi[:, k, :], W[k][:, :], ACT.Copy).then_inc(xt_hi_done, 1)

            def gate_r(t, e):
                act.wait_ge(z_mm, t * 3 * KT + (3 * e + 1))
                need(act, rh_lo_done, t * KT + e)
                act.activation(tr[:, :], Z[0][:, :], ACT.Tanh, scale=0.5).then_inc(tr_done, 1)

            def gate_f(t, e):
                act.wait_ge(z_mm, t * 3 * KT + (3 * e + 2))
                need(act, f_done, t * KT + e)
                act.activation(tf[:, :], Z[1][:, :], ACT.Tanh, scale=0.5).then_inc(tf_done, 1)

            def forget(t, e):
                act.wait_ge(tf_done, t * KT + (e + 1))
                need(act, hsq_done, t * (KT - 1) + (e - 1))
                need(act, tree_done, tree(t, e))
                act.activation(fg[:, :], tf[:, :], ACT.Copy, bias=0.5, scale=0.5).then_inc(f_done, 1)

            def gate_c(t, e):
                act.wait_ge(z_mm, t * 3 * KT + (3 * e + 3))
                need(act, rh_done, t * KT + e)
                need(act, sq_done, t * KT + e)
                act.activation(tc[:, :], Z[2][:, :], ACT.Tanh, scale=0.5).then_inc(tc_done, 1)

            def square(t, e):
                act.wait_ge(tree_done, tree(t, e + 1))
                if e == 0:
                    need(act, hsq_mm, t)
                    act.activation(hsq[:, :], tc[:, :], ACT.Square).then_inc(sq_done, 1)
                else:
                    act.activation(fg[:, :], tc[:, :], ACT.Square).then_inc(sq_done, 1)

            def rh_high(t, e):
                act.wait_ge(rh_done, t * KT + (e + 1))
                need(act, wo_mm, t * QT)
                act.activation(rh_hi[:, e, :], tr[:, :], ACT.Copy).then_inc(rh_hi_done, 1)

            def norm_f(n, b):
                act.wait_ge(b_nb_done, n + 1)
                need(act, zg_t, n * 2)
                for s in range(ST):
                    act.activation(fz[:, s, :], res[:, b * ST + s, :], ACT.Identity,
                                   bias=b_nb[:, s:s + 1], scale=b_rstd[:, s:s + 1]).then_inc(fn_done, 1)
                need(act, av_mm, n)
                act.wait_ge(fn_done, n * ST + ST)
                act.activation(fx_hi, fz, ACT.Copy).then_inc(fx_hi_done, 1)

            def ctx_high(n):
                act.wait_ge(ctx_here, n * 16 + 16)
                need(act, ffn_mm, n * ST)
                act.activation(cz_hi[:, :].rearrange("p (s d) -> p s d", s=ST), cx[:, :, :], ACT.Copy)\
                   .then_inc(ctx_hi_done, 1)

            def proj_high(n):
                act.wait_ge(g_mm, n + 1)
                need(act, relu_lo_done, n)
                act.activation(gt[:, :], W[2][:, :], ACT.Copy).then_inc(gt_done, 1)
                act.wait_ge(ph_mm, n + 1)
                act.activation(ph_hi[:, :], W[1][:, :], ACT.Identity, bias=phi_bc).then_inc(ph_hi_done, 1)
                act.wait_ge(th_mm, n + 1)
                need(act, out_mm, n * ST)
                act.activation(th_hi[:, :], W[0][:, :], ACT.Identity, bias=theta_bc).then_inc(th_hi_done, 1)

            def g_high(n):
                act.wait_ge(g_t, n + 1)
                act.activation(g_hi[:, :, :].rearrange("p j l -> p (j l)"), W[3][:, :], ACT.Copy)\
                   .then_inc(g_hi_done, 1)

            def exps(n):
                act.wait_ge(fx_lo_done, n + 1)
                for k in range(KT):
                    act.wait_ge(nmax_done, n * KT + (k + 1))
                    act.activation(prob[:, k, :], W[k][:, :], ACT.Exp, bias=nmax[:, k:k + 1],
                                   accum_out=rsum[:, k:k + 1]).then_inc(exp_done, 1)

            def pt_high(n):
                for k in range(KT):
                    act.wait_ge(prob_t, n * KT + (k + 1))
                    act.activation(pt_hi[:, k, :], W[k][:, :], ACT.Copy).then_inc(pt_hi_done, 1)

            def relu_high(n):
                act.wait_ge(t_bet_done, n + 1)
                act.activation(th_hi[:, :], gt[:, :], ACT.Relu).then_inc(relu_hi_done, 1)

            def z_high(n):
                for c, w in enumerate((W[3], W[0])):
                    act.wait_ge(zg_t, n * 2 + (c + 1))
                    act.activation(cz_hi[:, c * D:(c + 1) * D], w[:, :], ACT.Copy).then_inc(z_hi_done, 1)

            norm_x(0)
            act.wait_ge(w_here[0], 16)
            for k in range(KT):
                act.activation(w_hi[0][:, k, :], res[:, k, :], ACT.Copy).then_inc(w_hi_done, 1)
            xt_high(0)
            act.wait_ge(w_here[1], 16)
            for k in range(KT):
                act.activation(w_hi[1][:, k, :], prob[:, k, :], ACT.Copy).then_inc(w_hi_done, 1)
            act.wait_ge(w_here[2], 32)
            for k in range(KT):
                act.activation(w_hi[2][:, k, :], (cx if k < 2 else fin)[:, k % 2, :], ACT.Copy)\
                   .then_inc(w_hi_done, 1)

            def e_tile(t, e):
                gate_r(t, e)
                gate_f(t, e)
                forget(t, e)
                gate_c(t, e)
                square(t, e)
                rh_high(t, e)

            e_tile(0, 0)
            for c in range(2):
                act.wait_ge(pj_t, c + 1)
                act.activation(pj_hi[:, 2 * c:2 * c + 2, :].rearrange("p m n -> p (m n)"), W[c][:, :],
                               ACT.Copy).then_inc(pj_hi_done, 1)
            e_tile(0, 1)
            act.wait_ge(col_done, 1)
            act.wait_ge(w_here[3], 16)
            for k in range(KT):
                act.activation(wo_hi[:, k, :], res[:, k, :], ACT.Copy, scale=scale_bc[:, k:k + 1])\
                   .then_inc(w_hi_done, 1)
            e_tile(0, 2)
            for k in range(KT):
                act.wait_ge(q_t, k + 1)
                act.activation(wq[:, k, :], W[k][:, :], ACT.Copy).then_inc(wq_done, 1)
            norm_x(1)
            e_tile(0, 3)
            xt_high(1)
            ctx_high(0)
            norm_f(0, 0)

            def back(i, b, gates):
                n = i * 2 + (b - 2)
                first, second = gates and b == 0, gates and b == 1
                e = 2 * b
                if gates:
                    gate_r(i, e)
                if b:
                    norm_f(n, b)
                    ctx_high(n)
                proj_high(n)
                if first:
                    gate_f(i, e)
                g_high(n)
                exps(n)
                if first:
                    forget(i, e)
                    gate_c(i, e)
                if second:
                    gate_f(i, e)
                pt_high(n)
                if second:
                    forget(i, e)
                    gate_c(i, e)
                if gates:
                    square(i, e)
                    rh_high(i, e)
                if first:
                    gate_r(i, e + 1)
                relu_high(n)
                if second:
                    gate_r(i, e + 1)
                if gates:
                    gate_f(i, e + 1)
                z_high(n)
                if gates:
                    forget(i, e + 1)
                    gate_c(i, e + 1)
                    square(i, e + 1)
                    rh_high(i, e + 1)

            def step(i, load_next):
                back(i, 0, True)
                if load_next:
                    norm_x(i + 1)
                back(i, 1, True)
                if load_next:
                    xt_high(i + 1)
                ctx_high(i * 2)
                norm_f(i * 2, 0)

            with act.Fori(1, PAIRS - 1) as i:
                step(i, True)
            step(PAIRS - 1, False)
            back(PAIRS, 0, False)
            back(PAIRS, 1, False)

        @block.tensor
        def _(pe):
            pe.wait_ge(const_done, 4)

            def transpose_x(t):
                pe.wait_ge(xn_done, t * QT + QT)
                if not isinstance(t, int) or t > 0:
                    need(pe, x3_done, t * 2 * ST - 2 * ST)
                for k in range(KT):
                    for q in range(QT):
                        mm = pe.transpose(W[k][:, q * P:(q + 1) * P], x_in[:, q, k * P:(k + 1) * P], ident[:, :])
                    mm.then_inc(xt_mm, 1)

            free = (r_done, tf_done, c_done)

            def gates(t, first, count):
                for chunk in range(first, first + count):
                    group, k = divmod(chunk, KT)
                    e, m = divmod(group, 3)
                    if k == 0:
                        need(pe, free[m], t * KT + e)
                    if group == 0:
                        pe.wait_ge(xt_lo_done, t * KT + (k + 1))
                    if e == 0 and isinstance(t, int) and t == 0:
                        pe.wait_ge(w_lo_done, m * KT + k + 1)
                    cut = slice(e * P, (e + 1) * P)
                    pe.matmul(Z[m][:, :], w_hi[m][:, k, cut], xt_hi[:, k, :], start=(k == 0), stop=False)
                    pe.matmul(Z[m][:, :], w_hi[m][:, k, cut], xt_lo[:, k, :], start=False, stop=False)
                    mm = pe.matmul(Z[m][:, :], w_lo[m][:, k, cut], xt_hi[:, k, :], start=False,
                                   stop=(k == KT - 1))
                    if k == KT - 1:
                        mm.then_inc(z_mm, 1)

            def mix_out(t, next_x):
                pe.wait_ge(hsq_done, t * (KT - 1) + (KT - 1))
                for q in range(QT):
                    mm = pe.matmul(W[4][:, q:q + 1], hsq[:, q * P:(q + 1) * P], ones[:, 0:1], start=True, stop=True)
                mm.then_inc(hsq_mm, 1)
                if next_x:
                    pe.wait_ge(xt_lo_done, t * KT + 2 * KT)
                if isinstance(t, int) and t == 0:
                    pe.wait_ge(w_lo_done, 4 * KT)
                for k in range(KT):
                    pe.wait_ge(rh_lo_done, t * KT + (k + 1))
                    for q in range(QT):
                        cut = slice(q * P, (q + 1) * P)
                        pe.matmul(W[q][:, :], rh_hi[:, k, cut], wo_hi[:, k, :], start=(k == 0), stop=False)
                        pe.matmul(W[q][:, :], rh_hi[:, k, cut], wo_lo[:, k, :], start=False, stop=False)
                        mm = pe.matmul(W[q][:, :], rh_lo[:, k, cut], wo_hi[:, k, :], start=False,
                                       stop=(k == KT - 1))
                        if k == KT - 1:
                            mm.then_inc(wo_mm, 1)

            def project(bank, m, hi, lo, done):
                for s in range(ST):
                    wt_hi, wt_lo = pj_hi[:, m, s * P:(s + 1) * P], pj_lo[:, m, s * P:(s + 1) * P]
                    pe.matmul(W[bank][:, :], wt_hi, hi[s], start=(s == 0), stop=False)
                    pe.matmul(W[bank][:, :], wt_hi, lo[s], start=False, stop=False)
                    mm = pe.matmul(W[bank][:, :], wt_lo, hi[s], start=False, stop=(s == ST - 1))
                mm.then_inc(done, 1)

            def projections(n, b):
                pe.wait_ge(fx_lo_done, n + 1)
                if b == 0:
                    need(pe, x1_done, n * ST + 2 * ST)
                else:
                    need(pe, x3_done, n * ST)
                fh = [fx_hi[:, s, :] for s in range(ST)]
                fl = [fx_lo[:, s, :] for s in range(ST)]
                project(2, 2, fh, fl, g_mm)
                project(1, 1, fh, fl, ph_mm)
                pe.wait_ge(ctx_lo_done, n + 1)
                ch = [cz_hi[:, s * D:(s + 1) * D] for s in range(ST)]
                cl = [cz_lo[:, s * D:(s + 1) * D] for s in range(ST)]
                project(0, 0, ch, cl, th_mm)

            def turn_g(n):
                pe.wait_ge(gt_done, n + 1)
                for j in range(KT):
                    mm = pe.transpose(W[3][:, j * P:(j + 1) * P], gt[:, j * P:(j + 1) * P], ident[:, :])
                mm.then_inc(g_t, 1)

            def scores(n):
                pe.wait_ge(th_lo_done, n + 1)
                pe.wait_ge(ph_lo_done, n + 1)
                for k in range(KT):
                    if k == 3:
                        pe.wait_ge(g_lo_done, n + 1)
                    cut = slice(k * P, (k + 1) * P)
                    pe.matmul(W[k][:, :], th_hi[:, cut], ph_hi[:, :], start=True, stop=False)
                    pe.matmul(W[k][:, :], th_hi[:, cut], ph_lo[:, :], start=False, stop=False)
                    pe.matmul(W[k][:, :], th_lo[:, cut], ph_hi[:, :], start=False, stop=True).then_inc(score_mm, 1)

            def turn_prob(n):
                pe.wait_ge(prob_done, n * KT + KT)
                for j in range(KT):
                    for k in range(KT):
                        mm = pe.transpose(W[j][:, k * P:(k + 1) * P], prob[:, k, j * P:(j + 1) * P], ident[:, :])
                    mm.then_inc(prob_t, 1)

            def attend(n):
                for j in range(KT):
                    pe.wait_ge(pt_lo_done, n * KT + (j + 1))
                    pe.matmul(W[4][:, :], g_hi[:, j, :], pt_hi[:, j, :], start=(j == 0), stop=False)
                    pe.matmul(W[4][:, :], g_hi[:, j, :], pt_lo[:, j, :], start=False, stop=False)
                    mm = pe.matmul(W[4][:, :], g_lo[:, j, :], pt_hi[:, j, :], start=False, stop=(j == KT - 1))
                mm.then_inc(av_mm, 1)

            def mean_over(n):
                pe.wait_ge(t_mean_done, n + 1)
                pe.matmul(W[0][:, 0:1], avg[:, :], t_s[:, 0:1], start=True, stop=True).then_inc(mean_mm, 1)

            def second_over(n):
                pe.wait_ge(t_sec_done, n + 1)
                pe.matmul(W[3][:, 0:1], avg[:, :], t_s[:, 2:3], start=True, stop=True).then_inc(sec_mm, 1)

            def attn_out(n):
                pe.wait_ge(relu_lo_done, n + 1)
                for o in range(ST):
                    cut = slice(o * P, (o + 1) * P)
                    pe.matmul(W[1 + o][:, :], pj_hi[:, 3, cut], th_hi[:, :], start=True, stop=False)
                    pe.matmul(W[1 + o][:, :], pj_hi[:, 3, cut], th_lo[:, :], start=False, stop=False)
                    pe.matmul(W[1 + o][:, :], pj_lo[:, 3, cut], th_hi[:, :], start=False, stop=True)\
                      .then_inc(out_mm, 1)

            def turn_z(n):
                pe.wait_ge(zg_done, n * ST + ST)
                for c, w in enumerate((W[3], W[0])):
                    for k in range(2):
                        for s in range(ST):
                            at = (k * ST + s) * P
                            mm = pe.transpose(w[:, at:at + P], fz[:, s, (2 * c + k) * P:(2 * c + k + 1) * P],
                                              ident[:, :])
                    mm.then_inc(zg_t, 1)

            def feed(n):
                pe.wait_ge(z_lo_done, n * 2 + 2)
                for s in range(ST):
                    for k in range(KT):
                        at = (k * ST + s) * P
                        pe.matmul(W[1 + s][:, :], cz_hi[:, at:at + P], wq[:, k, :], start=(k == 0), stop=False)
                        mm = pe.matmul(W[1 + s][:, :], cz_lo[:, at:at + P], wq[:, k, :], start=False,
                                       stop=(k == KT - 1))
                    mm.then_inc(ffn_mm, 1)

            transpose_x(0)
            gates(0, 0, 12)
            pe.wait_ge(pj_here, 64)
            pe.wait_ge(xt_lo_done, KT)
            src = [cx[:, 0, 0:256], cx[:, 0, 256:512], cx[:, 1, 0:256], fin[:, 0, 0:256]]
            for m in range(4):
                for h in range(2):
                    at = ((m % 2) * 2 + h) * P
                    mm = pe.transpose(W[m // 2][:, at:at + P], src[m][:, h * P:(h + 1) * P], ident[:, :])
                if m % 2:
                    mm.then_inc(pj_t, 1)
            gates(0, 12, 6)
            pe.wait_ge(abs_done, 1)
            pe.matmul(W[4][:, 0:1], avg[:, :], abs_sum, start=True, stop=True).then_inc(abs_mean, 1)
            gates(0, 18, 14)
            pe.wait_ge(pj_lo_done, 2)
            pe.wait_ge(q_done, KT)
            for k in range(KT):
                for o in range(KT):
                    mm = pe.transpose(W[k][:, o * P:(o + 1) * P], prob[:, o, k * P:(k + 1) * P], ident[:, :])
                mm.then_inc(q_t, 1)
            gates(0, 32, 6)
            pe.wait_ge(beta_done, KT)
            pe.wait_ge(wq_done, KT)
            for k in range(KT):
                pe.matmul(W[4][:, :], beta_w[:, k * P:(k + 1) * P], f32(wq[:, k, :]), start=(k == 0), stop=False)
            pe.matmul(W[4][:, :], ones[0:1, :], brow[0:1, :], start=False, stop=True).then_inc(bias_mm, 1)
            gates(0, 38, 10)
            transpose_x(1)
            pe.wait_ge(bias_done, 1)
            mix_out(0, True)

            def back(i, b, with_gates):
                n = i * 2 + (b - 2)
                at = [24 * b + 4 * b]

                def fill(count):
                    if with_gates:
                        gates(i, at[0], count)
                    at[0] += count

                fill(6 if b == 0 else 0)
                projections(n, b)
                fill(2 if b == 0 else 1)
                turn_g(n)
                scores(n)
                fill(4)
                turn_prob(n)
                fill(2)
                attend(n)
                fill(2)
                mean_over(n)
                fill(1)
                second_over(n)
                fill(5 if b == 0 else 4)
                attn_out(n)
                fill(4)
                turn_z(n)
                fill(2)
                feed(n)

            def step(i, load_next):
                back(i, 0, True)
                back(i, 1, True)
                if load_next:
                    transpose_x(i + 1)
                else:
                    need(pe, x3_done, i * 2 * ST)
                mix_out(i, load_next)

            with pe.Fori(1, PAIRS - 1) as i:
                step(i, True)
            step(PAIRS - 1, False)
            back(PAIRS, 0, False)
            back(PAIRS, 1, False)

        @block.vector
        def _(dve):
            def stats(raw, mv, ve, tile, count, raw_done, mv_done, ve_done, first, unit, mul, add):
                for q in range(count):
                    dve.bn_stats(raw[:, q, :], tile(q)).then_inc(raw_done, 1)
                dve.drain()
                for q in range(count):
                    dve.bn_aggr(mv[:, q, :], raw[:, q, :]).then_inc(mv_done, 1)
                dve.wait_ge(mv_done, first + count)
                dve.tensor_scalar(ve[:, :], mv[:, :, 1], mul, add, ALU.mult, ALU.add).then_inc(ve_done, 1)

            def stats_x(t):
                dve.wait_ge(x_here, t * 16 + 16)
                stats(a_raw, a_mv, a_ve, lambda q: x_in[:, q, :], QT, a_raw_done, a_mv_done, a_ve_done,
                      t * QT, 1, 1.0, EPS)

            def shift_x(t):
                dve.wait_ge(a_rstd_done, t + 1)
                dve.scalar_tensor_tensor(out=a_nb[:, :], in0=a_mv[:, :, 0], scalar=-1.0, in1=a_rstd[:, :],
                                         op0=ALU.mult, op1=ALU.mult).then_inc(a_nb_done, 1)

            def xt_low(t):
                for k in range(KT):
                    dve.wait_ge(xt_hi_done, t * KT + (k + 1))
                    dve.tensor_tensor(xt_lo[:, k, :], W[k][:, :], f32(xt_hi[:, k, :]), ALU.subtract)\
                       .then_inc(xt_lo_done, 1)

            def gate_r(t, e):
                dve.wait_ge(tr_done, t * KT + (e + 1))
                dve.scalar_tensor_tensor(out=tr[:, :], in0=tr[:, :], scalar=1.0, in1=Z[0][:, :],
                                         op0=ALU.add, op1=ALU.mult).then_inc(r_done, 1)

            def combine(t, e, before, *args):
                need(dve, tree_done, tree(t, e) + before)
                if len(args) == 4:
                    dve.tensor_tensor(*args).then_inc(tree_done, 1)
                else:
                    dve.scalar_tensor_tensor(*args).then_inc(tree_done, 1)

            def gate_c(t, e):
                dve.wait_ge(tc_done, t * KT + (e + 1))
                dve.scalar_tensor_tensor(out=tc[:, :], in0=tc[:, :], scalar=1.0, in1=Z[2][:, :],
                                         op0=ALU.add, op1=ALU.mult).then_inc(c_done, 1)
                dve.wait_ge(c_done, t * KT + (e + 1))
                dve.wait_ge(f_done, t * KT + (e + 1))
                combine(t, e, 0, gg[:, :], fg[:, :], -1.0, tc[:, :], ALU.add, ALU.mult)
                for l in range(LEVELS):
                    n0, step = 4 * l + 1, 2 << l
                    fa, ca = level(fg, step // 2 - 1, step), level(tc, step // 2 - 1, step)
                    fb, cb, gb = (level(tile, step - 1, step) for tile in (fg, tc, gg))
                    product = tt[:, :, 0:S // step]
                    combine(t, e, n0 - 1, product, fb, ca, ALU.mult)
                    if l < LEVELS - 1:
                        combine(t, e, n0 + 1, fb, fa, fb, ALU.mult)
                    combine(t, e, n0 + 1, cb, product, gb, ALU.subtract)
                    if l < LEVELS - 1:
                        combine(t, e, n0 + 3, gb, fb, -1.0, cb, ALU.add, ALU.mult)
                n0 += 2
                for l in reversed(range(LEVELS - 1)):
                    step = 2 << l
                    f, c, g = (level(tile, step + step // 2 - 1, step) for tile in (fg, tc, gg))
                    product = tt[:, :, 0:S // step - 1]
                    combine(t, e, n0, product, f, level(tc, step - 1, step)[:, :, 0:S // step - 1], ALU.mult)
                    combine(t, e, n0 + 1, c, product, g, ALU.subtract)
                    n0 += 2
                assert n0 == TREE

            def rh_low(t, e):
                dve.wait_ge(rh_hi_done, t * KT + (e + 1))
                dve.tensor_tensor(rh_lo[:, e, :], tr[:, :], f32(rh_hi[:, e, :]), ALU.subtract)\
                   .then_inc(rh_lo_done, 1)

            def residual_1(t):
                dve.wait_ge(hsq_mm, t + 1)
                dve.tensor_scalar(m_ve[:, :], W[4][:, 0:QT], 1.0 / (4 * D), EPS, ALU.mult, ALU.add)\
                   .then_inc(m_ve_done, 1)
                dve.wait_ge(m_rstd_done, t + 1)
                for q in range(QT):
                    if q % ST == 0:
                        dve.wait_ge(res_here[q // ST], t * 16 + 16)
                    dve.wait_ge(wo_mm, t * QT + (q + 1))
                    dve.scalar_tensor_tensor(out=res[:, q, :], in0=W[q][:, :], scalar=m_rstd[:, q:q + 1],
                                             in1=res[:, q, :], op0=ALU.mult, op1=ALU.add).then_inc(x1_done, 1)

            def stats_b(n, b):
                dve.wait_ge(x1_done, n * ST + ST)
                stats(b_raw, b_mv, b_ve, lambda s: res[:, b * ST + s, :], ST, b_raw_done, b_mv_done,
                      b_ve_done, n * ST, ST, 1.0, EPS)

            def shift_b(n):
                dve.wait_ge(b_rstd_done, n + 1)
                need(dve, fn_done, n * ST)
                dve.scalar_tensor_tensor(out=b_nb[:, :], in0=b_mv[:, :, 0], scalar=-1.0, in1=b_rstd[:, :],
                                         op0=ALU.mult, op1=ALU.mult).then_inc(b_nb_done, 1)

            def fx_low(n):
                dve.wait_ge(fx_hi_done, n + 1)
                dve.tensor_tensor(fx_lo, fz, f32(fx_hi), ALU.subtract).then_inc(fx_lo_done, 1)

            def proj_low(n):
                dve.wait_ge(ph_hi_done, n + 1)
                dve.scalar_tensor_tensor(out=ph_lo[:, :], in0=W[1][:, :], scalar=phi_bc, in1=f32(ph_hi[:, :]),
                                         op0=ALU.add, op1=ALU.subtract).then_inc(ph_lo_done, 1)
                dve.wait_ge(th_hi_done, n + 1)
                dve.scalar_tensor_tensor(out=th_lo[:, :], in0=W[0][:, :], scalar=theta_bc, in1=f32(th_hi[:, :]),
                                         op0=ALU.add, op1=ALU.subtract).then_inc(th_lo_done, 1)

            def g_low(n):
                dve.wait_ge(g_hi_done, n + 1)
                dve.tensor_tensor(g_lo[:, :, :].rearrange("p j l -> p (j l)"), W[3][:, :],
                                  f32(g_hi[:, :, :]).rearrange("p j l -> p (j l)"), ALU.subtract)\
                   .then_inc(g_lo_done, 1)

            def row_max(n, k):
                dve.wait_ge(score_mm, n * KT + (k + 1))
                dve.tensor_reduce(nmax[:, k:k + 1], W[k][:, :], AX.X, ALU.max, negate=True).then_inc(nmax_done, 1)

            def row_norm(n, k):
                dve.wait_ge(exp_done, n * KT + (k + 1))
                dve.reciprocal(rinv[:, k:k + 1], rsum[:, k:k + 1]).then_inc(rinv_done, 1)
                dve.wait_ge(rinv_done, n * KT + (k + 1))
                dve.tensor_scalar(prob[:, k, :], prob[:, k, :], rinv[:, k:k + 1], None, ALU.mult)\
                   .then_inc(prob_done, 1)

            def softmax(n):
                row_max(n, 0)
                row_max(n, 1)
                row_norm(n, 0)
                row_max(n, 2)
                row_norm(n, 1)
                row_max(n, 3)
                row_norm(n, 2)
                row_norm(n, 3)

            def pt_low(n):
                for k in range(KT):
                    dve.wait_ge(pt_hi_done, n * KT + (k + 1))
                    dve.tensor_tensor(pt_lo[:, k, :], W[k][:, :], f32(pt_hi[:, k, :]), ALU.subtract)\
                       .then_inc(pt_lo_done, 1)

            def t_mean(n):
                dve.wait_ge(av_mm, n + 1)
                dve.bn_stats(t_raw[:, :], W[4][:, :]).then_inc(t_raw_done, 1)
                dve.drain()
                dve.bn_aggr(t_mv[:, :], t_raw[:, :]).then_inc(t_mv_done, 1)
                dve.wait_ge(t_mv_done, n + 1)
                dve.tensor_scalar(t_s[:, 0:1], t_mv[:, 0:1], g_bc, None, ALU.add).then_inc(t_mean_done, 1)

            def t_second(n):
                dve.wait_ge(mean_mm, n + 1)
                dve.tensor_scalar(t_s[:, 1:2], t_s[:, 0:1], W[0][:, 0:1], None, ALU.subtract).then_inc(t_dist_done, 1)
                dve.tensor_scalar(t_s[:, 3:4], g_bc, W[0][:, 0:1], None, ALU.subtract).then_inc(t_dist_done, 1)
                dve.wait_ge(t_dist_done, n * 2 + 2)
                dve.scalar_tensor_tensor(out=t_s[:, 2:3], in0=t_s[:, 1:2], scalar=t_s[:, 1:2], in1=t_mv[:, 1:2],
                                         op0=ALU.mult, op1=ALU.add).then_inc(t_sec_done, 1)
                dve.scalar_tensor_tensor(out=gt[:, :], in0=W[4][:, :], scalar=t_s[:, 3:4], in1=gamma_lt[:, :],
                                         op0=ALU.add, op1=ALU.mult).then_inc(t_gam_done, 1)

            def t_var(n):
                dve.wait_ge(sec_mm, n + 1)
                dve.tensor_scalar(t_s[:, 4:5], W[3][:, 0:1], EPS, None, ALU.add).then_inc(t_ve_done, 1)

            def t_norm(n):
                dve.wait_ge(t_rstd_done, n + 1)
                dve.wait_ge(t_gam_done, n + 1)
                dve.scalar_tensor_tensor(out=gt[:, :], in0=gt[:, :], scalar=t_s[:, 5:6], in1=beta_lt[:, :],
                                         op0=ALU.mult, op1=ALU.add).then_inc(t_bet_done, 1)

            def relu_low(n):
                dve.wait_ge(relu_hi_done, n + 1)
                dve.scalar_tensor_tensor(out=th_lo[:, :], in0=gt[:, :], scalar=0.0, in1=f32(th_hi[:, :]),
                                         op0=ALU.max, op1=ALU.subtract).then_inc(relu_lo_done, 1)

            def residual_2(n, b):
                dve.wait_ge(cx_done, n + 1)
                for o in range(ST):
                    dve.wait_ge(out_mm, n * ST + (o + 1))
                    dve.scalar_tensor_tensor(out=res[:, b * ST + o, :], in0=W[1 + o][:, :],
                                             scalar=out_bc[:, o:o + 1], in1=cx[:, o, :],
                                             op0=ALU.add, op1=ALU.add).then_inc(x2_done, 1)

            def stats_c(n, b):
                dve.wait_ge(x2_done, n * ST + ST)
                stats(c_raw, c_mv, c_ve, lambda s: res[:, b * ST + s, :], ST, c_raw_done, c_mv_done,
                      c_ve_done, n * ST, ST, 1.0 + EPS, EPS * EPS)
                for s in range(ST):
                    dve.scalar_tensor_tensor(out=fz[:, s, :], in0=res[:, b * ST + s, :], scalar=c_mv[:, s, 0:1],
                                             in1=gamma_bc[:, :], op0=ALU.subtract, op1=ALU.mult)\
                       .then_inc(zg_done, 1)

            def z_low(n):
                for c, w in enumerate((W[3], W[0])):
                    dve.wait_ge(z_hi_done, n * 2 + (c + 1))
                    dve.tensor_tensor(cz_lo[:, c * D:(c + 1) * D], w[:, :], f32(cz_hi[:, c * D:(c + 1) * D]),
                                      ALU.subtract).then_inc(z_lo_done, 1)

            def residual_3(n):
                dve.wait_ge(fin_done, n * ST + ST)
                dve.wait_ge(c_rstd_done, n + 1)
                for s in range(ST):
                    dve.wait_ge(ffn_mm, n * ST + (s + 1))
                    dve.scalar_tensor_tensor(out=fin[:, s, :], in0=W[1 + s][:, :], scalar=c_rstd[:, s:s + 1],
                                             in1=fin[:, s, :], op0=ALU.mult, op1=ALU.add).then_inc(x3_done, 1)

            stats_x(0)
            shift_x(0)
            for k in range(KT):
                dve.wait_ge(w_hi_done, k + 1)
                dve.tensor_tensor(w_lo[0][:, k, :], res[:, k, :], f32(w_hi[0][:, k, :]), ALU.subtract)\
                   .then_inc(w_lo_done, 1)
            xt_low(0)
            for m in range(1, 3):
                for k in range(KT):
                    src = prob[:, k, :] if m == 1 else (cx if k < 2 else fin)[:, k % 2, :]
                    dve.wait_ge(w_hi_done, m * KT + k + 1)
                    dve.tensor_tensor(w_lo[m][:, k, :], src, f32(w_hi[m][:, k, :]), ALU.subtract)\
                       .then_inc(w_lo_done, 1)

            def e_tile(t, e):
                gate_r(t, e)
                gate_c(t, e)

            e_tile(0, 0)
            dve.wait_ge(small_here, 16 * 10)
            dve.tensor_scalar(scale_bc, scale_bc, 0.25, None, ALU.mult).then_inc(col_done, 1)
            dve.wait_ge(q_here, 16)
            dve.tensor_reduce(abs_sum, prob[:, :, :], AX.XY, ALU.add, apply_absolute_value=True).then_inc(abs_done, 1)
            for c in range(2):
                dve.wait_ge(pj_hi_done, c + 1)
                dve.tensor_tensor(pj_lo[:, 2 * c:2 * c + 2, :].rearrange("p m n -> p (m n)"), W[c][:, :],
                                  f32(pj_hi[:, 2 * c:2 * c + 2, :]).rearrange("p m n -> p (m n)"), ALU.subtract)\
                   .then_inc(pj_lo_done, 1)
            rh_low(0, 0)
            dve.wait_ge(abs_mean, 1)
            half = 0.5 / (D * D // P)
            dve.tensor_scalar(thr, W[4][:, 0:1], half, 0.5 * Q_EPS, ALU.mult, ALU.add).then_inc(thr_done, 1)
            dve.tensor_scalar(neg_thr, W[4][:, 0:1], -half, -0.5 * Q_EPS, ALU.mult, ALU.add).then_inc(thr_done, 1)
            dve.wait_ge(thr_done, 2)
            for o in range(KT):
                need(dve, q_done, o)
                dve.tensor_scalar(gt[:, :], prob[:, o, :], neg_thr, None, ALU.is_lt).then_inc(below_done, 1)
                dve.wait_ge(below_done, o + 1)
                dve.scalar_tensor_tensor(out=prob[:, o, :], in0=prob[:, o, :], scalar=thr, in1=gt[:, :],
                                         op0=ALU.is_gt, op1=ALU.subtract).then_inc(q_done, 1)
            e_tile(0, 1)
            rh_low(0, 1)
            dve.wait_ge(const_done, 4)
            for k in range(KT):
                dve.tensor_scalar(beta_w[:, k * P:(k + 1) * P], ones[:, :], beta_c[:, k:k + 1], None, ALU.mult)\
                   .then_inc(beta_done, 1)
            for k in range(KT):
                dve.wait_ge(w_hi_done, 3 * KT + k + 1)
                dve.scalar_tensor_tensor(out=wo_lo[:, k, :], in0=res[:, k, :], scalar=scale_bc[:, k:k + 1],
                                         in1=f32(wo_hi[:, k, :]), op0=ALU.mult, op1=ALU.subtract)\
                   .then_inc(w_lo_done, 1)
            e_tile(0, 2)
            rh_low(0, 2)
            stats_x(1)
            shift_x(1)
            dve.wait_ge(bias_mm, 1)
            dve.tensor_copy(bias_bc[:, :], W[4][:, :]).then_inc(bias_done, 1)
            e_tile(0, 3)
            rh_low(0, 3)
            xt_low(1)
            residual_1(0)
            stats_b(0, 0)
            shift_b(0)
            fx_low(0)

            def back(i, b, gates, load_next):
                n = i * 2 + (b - 2)
                first, second = gates and b == 0, gates and b == 1
                e = 2 * b
                if gates:
                    gate_r(i, e)
                if b:
                    stats_b(n, b)
                    shift_b(n)
                    fx_low(n)
                proj_low(n)
                g_low(n)
                softmax(n)
                if first:
                    gate_c(i, e)
                pt_low(n)
                if first:
                    rh_low(i, e)
                t_mean(n)
                if first:
                    gate_r(i, e + 1)
                t_second(n)
                t_var(n)
                if second:
                    gate_c(i, e)
                t_norm(n)
                relu_low(n)
                if second:
                    rh_low(i, e)
                    gate_r(i, e + 1)
                residual_2(n, b)
                stats_c(n, b)
                z_low(n)
                if gates:
                    gate_c(i, e + 1)
                    rh_low(i, e + 1)
                if load_next and b == 0:
                    stats_x(i + 1)
                    shift_x(i + 1)
                residual_3(n)

            def step(i, load_next):
                back(i, 0, True, load_next)
                back(i, 1, True, load_next)
                if load_next:
                    xt_low(i + 1)
                residual_1(i)
                stats_b(i * 2, 0)
                shift_b(i * 2)
                fx_low(i * 2)

            with dve.Fori(1, PAIRS - 1) as i:
                step(i, True)
            step(PAIRS - 1, False)
            back(PAIRS, 0, False, False)
            back(PAIRS, 1, False, False)


_INS = ['x', 'ctx_2048', 'L0_attn_Wr', 'L0_attn_Wf', 'L0_attn_Wc', 'L0_attn_Wo', 'L0_attn_ln_scale',
        'L0_xattn_theta_w', 'L0_xattn_theta_b', 'L0_xattn_phi_w', 'L0_xattn_phi_b', 'L0_xattn_g_w',
        'L0_xattn_g_b', 'L0_xattn_ln_gamma', 'L0_xattn_ln_beta', 'L0_xattn_out_w', 'L0_xattn_out_b',
        'L0_ffn_weight', 'L0_ffn_bias', 'L0_ffn_ln_gamma', 'L0_ffn_ln_beta']
_OUT = ((16, 256, 512), 'float32')


def kernel(**inputs):
    import numpy as _np
    import concourse.bacc as _bacc
    from concourse import mybir as _mybir
    from concourse.bass_utils import run_bass_kernel_spmd as _run

    nc = _bacc.Bacc("TRN2", target_bir_lowering=False, num_devices=1)
    arrays, args = {}, []
    for name in _INS:
        a = _np.ascontiguousarray(inputs[name])
        arrays[f"in_{name}_dram"] = a
        args.append(nc.dram_tensor(f"in_{name}_dram", a.shape, _mybir.dt.from_np(a.dtype), kind="ExternalInput").ap())
    shape, dtype = _OUT
    args.append(nc.dram_tensor("out_0_dram", shape, _mybir.dt.from_np(_np.dtype(dtype)), kind="ExternalOutput").ap())
    build(nc, *args)
    r = _run(nc, [arrays], core_ids=[0])
    return r.results[0]["out_0_dram"]
```

```python
from contextlib import ExitStack

import concourse.bass as bass
from concourse import mybir

F32 = mybir.dt.float32
F32R = mybir.dt.float32r
ALU = mybir.AluOpType
ACT = mybir.ActivationFunctionType
AX = mybir.AxisListType

P = 128
EPS = 1e-5
Q_EPS = 1e-5


def need(eng, sem, value):
    if not isinstance(value, int) or value > 0:
        eng.wait_ge(sem, value)


def f32(ap):
    return ap.bitcast(F32)


def build(nc, x, ctx_in, wr, wf, wc, wo, ln_scale, theta_w, theta_b, phi_w, phi_b, g_w, g_b,
          ln_gamma, ln_beta, out_w, out_b, ffn_w, ffn_bias, ffn_gamma, ffn_beta, out):
    B, S, D = x.shape
    L = theta_w.shape[0]
    PAIRS = B // 2
    KT = D // P
    LEVELS = S.bit_length() - 1
    assert S == 1 << LEVELS
    ST = S // P
    QT = 2 * ST
    R, F, C = range(3)
    GROUPS = [(m, e) for e in range(KT) for m in (F, C)] + [(R, e) for e in range(KT)]
    TURN = {group: n for n, group in enumerate(GROUPS)}
    assert len(GROUPS) % 3 == 0
    assert L == P and D == 512 and S == 256 and B % 2 == 0 and PAIRS >= 3

    x_rows = x.rearrange("b (s p) d -> p (b s) d", p=P)
    ctx_rows = ctx_in.rearrange("b (s p) d -> p (b s) d", p=P)
    out_rows = out.rearrange("b (s p) d -> p (b s) d", p=P)

    stack = ExitStack()
    with stack:
        def sb(name, shape, dt=F32):
            return stack.enter_context(nc.sbuf_tensor(name, shape, dt))

        def sem(name):
            return stack.enter_context(nc.semaphore(name))

        ident = sb("ident", [P, P])
        avg = sb("avg", [P, P])
        minus_half = sb("minus_half", [P, 4])
        w_hi = [sb(f"w{m}_hi", [P, KT, D], F32R) for m in "rfc"]
        w_lo = [sb(f"w{m}_lo", [P, KT, D], F32R) for m in "rfc"]
        wo_hi = sb("wo_hi", [P, KT, D], F32R)
        wo_lo = sb("wo_lo", [P, KT, D], F32R)
        wq = sb("wq", [P, KT, D], F32R)
        pj_hi = sb("pj_hi", [P, 4, 2 * P], F32R)
        pj_lo = sb("pj_lo", [P, 4, 2 * P], F32R)
        gamma_lt = sb("gamma_lt", [P, D])
        beta_lt = sb("beta_lt", [P, D])
        gamma_bc = sb("gamma_bc", [P, D])
        bias_bc = sb("bias_bc", [P, D])
        cols = sb("cols", [P, 16])
        theta_bc, phi_bc, g_bc = cols[:, 0:1], cols[:, 1:2], cols[:, 2:3]
        out_bc, scale_bc, beta_c = cols[:, 3:5], cols[:, 5:9], cols[:, 9:13]
        thr, neg_thr, abs_sum = cols[:, 13:14], cols[:, 14:15], cols[:, 15:16]

        x_in = sb("x_in", [P, QT, D])
        xt_hi = sb("xt_hi", [P, KT, D], F32R)
        xt_lo = sb("xt_lo", [P, KT, D], F32R)
        r2 = sb("r2", [P, KT, D])
        fs = sb("fs", [P, KT, D])
        cs = sb("cs", [P, KT, D])
        gs = sb("gs", [P, KT, D // 2])
        tt = sb("tt", [P, 2, D])
        res = sb("res", [P, QT, D])
        cx = sb("cx", [P, ST, D])
        fin = sb("fin", [P, ST, D])
        cz_hi = sb("cz_hi", [P, 2 * D], F32R)
        cz_lo = sb("cz_lo", [P, 2 * D], F32R)
        th_hi = sb("th_hi", [P, D], F32R)
        th_lo = sb("th_lo", [P, D], F32R)
        ph_hi = sb("ph_hi", [P, D], F32R)
        ph_lo = sb("ph_lo", [P, D], F32R)
        gt = sb("gt", [P, D])
        g_hi = sb("g_hi", [P, KT, P], F32R)
        g_lo = sb("g_lo", [P, KT, P], F32R)
        prob = sb("prob", [P, KT, D])
        fz = prob[:, 0:ST, :]
        pt_hi = sb("pt_hi", [P, KT, D], F32R)
        pt_lo = sb("pt_lo", [P, KT, D], F32R)
        rh_hi, rh_lo = pt_hi, pt_lo
        brow, ones = tt[0:1, 0, :], tt[:, 1, 0:P]
        beta_w = fin[:, 1, :]
        fx_hi, fx_lo = pt_hi[:, 0:ST, :], pt_lo[:, 0:ST, :]
        a_raw = sb("a_raw", [P, QT, 6])
        a_mv = sb("a_mv", [P, QT, 2])
        b_raw = sb("b_raw", [P, QT, 6])
        b_mv = sb("b_mv", [P, QT, 2])
        c_raw = sb("c_raw", [P, ST, 6])
        c_mv = sb("c_mv", [P, ST, 2])
        t_raw = c_raw[:, 0, :]
        per_row = sb("per_row", [P, 13, QT])
        a_ve, a_rstd, a_nb, m_ve, m_rstd, b_ve, b_rstd, b_nb, nmax, rsum, rinv = (per_row[:, n, :] for n in range(11))
        c_ve, c_rstd = (per_row[:, n, 0:ST] for n in (11, 12))
        t_mv = sb("t_mv", [P, 2])
        t_s = sb("t_s", [P, 6])

        Z = [stack.enter_context(nc.psum_tensor(f"z{m}", [P, D], F32)) for m in range(3)]
        W = [stack.enter_context(nc.psum_tensor(f"work{n}", [P, D], F32)) for n in range(5)]
        XT = [W[4], Z[0], Z[1], Z[2]]
        SC = [W[0], W[1], W[3], W[2]]
        Y = [W[0], W[3], W[1], W[2]]

        x_here = sem("x_here")
        res_here = [sem(f"res_here_{b}") for b in range(2)]
        ctx_here = sem("ctx_here")
        stored = sem("stored")
        w_here = [sem(f"w{m}_here") for m in "rfco"]
        q_here = sem("q_here")
        pj_here = sem("pj_here")
        small_here = sem("small_here")
        ident_zero = sem("ident_zero")
        const_done = sem("const_done")
        w_hi_done = sem("w_hi_done")
        w_lo_done = sem("w_lo_done")
        col_done = sem("col_done")
        abs_done = sem("abs_done")
        abs_mean = sem("abs_mean")
        thr_done = sem("thr_done")
        below_done = sem("below_done")
        q_done = sem("q_done")
        q_t = sem("q_t")
        wq_done = sem("wq_done")
        beta_done = sem("beta_done")
        bias_mm = sem("bias_mm")
        bias_done = sem("bias_done")
        pj_t = sem("pj_t")
        pj_hi_done = sem("pj_hi_done")
        pj_lo_done = sem("pj_lo_done")
        a_mv_done = sem("a_mv_done")
        a_ve_done = sem("a_ve_done")
        a_rstd_done = sem("a_rstd_done")
        a_nb_done = sem("a_nb_done")
        xn_done = sem("xn_done")
        xt_mm = sem("xt_mm")
        xt_hi_done = sem("xt_hi_done")
        xt_lo_done = sem("xt_lo_done")
        z_mm = sem("z_mm")
        tr_done = sem("tr_done")
        tf_done = sem("tf_done")
        tc_done = sem("tc_done")
        r_done = sem("r_done")
        f_less_done = sem("f_less_done")
        f_done = sem("f_done")
        c_done = sem("c_done")
        g0_done = sem("g0_done")
        up_t = sem("up_t")
        up_g = sem("up_g")
        up_f = sem("up_f")
        up_c = sem("up_c")
        down_t = sem("down_t")
        down_h = sem("down_h")
        sq_done = sem("sq_done")
        hsq_done = sem("hsq_done")
        rh_done = sem("rh_done")
        rh_hi_done = sem("rh_hi_done")
        rh_lo_done = sem("rh_lo_done")
        hsq_mm = sem("hsq_mm")
        m_ve_done = sem("m_ve_done")
        m_rstd_done = sem("m_rstd_done")
        wo_mm = sem("wo_mm")
        x1_done = sem("x1_done")
        b_mv_done = sem("b_mv_done")
        b_ve_done = sem("b_ve_done")
        b_rstd_done = sem("b_rstd_done")
        b_nb_done = sem("b_nb_done")
        fn_done = sem("fn_done")
        fx_hi_done = sem("fx_hi_done")
        fx_lo_done = sem("fx_lo_done")
        ctx_hi_done = sem("ctx_hi_done")
        ctx_lo_done = sem("ctx_lo_done")
        cx_done = sem("cx_done")
        g_mm = sem("g_mm")
        ph_mm = sem("ph_mm")
        th_mm = sem("th_mm")
        gt_done = sem("gt_done")
        ph_hi_done = sem("ph_hi_done")
        ph_lo_done = sem("ph_lo_done")
        th_hi_done = sem("th_hi_done")
        th_lo_done = sem("th_lo_done")
        g_t = sem("g_t")
        g_hi_done = sem("g_hi_done")
        g_lo_done = sem("g_lo_done")
        score_mm = sem("score_mm")
        nmax_done = sem("nmax_done")
        exp_done = sem("exp_done")
        rinv_done = sem("rinv_done")
        prob_done = sem("prob_done")
        prob_t = sem("prob_t")
        pt_hi_done = sem("pt_hi_done")
        pt_lo_done = sem("pt_lo_done")
        av_mm = sem("av_mm")
        t_mv_done = sem("t_mv_done")
        t_mean_done = sem("t_mean_done")
        mean_mm = sem("mean_mm")
        t_dist_done = sem("t_dist_done")
        t_sec_done = sem("t_sec_done")
        sec_mm = sem("sec_mm")
        t_ve_done = sem("t_ve_done")
        t_rstd_done = sem("t_rstd_done")
        t_gam_done = sem("t_gam_done")
        t_bet_done = sem("t_bet_done")
        relu_hi_done = sem("relu_hi_done")
        relu_lo_done = sem("relu_lo_done")
        out_mm = sem("out_mm")
        x2_done = sem("x2_done")
        c_mv_done = sem("c_mv_done")
        c_ve_done = sem("c_ve_done")
        c_rstd_done = sem("c_rstd_done")
        zg_done = sem("zg_done")
        fin_done = sem("fin_done")
        zg_t = sem("zg_t")
        z_hi_done = sem("z_hi_done")
        z_lo_done = sem("z_lo_done")
        ffn_mm = sem("ffn_mm")
        x3_done = sem("x3_done")

        def level(tile, start, step, less=0):
            count = (S - start + step - 1) // step - less
            return tile[:, :, :].rearrange("p e (s n) -> p (e s) n", n=S)[:, :, start:start + (count - 1) * step + 1:step]

        def products(count):
            return tt[:, :, :].rearrange("p a d -> p (a d)")[:, 0:2 * KT * count]\
                .rearrange("p (q n) -> p q n", n=count)

        def up_product_f(eng, t, l):
            step = 2 << l
            eng.wait_ge(up_t, t * LEVELS + (l + 1))
            eng.wait_ge(up_g, t * LEVELS + (l + 1))
            eng.tensor_tensor(level(fs, step - 1, step), level(fs, step // 2 - 1, step), level(fs, step - 1, step),
                              ALU.mult).then_inc(up_f, 1)

        block = stack.enter_context(nc.Block())

        def store(eng, n):
            need(eng, x3_done, n * ST + ST)
            eng.dma_start(out_rows[:, bass.ds(n * ST, ST), :], fin[:, :, :]).then_inc(stored, 16)

        @block.sync
        def _(sp):
            def load_x(t):
                need(sp, xt_mm, t * KT)
                sp.dma_start(x_in[:, :, :], x_rows[:, bass.ds(t * QT, QT), :]).then_inc(x_here, 16)

            def load_res(t, b):
                n = t * 2 + (b - 2)
                if not isinstance(t, int) or t > 0:
                    need(sp, fin_done, n * ST + ST)
                    need(sp, zg_done, n * ST + ST)
                sp.dma_start(res[:, b * ST:(b + 1) * ST, :],
                             x_rows[:, bass.ds(t * QT + b * ST, ST), :]).then_inc(res_here[b], 16)

            def load_ctx(n):
                need(sp, x2_done, n * ST)
                sp.dma_start(cx[:, :, :], ctx_rows[:, bass.ds(n * ST, ST), :]).then_inc(ctx_here, 16)

            load_x(0)
            rows = lambda w: w.rearrange("(k p) n -> p k n", p=P)
            sp.dma_start(prob[:, :, :], rows(wf)).then_inc(w_here[F], 16)
            sp.dma_start(cx[:, :, :], rows(wc)[:, 0:2, :]).then_inc(w_here[C], 16)
            sp.dma_start(fin[:, :, :], rows(wc)[:, 2:4, :]).then_inc(w_here[C], 16)
            sp.dma_start(res[:, :, :], rows(wr)).then_inc(w_here[R], 16)
            sp.wait_ge(w_lo_done, 3 * KT)
            sp.dma_start(prob[:, :, :], rows(ffn_w)).then_inc(q_here, 16)
            for n, w in enumerate((theta_w, phi_w, g_w)):
                sp.dma_start(cx[:, 0, 0:256] if n == 0 else cx[:, n // 2, (n % 2) * 256:(n % 2) * 256 + 256],
                             w).then_inc(pj_here, 16)
            sp.dma_start(fin[:, 0, 0:256].rearrange("p (o l) -> p o l", o=2), rows(out_w)).then_inc(pj_here, 16)
            sp.dma_start(res[:, :, :], rows(wo)).then_inc(w_here[3], 16)
            sp.dma_start(gamma_bc[:, :], ffn_gamma.rearrange("(a d) -> a d", a=1).to_broadcast([P, D]))\
              .then_inc(small_here, 16)
            sp.dma_start(gamma_lt[:, :], ln_gamma).then_inc(small_here, 16)
            sp.dma_start(beta_lt[:, :], ln_beta).then_inc(small_here, 16)
            load_x(1)
            sp.wait_ge(w_lo_done, 4 * KT)
            load_res(0, 0)
            load_res(0, 1)
            sp.wait_ge(pj_lo_done, 2)
            load_ctx(0)

            def step(i, load_next):
                if load_next:
                    load_x(i + 1)
                load_ctx(i * 2 - 1)
                load_res(i, 0)
                store(sp, i * 2 - 2)
                load_ctx(i * 2)
                load_res(i, 1)
                store(sp, i * 2 - 1)

            with sp.Fori(1, PAIRS - 1) as i:
                step(i, True)
            step(PAIRS - 1, False)
            load_ctx(2 * PAIRS - 1)
            store(sp, 2 * PAIRS - 2)
            store(sp, 2 * PAIRS - 1)
            sp.wait_ge(stored, 16 * B)

        @block.gpsimd
        def _(pool):
            pool.memset(ident[:, :], 0.0).then_inc(ident_zero, 1)
            pool.memset(avg[:, :], 1.0 / P).then_inc(const_done, 1)
            pool.memset(ones, 1.0).then_inc(const_done, 1)
            pool.memset(minus_half[:, :], -0.5).then_inc(const_done, 1)
            pool.wait_ge(ident_zero, 1)
            pool.affine_select(out=ident[:, :], in_=ident[:, :], compare_op=ALU.not_equal, fill=1.0,
                               base=0, pattern=[[-1, P]], channel_multiplier=1).then_inc(const_done, 1)
            pool.wait_ge(const_done, 4)

            def rsqrt(out_ap, in_ap, width, done):
                pool.tensor_tensor(out_ap, in_ap, minus_half[:, 0:width], ALU.pow).then_inc(done, 1)

            def norm_x(t):
                pool.wait_ge(a_ve_done, t + 1)
                need(pool, xn_done, t * QT)
                rsqrt(a_rstd[:, :], a_ve[:, :], QT, a_rstd_done)

            def even_g(t, e):
                pool.wait_ge(f_less_done, t * KT + (e + 1))
                pool.wait_ge(c_done, t * KT + (e + 1))
                pool.tensor_tensor(gs[:, e, :], gs[:, e, :], cs[:, e, 0:D:2], ALU.mult).then_inc(g0_done, 1)

            def sum_sq(t):
                for e in range(1, KT):
                    pool.wait_ge(sq_done, t * KT + (e + 1))
                    need(pool, hsq_done, t * (KT - 1) + (e - 1))
                    pool.tensor_tensor(fs[:, 0, :], fs[:, 0, :], fs[:, e, :], ALU.add).then_inc(hsq_done, 1)

            def norm_m(t):
                pool.wait_ge(m_ve_done, t + 1)
                need(pool, x1_done, t * QT)
                rsqrt(m_rstd[:, :], m_ve[:, :], QT, m_rstd_done)

            def norm_b(n, b):
                pool.wait_ge(b_ve_done, n + 1)
                need(pool, fn_done, n * ST - ST)
                rsqrt(b_rstd[:, b * ST:(b + 1) * ST], b_ve[:, b * ST:(b + 1) * ST], ST, b_rstd_done)

            def ctx_low(n):
                pool.wait_ge(ctx_hi_done, n + 1)
                pool.tensor_tensor(cz_lo[:, :].rearrange("p (s d) -> p s d", s=ST), cx[:, :, :],
                                   f32(cz_hi[:, :]).rearrange("p (s d) -> p s d", s=ST), ALU.subtract)\
                    .then_inc(ctx_lo_done, 1)

            def ctx_plus(n, b):
                pool.wait_ge(ctx_lo_done, n + 1)
                pool.wait_ge(x1_done, n * ST + ST)
                pool.tensor_tensor(cx[:, :, :], cx[:, :, :], res[:, b * ST:(b + 1) * ST, :], ALU.add)\
                    .then_inc(cx_done, 1)

            def norm_t(n):
                pool.wait_ge(t_ve_done, n + 1)
                rsqrt(t_s[:, 5:6], t_s[:, 4:5], 1, t_rstd_done)

            def norm_c(n):
                pool.wait_ge(c_ve_done, n + 1)
                need(pool, x3_done, n * ST)
                rsqrt(c_rstd[:, :], c_ve[:, :], ST, c_rstd_done)

            def fin_sum(n, b):
                pool.wait_ge(x2_done, n * ST + ST)
                need(pool, stored, n * 16)
                for s in range(ST):
                    pool.tensor_tensor(fin[:, s, :], res[:, b * ST + s, :], bias_bc[:, :], ALU.add)\
                        .then_inc(fin_done, 1)

            def back(i, b, gates, load_next):
                n = i * 2 + (b - 2)
                ctx_low(n)
                if gates and b == 1:
                    up_product_f(pool, i, 0)
                    up_product_f(pool, i, 1)
                if b == 0 and load_next:
                    norm_x(i + 1)
                ctx_plus(n, b)
                if gates and b == 0:
                    even_g(i, 0)
                    even_g(i, 1)
                norm_t(n)
                norm_c(n)
                if gates and b == 0:
                    even_g(i, 2)
                fin_sum(n, b)
                if gates and b == 0:
                    even_g(i, 3)

            def finish(t):
                sum_sq(t)
                norm_m(t)
                norm_b(t * 2, 0)
                norm_b(t * 2 + 1, 1)

            norm_x(0)
            for e in range(KT):
                even_g(0, e)
            up_product_f(pool, 0, 0)
            up_product_f(pool, 0, 1)
            norm_x(1)
            pool.wait_ge(bias_done, 1)
            finish(0)

            def step(i, load_next):
                back(i, 0, True, load_next)
                back(i, 1, True, load_next)
                finish(i)

            with pool.Fori(1, PAIRS - 1) as i:
                step(i, True)
            step(PAIRS - 1, False)
            back(PAIRS, 0, False, False)
            back(PAIRS, 1, False, False)

        @block.scalar
        def _(act):
            col = lambda v: v.rearrange("(k p) -> p k", p=P)
            with nc.allow_non_contiguous_dma(reason="vectors of a few hundred elements, once"):
                for dst, src in ((theta_bc, theta_b), (phi_bc, phi_b), (g_bc, g_b), (out_bc, out_b),
                                 (scale_bc, ln_scale), (beta_c, ffn_beta)):
                    act.dma_start(dst, col(src)).then_inc(small_here, 16)
            act.dma_start(brow, ffn_bias.rearrange("(a d) -> a d", a=1)).then_inc(small_here, 16)

            def norm_x(t):
                act.wait_ge(a_nb_done, t + 1)
                for q in range(QT):
                    act.activation(x_in[:, q, :], x_in[:, q, :], ACT.Identity, bias=a_nb[:, q:q + 1],
                                   scale=a_rstd[:, q:q + 1]).then_inc(xn_done, 1)

            def xt_high(t):
                need(act, z_mm, t * 3 * KT)
                for k in range(KT):
                    act.wait_ge(xt_mm, t * KT + (k + 1))
                    act.activation(xt_hi[:, k, :], XT[k][:, :], ACT.Copy).then_inc(xt_hi_done, 1)

            def gate(t, m, e, tile, done):
                turn = TURN[m, e]
                act.wait_ge(z_mm, t * len(GROUPS) + (turn + 1))
                act.activation(tile[:, e, :], Z[turn % 3][:, :], ACT.Tanh, scale=0.5).then_inc(done, 1)

            def gate_r(t, e):
                need(act, rh_lo_done, t * KT)
                gate(t, R, e, r2, tr_done)

            def gate_f(t, e):
                need(act, hsq_mm, t)
                need(act, down_h, t * (LEVELS - 1))
                gate(t, F, e, fs, tf_done)
                act.wait_ge(tf_done, t * KT + (e + 1))
                act.activation(gs[:, e, :], fs[:, e, 0:D:2], ACT.Copy, bias=-0.5, scale=0.5).then_inc(f_less_done, 1)
                act.wait_ge(f_less_done, t * KT + (e + 1))
                act.activation(fs[:, e, :], fs[:, e, :], ACT.Copy, bias=0.5, scale=0.5).then_inc(f_done, 1)

            def gate_c(t, e):
                need(act, rh_done, t * KT)
                need(act, sq_done, t * KT)
                gate(t, C, e, cs, tc_done)

            def rh_high(t):
                for e in range(KT):
                    act.wait_ge(rh_done, t * KT + (e + 1))
                    need(act, av_mm, t * 2)
                    act.activation(rh_hi[:, e, :], r2[:, e, :], ACT.Copy).then_inc(rh_hi_done, 1)
                    if e == 0:
                        act.wait_ge(down_h, t * (LEVELS - 1) + (LEVELS - 1))
                    act.activation(fs[:, e, :], cs[:, e, :], ACT.Square).then_inc(sq_done, 1)

            def norm_f(n, b):
                act.wait_ge(b_nb_done, n + 1)
                need(act, fx_lo_done, n * ST)
                for s in range(ST):
                    act.activation(tt[:, s, :], res[:, b * ST + s, :], ACT.Identity,
                                   bias=b_nb[:, b * ST + s:b * ST + s + 1],
                                   scale=b_rstd[:, b * ST + s:b * ST + s + 1]).then_inc(fn_done, 1)

            def fx_high(n, b):
                if b == 0:
                    act.wait_ge(wo_mm, n * (QT // 2) + QT)
                else:
                    act.wait_ge(av_mm, n)
                for s in range(ST):
                    act.wait_ge(fn_done, n * ST + (s + 1))
                    act.activation(fx_hi[:, s, :], tt[:, s, :], ACT.Copy).then_inc(fx_hi_done, 1)

            def ctx_high(n):
                act.wait_ge(ctx_here, n * 16 + 16)
                need(act, ffn_mm, n * ST)
                act.activation(cz_hi[:, :].rearrange("p (s d) -> p s d", s=ST), cx[:, :, :], ACT.Copy)\
                   .then_inc(ctx_hi_done, 1)

            def proj_high(n):
                act.wait_ge(g_mm, n + 1)
                need(act, relu_lo_done, n)
                act.activation(gt[:, :], W[4][:, :], ACT.Copy).then_inc(gt_done, 1)
                act.wait_ge(ph_mm, n + 1)
                act.activation(ph_hi[:, :], W[3][:, :], ACT.Identity, bias=phi_bc).then_inc(ph_hi_done, 1)
                act.wait_ge(th_mm, n + 1)
                need(act, out_mm, n * ST)
                act.activation(th_hi[:, :], W[0][:, :], ACT.Identity, bias=theta_bc).then_inc(th_hi_done, 1)

            def g_high(n):
                act.wait_ge(g_t, n + 1)
                act.activation(g_hi[:, :, :].rearrange("p j l -> p (j l)"), W[2][:, :], ACT.Copy)\
                   .then_inc(g_hi_done, 1)

            def softmax(n):
                need(act, zg_t, n * 2)
                for k in range(KT + 1):
                    if k < KT:
                        act.wait_ge(nmax_done, n * KT + (k + 1))
                        act.activation(prob[:, k, :], SC[k][:, :], ACT.Exp, bias=nmax[:, k:k + 1],
                                       accum_out=rsum[:, k:k + 1]).then_inc(exp_done, 1)
                    if k:
                        act.wait_ge(rinv_done, n * KT + k)
                        act.activation(prob[:, k - 1, :], prob[:, k - 1, :], ACT.Copy, scale=rinv[:, k - 1:k])\
                           .then_inc(prob_done, 1)

            def pt_high(n):
                for k in range(KT):
                    act.wait_ge(prob_t, n * KT + (k + 1))
                    act.activation(pt_hi[:, k, :], W[k][:, :], ACT.Copy).then_inc(pt_hi_done, 1)

            def relu_high(n):
                act.wait_ge(t_bet_done, n + 1)
                act.activation(th_hi[:, :], gt[:, :], ACT.Relu).then_inc(relu_hi_done, 1)

            def z_high(n):
                for c, w in enumerate((W[3], W[0])):
                    act.wait_ge(zg_t, n * 2 + (c + 1))
                    act.activation(cz_hi[:, c * D:(c + 1) * D], w[:, :], ACT.Copy).then_inc(z_hi_done, 1)

            norm_x(0)
            act.wait_ge(w_here[F], 16)
            for k in range(KT):
                act.activation(w_hi[F][:, k, :], prob[:, k, :], ACT.Copy).then_inc(w_hi_done, 1)
            xt_high(0)
            act.wait_ge(w_here[C], 32)
            for k in range(KT):
                act.activation(w_hi[C][:, k, :], (cx if k < 2 else fin)[:, k % 2, :], ACT.Copy)\
                   .then_inc(w_hi_done, 1)
            gate_f(0, 0)
            act.wait_ge(w_here[R], 16)
            for k in range(KT):
                act.activation(w_hi[R][:, k, :], res[:, k, :], ACT.Copy).then_inc(w_hi_done, 1)
            gate_c(0, 0)
            gate_f(0, 1)
            for c in range(2):
                act.wait_ge(pj_t, c + 1)
                act.activation(pj_hi[:, 2 * c:2 * c + 2, :].rearrange("p m n -> p (m n)"), W[c][:, :],
                               ACT.Copy).then_inc(pj_hi_done, 1)
            gate_c(0, 1)
            gate_f(0, 2)
            gate_c(0, 2)
            gate_f(0, 3)
            gate_c(0, 3)
            gate_r(0, 0)
            act.wait_ge(col_done, 1)
            act.wait_ge(w_here[3], 16)
            for k in range(KT):
                act.activation(wo_hi[:, k, :], res[:, k, :], ACT.Copy, scale=scale_bc[:, k:k + 1])\
                   .then_inc(w_hi_done, 1)
            for k in range(KT):
                act.wait_ge(q_t, k + 1)
                act.activation(wq[:, k, :], W[k][:, :], ACT.Copy).then_inc(wq_done, 1)
            gate_r(0, 1)
            gate_r(0, 2)
            norm_x(1)
            gate_r(0, 3)

            def finish(t, load_next):
                rh_high(t)
                if load_next:
                    xt_high(t + 1)
                ctx_high(t * 2)
                norm_f(t * 2, 0)
                fx_high(t * 2, 0)

            finish(0, True)

            def back(i, b, gates, load_next):
                n = i * 2 + (b - 2)
                first, second = gates and b == 0, gates and b == 1
                if first:
                    gate_f(i, 0)
                    gate_c(i, 0)
                if second and load_next:
                    norm_x(i + 1)
                if b:
                    ctx_high(n)
                proj_high(n)
                if b == 0:
                    norm_f(n + 1, 1)
                g_high(n)
                softmax(n)
                if first:
                    gate_f(i, 1)
                if second:
                    gate_r(i, 0)
                pt_high(n)
                if first:
                    gate_c(i, 1)
                if b == 0:
                    fx_high(n + 1, 1)
                if first:
                    gate_f(i, 2)
                if second:
                    gate_r(i, 1)
                relu_high(n)
                if first:
                    gate_c(i, 2)
                    gate_f(i, 3)
                if second:
                    gate_r(i, 2)
                z_high(n)
                if first:
                    gate_c(i, 3)
                if second:
                    gate_r(i, 3)

            def step(i, load_next):
                back(i, 0, True, load_next)
                back(i, 1, True, load_next)
                finish(i, load_next)

            with act.Fori(1, PAIRS - 1) as i:
                step(i, True)
            step(PAIRS - 1, False)
            back(PAIRS, 0, False, False)
            back(PAIRS, 1, False, False)

        @block.tensor
        def _(pe):
            pe.wait_ge(const_done, 4)

            def transpose_x(t):
                pe.wait_ge(xn_done, t * QT + QT)
                need(pe, r_done, t * KT)
                for k in range(KT):
                    for q in range(QT):
                        mm = pe.transpose(XT[k][:, q * P:(q + 1) * P], x_in[:, q, k * P:(k + 1) * P], ident[:, :])
                    mm.then_inc(xt_mm, 1)

            free = (r_done, tf_done, c_done)

            def gates(t, first, count):
                for chunk in range(first, first + count):
                    turn, k = divmod(chunk, KT)
                    m, e = GROUPS[turn]
                    bank = Z[turn % 3]
                    if k == 0 and turn >= 3:
                        m_last, e_last = GROUPS[turn - 3]
                        pe.wait_ge(free[m_last], t * KT + (e_last + 1))
                    if turn == 0:
                        pe.wait_ge(xt_lo_done, t * KT + KT)
                    if e == 0 and isinstance(t, int) and t == 0:
                        pe.wait_ge(w_lo_done, (F, C, R).index(m) * KT + k + 1)
                    cut = slice(e * P, (e + 1) * P)
                    pe.matmul(bank[:, :], w_hi[m][:, k, cut], xt_hi[:, k, :], start=(k == 0), stop=False)
                    pe.matmul(bank[:, :], w_hi[m][:, k, cut], xt_lo[:, k, :], start=False, stop=False)
                    mm = pe.matmul(bank[:, :], w_lo[m][:, k, cut], xt_hi[:, k, :], start=False,
                                   stop=(k == KT - 1))
                    if k == KT - 1:
                        mm.then_inc(z_mm, 1)

            def mix_out(t, next_x):
                if isinstance(t, int) and t == 0:
                    pe.wait_ge(w_lo_done, 4 * KT)
                for b in range(2):
                    if b == 1:
                        if not isinstance(t, int) or t > 0:
                            need(pe, x3_done, t * QT)
                        if next_x:
                            pe.wait_ge(xt_lo_done, t * KT + (KT + 1))
                        pe.wait_ge(hsq_done, t * (KT - 1) + (KT - 1))
                        for q in range(QT):
                            mm = pe.matmul(W[4][:, q:q + 1], fs[:, 0, q * P:(q + 1) * P], avg[:, 0:1],
                                           start=True, stop=True)
                        mm.then_inc(hsq_mm, 1)
                    for k in range(KT):
                        pe.wait_ge(rh_lo_done, t * KT + (k + 1))
                        for q in range(b * ST, (b + 1) * ST):
                            cut = slice(q * P, (q + 1) * P)
                            pe.matmul(Y[q][:, :], rh_hi[:, k, cut], wo_hi[:, k, :], start=(k == 0), stop=False)
                            pe.matmul(Y[q][:, :], rh_hi[:, k, cut], wo_lo[:, k, :], start=False, stop=False)
                            mm = pe.matmul(Y[q][:, :], rh_lo[:, k, cut], wo_hi[:, k, :], start=False,
                                           stop=(k == KT - 1))
                            if k == KT - 1:
                                mm.then_inc(wo_mm, 1)

            def project(bank, m, hi, lo, done):
                for s in range(ST):
                    wt_hi, wt_lo = pj_hi[:, m, s * P:(s + 1) * P], pj_lo[:, m, s * P:(s + 1) * P]
                    pe.matmul(W[bank][:, :], wt_hi, hi[s], start=(s == 0), stop=False)
                    pe.matmul(W[bank][:, :], wt_hi, lo[s], start=False, stop=False)
                    mm = pe.matmul(W[bank][:, :], wt_lo, hi[s], start=False, stop=(s == ST - 1))
                mm.then_inc(done, 1)

            def projections(n, b, fill):
                pe.wait_ge(fx_lo_done, n * ST + ST)
                if b == 0:
                    need(pe, x1_done, n * ST + 2 * ST)
                fh = [fx_hi[:, s, :] for s in range(ST)]
                fl = [fx_lo[:, s, :] for s in range(ST)]
                project(4, 2, fh, fl, g_mm)
                project(3, 1, fh, fl, ph_mm)
                fill(2 * b)
                pe.wait_ge(ctx_lo_done, n + 1)
                ch = [cz_hi[:, s * D:(s + 1) * D] for s in range(ST)]
                cl = [cz_lo[:, s * D:(s + 1) * D] for s in range(ST)]
                project(0, 0, ch, cl, th_mm)

            def turn_g(n, b):
                pe.wait_ge(gt_done, n + 1)
                if b:
                    need(pe, x3_done, n * ST)
                for j in range(KT):
                    mm = pe.transpose(W[2][:, j * P:(j + 1) * P], gt[:, j * P:(j + 1) * P], ident[:, :])
                mm.then_inc(g_t, 1)

            def scores(n):
                pe.wait_ge(th_lo_done, n + 1)
                pe.wait_ge(ph_lo_done, n + 1)
                for k in range(KT):
                    if k == 3:
                        pe.wait_ge(g_lo_done, n + 1)
                    cut = slice(k * P, (k + 1) * P)
                    pe.matmul(SC[k][:, :], th_hi[:, cut], ph_hi[:, :], start=True, stop=False)
                    pe.matmul(SC[k][:, :], th_hi[:, cut], ph_lo[:, :], start=False, stop=False)
                    pe.matmul(SC[k][:, :], th_lo[:, cut], ph_hi[:, :], start=False, stop=True).then_inc(score_mm, 1)

            def turn_prob(n):
                pe.wait_ge(prob_done, n * KT + KT)
                for j in range(KT):
                    for k in range(KT):
                        mm = pe.transpose(W[j][:, k * P:(k + 1) * P], prob[:, k, j * P:(j + 1) * P], ident[:, :])
                    mm.then_inc(prob_t, 1)

            def attend(n):
                for j in range(KT):
                    pe.wait_ge(pt_lo_done, n * KT + (j + 1))
                    pe.matmul(W[4][:, :], g_hi[:, j, :], pt_hi[:, j, :], start=(j == 0), stop=False)
                    pe.matmul(W[4][:, :], g_hi[:, j, :], pt_lo[:, j, :], start=False, stop=False)
                    mm = pe.matmul(W[4][:, :], g_lo[:, j, :], pt_hi[:, j, :], start=False, stop=(j == KT - 1))
                mm.then_inc(av_mm, 1)

            def mean_over(n):
                pe.wait_ge(t_mean_done, n + 1)
                pe.matmul(W[0][:, 0:1], avg[:, :], t_s[:, 0:1], start=True, stop=True).then_inc(mean_mm, 1)

            def second_over(n):
                pe.wait_ge(t_sec_done, n + 1)
                pe.matmul(W[3][:, 0:1], avg[:, :], t_s[:, 2:3], start=True, stop=True).then_inc(sec_mm, 1)

            def attn_out(n):
                pe.wait_ge(relu_lo_done, n + 1)
                for o in range(ST):
                    cut = slice(o * P, (o + 1) * P)
                    pe.matmul(W[1 + o][:, :], pj_hi[:, 3, cut], th_hi[:, :], start=True, stop=False)
                    pe.matmul(W[1 + o][:, :], pj_hi[:, 3, cut], th_lo[:, :], start=False, stop=False)
                    pe.matmul(W[1 + o][:, :], pj_lo[:, 3, cut], th_hi[:, :], start=False, stop=True)\
                      .then_inc(out_mm, 1)

            def turn_z(n):
                pe.wait_ge(zg_done, n * ST + ST)
                for c, w in enumerate((W[3], W[0])):
                    for k in range(2):
                        for s in range(ST):
                            at = (k * ST + s) * P
                            mm = pe.transpose(w[:, at:at + P], fz[:, s, (2 * c + k) * P:(2 * c + k + 1) * P],
                                              ident[:, :])
                    mm.then_inc(zg_t, 1)

            def feed(n):
                pe.wait_ge(z_lo_done, n * 2 + 2)
                for s in range(ST):
                    for k in range(KT):
                        at = (k * ST + s) * P
                        pe.matmul(W[1 + s][:, :], cz_hi[:, at:at + P], wq[:, k, :], start=(k == 0), stop=False)
                        mm = pe.matmul(W[1 + s][:, :], cz_lo[:, at:at + P], wq[:, k, :], start=False,
                                       stop=(k == KT - 1))
                    mm.then_inc(ffn_mm, 1)

            transpose_x(0)
            gates(0, 0, 16)
            pe.wait_ge(pj_here, 64)
            pe.wait_ge(xt_lo_done, KT)
            src = [cx[:, 0, 0:256], cx[:, 0, 256:512], cx[:, 1, 0:256], fin[:, 0, 0:256]]
            for m in range(4):
                for h in range(2):
                    at = ((m % 2) * 2 + h) * P
                    mm = pe.transpose(W[m // 2][:, at:at + P], src[m][:, h * P:(h + 1) * P], ident[:, :])
                if m % 2:
                    mm.then_inc(pj_t, 1)
            gates(0, 16, 4)
            pe.wait_ge(abs_done, 1)
            pe.matmul(W[4][:, 0:1], avg[:, :], abs_sum, start=True, stop=True).then_inc(abs_mean, 1)
            gates(0, 20, 14)
            pe.wait_ge(pj_lo_done, 2)
            pe.wait_ge(q_done, KT)
            for k in range(KT):
                for o in range(KT):
                    mm = pe.transpose(W[k][:, o * P:(o + 1) * P], prob[:, o, k * P:(k + 1) * P], ident[:, :])
                mm.then_inc(q_t, 1)
            gates(0, 34, 6)
            pe.wait_ge(beta_done, KT)
            pe.wait_ge(wq_done, KT)
            for k in range(KT):
                pe.matmul(W[4][:, :], beta_w[:, k * P:(k + 1) * P], f32(wq[:, k, :]), start=(k == 0), stop=False)
            pe.matmul(W[4][:, :], ones[0:1, :], brow, start=False, stop=True).then_inc(bias_mm, 1)
            gates(0, 40, 8)
            transpose_x(1)
            pe.wait_ge(bias_done, 1)
            mix_out(0, True)

            FILLS = ((8, 2, 5, 3, 2, 1, 5, 4, 2), (0, 0, 4, 2, 2, 1, 2, 2, 1))
            assert sum(FILLS[0]) == 8 * KT and sum(FILLS[1]) + 2 == 4 * KT

            def back(i, b, with_gates):
                n = i * 2 + (b - 2)
                at = [32 * b]
                fills = FILLS[b]

                def fill(count):
                    if with_gates:
                        gates(i, at[0], count)
                    at[0] += count

                fill(fills[0])
                projections(n, b, fill)
                fill(fills[1])
                turn_g(n, b)
                scores(n)
                fill(fills[2])
                turn_prob(n)
                fill(fills[3])
                attend(n)
                fill(fills[4])
                mean_over(n)
                fill(fills[5])
                second_over(n)
                fill(fills[6])
                attn_out(n)
                fill(fills[7])
                turn_z(n)
                fill(fills[8])
                feed(n)

            def step(i, load_next):
                back(i, 0, True)
                back(i, 1, True)
                if load_next:
                    transpose_x(i + 1)
                mix_out(i, load_next)

            with pe.Fori(1, PAIRS - 1) as i:
                step(i, True)
            step(PAIRS - 1, False)
            back(PAIRS, 0, False)
            back(PAIRS, 1, False)

        @block.vector
        def _(dve):
            def stats(raw, mv, ve, tile, count, mv_done, ve_done, first, mul, add):
                for q in range(count):
                    dve.bn_stats(raw[:, q, :], tile(q))
                dve.drain()
                for q in range(count):
                    dve.bn_aggr(mv[:, q, :], raw[:, q, :]).then_inc(mv_done, 1)
                dve.wait_ge(mv_done, first + count)
                dve.tensor_scalar(ve[:, :], mv[:, :, 1], mul, add, ALU.mult, ALU.add).then_inc(ve_done, 1)

            def stats_x(t):
                dve.wait_ge(x_here, t * 16 + 16)
                stats(a_raw, a_mv, a_ve, lambda q: x_in[:, q, :], QT, a_mv_done, a_ve_done,
                      t * QT, 1.0, EPS)

            def shift_x(t):
                dve.wait_ge(a_rstd_done, t + 1)
                dve.scalar_tensor_tensor(out=a_nb[:, :], in0=a_mv[:, :, 0], scalar=-1.0, in1=a_rstd[:, :],
                                         op0=ALU.mult, op1=ALU.mult).then_inc(a_nb_done, 1)

            def xt_low(t, tiles):
                for k in tiles:
                    dve.wait_ge(xt_hi_done, t * KT + (k + 1))
                    dve.tensor_tensor(xt_lo[:, k, :], XT[k][:, :], f32(xt_hi[:, k, :]), ALU.subtract)\
                       .then_inc(xt_lo_done, 1)

            def gate(t, m, e, tile, tanh_done, done):
                dve.wait_ge(tanh_done, t * KT + (e + 1))
                dve.scalar_tensor_tensor(out=tile[:, e, :], in0=tile[:, e, :], scalar=1.0,
                                         in1=Z[TURN[m, e] % 3][:, :], op0=ALU.add, op1=ALU.mult).then_inc(done, 1)

            def gate_r(t, e):
                gate(t, R, e, r2, tr_done, r_done)

            def gate_c(t, e):
                gate(t, C, e, cs, tc_done, c_done)

            def up(t, l):
                step = 2 << l
                ca, fb, cb = level(cs, step // 2 - 1, step), level(fs, step - 1, step), level(cs, step - 1, step)
                product = products(S // step)
                if l == 0:
                    dve.wait_ge(f_done, t * KT + KT)
                    dve.wait_ge(c_done, t * KT + KT)
                else:
                    dve.wait_ge(up_f, t * (LEVELS - 1) + l)
                    dve.wait_ge(up_c, t * LEVELS + l)
                dve.tensor_tensor(product, fb, ca, ALU.mult).then_inc(up_t, 1)
                if l == 0:
                    f, c = fb, cb
                else:
                    f, c = level(fs, step - 1, step // 2), level(cs, step - 1, step // 2)
                dve.wait_ge(up_t, t * LEVELS + (l + 1))
                dve.scalar_tensor_tensor(out=c, in0=f, scalar=-1.0, in1=c, op0=ALU.add, op1=ALU.mult)\
                   .then_inc(up_g, 1)
                if 2 <= l < LEVELS - 1:
                    up_product_f(dve, t, l)
                dve.wait_ge(up_g, t * LEVELS + (l + 1))
                dve.tensor_tensor(cb, product, cb, ALU.subtract).then_inc(up_c, 1)

            def down(t, l):
                step, turn = 2 << l, LEVELS - 2 - l
                start = step + step // 2 - 1
                f, c, before = level(fs, start, step), level(cs, start, step), level(cs, step - 1, step, less=1)
                product = products(S // step - 1)
                dve.wait_ge(up_c, t * LEVELS + LEVELS)
                need(dve, down_h, t * (LEVELS - 1) + turn)
                dve.tensor_tensor(product, f, before, ALU.mult).then_inc(down_t, 1)
                dve.wait_ge(down_t, t * (LEVELS - 1) + (turn + 1))
                if l:
                    g = c
                else:
                    dve.wait_ge(g0_done, t * KT + KT)
                    g = gs[:, :, :].rearrange("p e (s n) -> p (e s) n", n=S // 2)[:, :, 1:]
                dve.tensor_tensor(c, product, g, ALU.subtract).then_inc(down_h, 1)

            def rh_product(t, e):
                dve.wait_ge(down_h, t * (LEVELS - 1) + (LEVELS - 1))
                dve.wait_ge(r_done, t * KT + (e + 1))
                dve.tensor_tensor(r2[:, e, :], r2[:, e, :], cs[:, e, :], ALU.mult).then_inc(rh_done, 1)

            def rh_low(t, e):
                dve.wait_ge(rh_hi_done, t * KT + (e + 1))
                dve.tensor_tensor(rh_lo[:, e, :], r2[:, e, :], f32(rh_hi[:, e, :]), ALU.subtract)\
                   .then_inc(rh_lo_done, 1)

            def mix(t):
                rh_product(t, 0)
                for e in range(1, KT):
                    rh_product(t, e)
                    rh_low(t, e - 1)
                rh_low(t, KT - 1)

            def residual_1(t, b):
                dve.wait_ge(m_rstd_done, t + 1)
                dve.wait_ge(res_here[b], t * 16 + 16)
                for q in range(b * ST, (b + 1) * ST):
                    dve.wait_ge(wo_mm, t * QT + (q + 1))
                    dve.scalar_tensor_tensor(out=res[:, q, :], in0=Y[q][:, :], scalar=m_rstd[:, q:q + 1],
                                             in1=res[:, q, :], op0=ALU.mult, op1=ALU.add).then_inc(x1_done, 1)
                n = t * 2 + b
                part = slice(b * ST, (b + 1) * ST)
                dve.wait_ge(x1_done, n * ST + ST)
                stats(b_raw[:, part, :], b_mv[:, part, :], b_ve[:, part], lambda s: res[:, b * ST + s, :], ST,
                      b_mv_done, b_ve_done, n * ST, 1.0, EPS)

            def shift_b(n, b):
                part = slice(b * ST, (b + 1) * ST)
                dve.wait_ge(b_rstd_done, n + 1)
                dve.scalar_tensor_tensor(out=b_nb[:, part], in0=b_mv[:, part, 0], scalar=-1.0, in1=b_rstd[:, part],
                                         op0=ALU.mult, op1=ALU.mult).then_inc(b_nb_done, 1)

            def fx_low(n):
                for s in range(ST):
                    dve.wait_ge(fx_hi_done, n * ST + (s + 1))
                    dve.tensor_tensor(fx_lo[:, s, :], tt[:, s, :], f32(fx_hi[:, s, :]), ALU.subtract)\
                       .then_inc(fx_lo_done, 1)

            def finish(t, load_next, last=None):
                down(t, 0)
                mix(t)
                if last is not None:
                    residual_3(last)
                if load_next:
                    xt_low(t + 1, (0,))
                dve.wait_ge(hsq_mm, t + 1)
                dve.tensor_scalar(m_ve[:, :], W[4][:, 0:QT], P / (4 * D), EPS, ALU.mult, ALU.add)\
                   .then_inc(m_ve_done, 1)
                if load_next:
                    xt_low(t + 1, range(1, KT))
                residual_1(t, 0)
                residual_1(t, 1)
                shift_b(t * 2, 0)
                fx_low(t * 2)
                shift_b(t * 2 + 1, 1)

            def proj_low(n):
                dve.wait_ge(ph_hi_done, n + 1)
                dve.scalar_tensor_tensor(out=ph_lo[:, :], in0=W[3][:, :], scalar=phi_bc, in1=f32(ph_hi[:, :]),
                                         op0=ALU.add, op1=ALU.subtract).then_inc(ph_lo_done, 1)
                dve.wait_ge(th_hi_done, n + 1)
                dve.scalar_tensor_tensor(out=th_lo[:, :], in0=W[0][:, :], scalar=theta_bc, in1=f32(th_hi[:, :]),
                                         op0=ALU.add, op1=ALU.subtract).then_inc(th_lo_done, 1)

            def g_low(n):
                dve.wait_ge(g_hi_done, n + 1)
                dve.tensor_tensor(g_lo[:, :, :].rearrange("p j l -> p (j l)"), W[2][:, :],
                                  f32(g_hi[:, :, :]).rearrange("p j l -> p (j l)"), ALU.subtract)\
                   .then_inc(g_lo_done, 1)

            def row_max(n, k):
                dve.wait_ge(score_mm, n * KT + (k + 1))
                dve.tensor_reduce(nmax[:, k:k + 1], SC[k][:, :], AX.X, ALU.max, negate=True).then_inc(nmax_done, 1)

            def row_norm(n, k):
                dve.wait_ge(exp_done, n * KT + (k + 1))
                dve.reciprocal(rinv[:, k:k + 1], rsum[:, k:k + 1]).then_inc(rinv_done, 1)

            def softmax(n):
                row_max(n, 0)
                row_max(n, 1)
                row_norm(n, 0)
                row_max(n, 2)
                row_norm(n, 1)
                row_max(n, 3)
                row_norm(n, 2)
                row_norm(n, 3)

            def pt_low(n):
                for k in range(KT):
                    dve.wait_ge(pt_hi_done, n * KT + (k + 1))
                    dve.tensor_tensor(pt_lo[:, k, :], W[k][:, :], f32(pt_hi[:, k, :]), ALU.subtract)\
                       .then_inc(pt_lo_done, 1)

            def t_mean(n):
                dve.wait_ge(av_mm, n + 1)
                dve.bn_stats(t_raw, W[4][:, :])
                dve.drain()
                dve.bn_aggr(t_mv[:, :], t_raw).then_inc(t_mv_done, 1)
                dve.wait_ge(t_mv_done, n + 1)
                dve.tensor_scalar(t_s[:, 0:1], t_mv[:, 0:1], g_bc, None, ALU.add).then_inc(t_mean_done, 1)

            def t_second(n):
                dve.wait_ge(mean_mm, n + 1)
                dve.tensor_scalar(t_s[:, 1:2], t_s[:, 0:1], W[0][:, 0:1], None, ALU.subtract).then_inc(t_dist_done, 1)
                dve.tensor_scalar(t_s[:, 3:4], g_bc, W[0][:, 0:1], None, ALU.subtract).then_inc(t_dist_done, 1)
                dve.wait_ge(t_dist_done, n * 2 + 2)
                dve.scalar_tensor_tensor(out=t_s[:, 2:3], in0=t_s[:, 1:2], scalar=t_s[:, 1:2], in1=t_mv[:, 1:2],
                                         op0=ALU.mult, op1=ALU.add).then_inc(t_sec_done, 1)
                dve.scalar_tensor_tensor(out=gt[:, :], in0=W[4][:, :], scalar=t_s[:, 3:4], in1=gamma_lt[:, :],
                                         op0=ALU.add, op1=ALU.mult).then_inc(t_gam_done, 1)

            def t_var(n):
                dve.wait_ge(sec_mm, n + 1)
                dve.tensor_scalar(t_s[:, 4:5], W[3][:, 0:1], EPS, None, ALU.add).then_inc(t_ve_done, 1)

            def t_norm(n):
                dve.wait_ge(t_rstd_done, n + 1)
                dve.wait_ge(t_gam_done, n + 1)
                dve.scalar_tensor_tensor(out=gt[:, :], in0=gt[:, :], scalar=t_s[:, 5:6], in1=beta_lt[:, :],
                                         op0=ALU.mult, op1=ALU.add).then_inc(t_bet_done, 1)

            def relu_low(n):
                dve.wait_ge(relu_hi_done, n + 1)
                dve.scalar_tensor_tensor(out=th_lo[:, :], in0=gt[:, :], scalar=0.0, in1=f32(th_hi[:, :]),
                                         op0=ALU.max, op1=ALU.subtract).then_inc(relu_lo_done, 1)

            def residual_2(n, b):
                dve.wait_ge(cx_done, n + 1)
                for o in range(ST):
                    dve.wait_ge(out_mm, n * ST + (o + 1))
                    dve.scalar_tensor_tensor(out=res[:, b * ST + o, :], in0=W[1 + o][:, :],
                                             scalar=out_bc[:, o:o + 1], in1=cx[:, o, :],
                                             op0=ALU.add, op1=ALU.add).then_inc(x2_done, 1)

            def stats_c(n, b):
                dve.wait_ge(x2_done, n * ST + ST)
                stats(c_raw, c_mv, c_ve, lambda s: res[:, b * ST + s, :], ST, c_mv_done,
                      c_ve_done, n * ST, 1.0 + EPS, EPS * EPS)
                for s in range(ST):
                    dve.scalar_tensor_tensor(out=fz[:, s, :], in0=res[:, b * ST + s, :], scalar=c_mv[:, s, 0:1],
                                             in1=gamma_bc[:, :], op0=ALU.subtract, op1=ALU.mult)\
                       .then_inc(zg_done, 1)

            def z_low(n):
                for c, w in enumerate((W[3], W[0])):
                    dve.wait_ge(z_hi_done, n * 2 + (c + 1))
                    dve.tensor_tensor(cz_lo[:, c * D:(c + 1) * D], w[:, :], f32(cz_hi[:, c * D:(c + 1) * D]),
                                      ALU.subtract).then_inc(z_lo_done, 1)

            def residual_3(n):
                dve.wait_ge(fin_done, n * ST + ST)
                dve.wait_ge(c_rstd_done, n + 1)
                for s in range(ST):
                    dve.wait_ge(ffn_mm, n * ST + (s + 1))
                    dve.scalar_tensor_tensor(out=fin[:, s, :], in0=W[1 + s][:, :], scalar=c_rstd[:, s:s + 1],
                                             in1=fin[:, s, :], op0=ALU.mult, op1=ALU.add).then_inc(x3_done, 1)

            stats_x(0)
            shift_x(0)
            for k in range(KT):
                dve.wait_ge(w_hi_done, k + 1)
                dve.tensor_tensor(w_lo[F][:, k, :], prob[:, k, :], f32(w_hi[F][:, k, :]), ALU.subtract)\
                   .then_inc(w_lo_done, 1)
            xt_low(0, range(KT))
            for k in range(KT):
                dve.wait_ge(w_hi_done, KT + k + 1)
                dve.tensor_tensor(w_lo[C][:, k, :], (cx if k < 2 else fin)[:, k % 2, :], f32(w_hi[C][:, k, :]),
                                  ALU.subtract).then_inc(w_lo_done, 1)
            for k in range(KT):
                dve.wait_ge(w_hi_done, 2 * KT + k + 1)
                dve.tensor_tensor(w_lo[R][:, k, :], res[:, k, :], f32(w_hi[R][:, k, :]), ALU.subtract)\
                   .then_inc(w_lo_done, 1)
            gate_c(0, 0)
            dve.wait_ge(small_here, 16 * 10)
            dve.tensor_scalar(scale_bc, scale_bc, 0.25, None, ALU.mult).then_inc(col_done, 1)
            dve.wait_ge(q_here, 16)
            dve.tensor_reduce(abs_sum, prob[:, :, :], AX.XY, ALU.add, apply_absolute_value=True).then_inc(abs_done, 1)
            for c in range(2):
                dve.wait_ge(pj_hi_done, c + 1)
                dve.tensor_tensor(pj_lo[:, 2 * c:2 * c + 2, :].rearrange("p m n -> p (m n)"), W[c][:, :],
                                  f32(pj_hi[:, 2 * c:2 * c + 2, :]).rearrange("p m n -> p (m n)"), ALU.subtract)\
                   .then_inc(pj_lo_done, 1)
            gate_c(0, 1)
            dve.wait_ge(abs_mean, 1)
            half = 0.5 / (D * D // P)
            dve.tensor_scalar(thr, W[4][:, 0:1], half, 0.5 * Q_EPS, ALU.mult, ALU.add).then_inc(thr_done, 1)
            dve.tensor_scalar(neg_thr, W[4][:, 0:1], -half, -0.5 * Q_EPS, ALU.mult, ALU.add).then_inc(thr_done, 1)
            dve.wait_ge(thr_done, 2)
            for o in range(KT):
                need(dve, q_done, o)
                dve.tensor_scalar(gt[:, :], prob[:, o, :], neg_thr, None, ALU.is_lt).then_inc(below_done, 1)
                dve.wait_ge(below_done, o + 1)
                dve.scalar_tensor_tensor(out=prob[:, o, :], in0=prob[:, o, :], scalar=thr, in1=gt[:, :],
                                         op0=ALU.is_gt, op1=ALU.subtract).then_inc(q_done, 1)
            gate_c(0, 2)
            dve.wait_ge(const_done, 4)
            for k in range(KT):
                dve.tensor_scalar(beta_w[:, k * P:(k + 1) * P], ones, beta_c[:, k:k + 1], None, ALU.mult)\
                   .then_inc(beta_done, 1)
            gate_c(0, 3)
            gate_r(0, 0)
            for k in range(KT):
                dve.wait_ge(w_hi_done, 3 * KT + k + 1)
                dve.scalar_tensor_tensor(out=wo_lo[:, k, :], in0=res[:, k, :], scalar=scale_bc[:, k:k + 1],
                                         in1=f32(wo_hi[:, k, :]), op0=ALU.mult, op1=ALU.subtract)\
                   .then_inc(w_lo_done, 1)
            dve.wait_ge(bias_mm, 1)
            dve.tensor_copy(bias_bc[:, :], W[4][:, :]).then_inc(bias_done, 1)
            up(0, 0)
            gate_r(0, 1)
            up(0, 1)
            stats_x(1)
            shift_x(1)
            gate_r(0, 2)
            for l in range(2, LEVELS):
                up(0, l)
            for l in range(LEVELS - 2, 0, -1):
                down(0, l)
            gate_r(0, 3)
            finish(0, True)

            def back(i, b, gates, load_next):
                n = i * 2 + (b - 2)
                first, second = gates and b == 0, gates and b == 1
                if first:
                    if load_next:
                        stats_x(i + 1)
                        shift_x(i + 1)
                    gate_c(i, 0)
                if b:
                    residual_3(n - 1)
                if second:
                    up(i, 0)
                proj_low(n)
                g_low(n)
                if second:
                    up(i, 1)
                softmax(n)
                if second:
                    gate_r(i, 0)
                    up(i, 2)
                pt_low(n)
                if first:
                    gate_c(i, 1)
                if second:
                    up(i, 3)
                    up(i, 4)
                t_mean(n)
                if second:
                    up(i, 5)
                t_second(n)
                if b == 0:
                    fx_low(n + 1)
                if second:
                    up(i, 6)
                    up(i, 7)
                t_var(n)
                if second:
                    gate_r(i, 1)
                    down(i, 6)
                    down(i, 5)
                t_norm(n)
                relu_low(n)
                if first:
                    gate_c(i, 2)
                if second:
                    down(i, 4)
                    down(i, 3)
                residual_2(n, b)
                stats_c(n, b)
                if second:
                    gate_r(i, 2)
                    down(i, 2)
                    down(i, 1)
                z_low(n)
                if first:
                    gate_c(i, 3)
                if second:
                    gate_r(i, 3)

            def step(i, load_next):
                back(i, 0, True, load_next)
                back(i, 1, True, load_next)
                finish(i, load_next, i * 2 - 1)

            with dve.Fori(1, PAIRS - 1) as i:
                step(i, True)
            step(PAIRS - 1, False)
            back(PAIRS, 0, False, False)
            back(PAIRS, 1, False, False)
            residual_3(2 * PAIRS - 1)


_INS = ['x', 'ctx_2048', 'L0_attn_Wr', 'L0_attn_Wf', 'L0_attn_Wc', 'L0_attn_Wo', 'L0_attn_ln_scale',
        'L0_xattn_theta_w', 'L0_xattn_theta_b', 'L0_xattn_phi_w', 'L0_xattn_phi_b', 'L0_xattn_g_w',
        'L0_xattn_g_b', 'L0_xattn_ln_gamma', 'L0_xattn_ln_beta', 'L0_xattn_out_w', 'L0_xattn_out_b',
        'L0_ffn_weight', 'L0_ffn_bias', 'L0_ffn_ln_gamma', 'L0_ffn_ln_beta']
_OUT = ((16, 256, 512), 'float32')


def kernel(**inputs):
    import numpy as _np
    import concourse.bacc as _bacc
    from concourse import mybir as _mybir
    from concourse.bass_utils import run_bass_kernel_spmd as _run

    nc = _bacc.Bacc("TRN2", target_bir_lowering=False, num_devices=1)
    arrays, args = {}, []
    for name in _INS:
        a = _np.ascontiguousarray(inputs[name])
        arrays[f"in_{name}_dram"] = a
        args.append(nc.dram_tensor(f"in_{name}_dram", a.shape, _mybir.dt.from_np(a.dtype), kind="ExternalInput").ap())
    shape, dtype = _OUT
    args.append(nc.dram_tensor("out_0_dram", shape, _mybir.dt.from_np(_np.dtype(dtype)), kind="ExternalOutput").ap())
    build(nc, *args)
    r = _run(nc, [arrays], core_ids=[0])
    return r.results[0]["out_0_dram"]
```

```python
from contextlib import ExitStack

import concourse.bass as bass
from concourse import mybir

F32 = mybir.dt.float32
F32R = mybir.dt.float32r
ALU = mybir.AluOpType
ACT = mybir.ActivationFunctionType
AX = mybir.AxisListType

P = 128
EPS = 1e-5
Q_EPS = 1e-5


def need(eng, sem, value):
    if not isinstance(value, int) or value > 0:
        eng.wait_ge(sem, value)


def f32(ap):
    return ap.bitcast(F32)


def build(nc, x, ctx_in, wr, wf, wc, wo, ln_scale, theta_w, theta_b, phi_w, phi_b, g_w, g_b,
          ln_gamma, ln_beta, out_w, out_b, ffn_w, ffn_bias, ffn_gamma, ffn_beta, out):
    B, S, D = x.shape
    L = theta_w.shape[0]
    PAIRS = B // 2
    KT = D // P
    LEVELS = S.bit_length() - 1
    TOP = 4
    assert S == 1 << LEVELS
    ST = S // P
    QT = 2 * ST
    R, F, C = range(3)
    GROUPS = [(m, e) for e in range(KT) for m in (F, C)] + [(R, e) for e in range(KT)]
    TURN = {group: n for n, group in enumerate(GROUPS)}
    assert len(GROUPS) % 3 == 0
    assert L == P and D == 512 and S == 256 and B % 2 == 0 and PAIRS >= 3

    x_rows = x.rearrange("b (s p) d -> p (b s) d", p=P)
    ctx_rows = ctx_in.rearrange("b (s p) d -> p (b s) d", p=P)
    out_rows = out.rearrange("b (s p) d -> p (b s) d", p=P)

    stack = ExitStack()
    with stack:
        def sb(name, shape, dt=F32):
            return stack.enter_context(nc.sbuf_tensor(name, shape, dt))

        def sem(name):
            return stack.enter_context(nc.semaphore(name))

        ident = sb("ident", [P, P])
        avg = sb("avg", [P, P])
        minus_half = sb("minus_half", [P, 4])
        w_hi = [sb(f"w{m}_hi", [P, KT, D], F32R) for m in "rfc"]
        w_lo = [sb(f"w{m}_lo", [P, KT, D], F32R) for m in "rfc"]
        wo_hi = sb("wo_hi", [P, KT, D], F32R)
        wo_lo = sb("wo_lo", [P, KT, D], F32R)
        wq = sb("wq", [P, KT, D], F32R)
        pj_hi = sb("pj_hi", [P, 4, 2 * P], F32R)
        pj_lo = sb("pj_lo", [P, 4, 2 * P], F32R)
        gamma_lt = sb("gamma_lt", [P, D])
        beta_lt = sb("beta_lt", [P, D])
        gamma_bc = sb("gamma_bc", [P, D])
        bias_bc = sb("bias_bc", [P, D])
        cols = sb("cols", [P, 16])
        theta_bc, phi_bc, g_bc = cols[:, 0:1], cols[:, 1:2], cols[:, 2:3]
        out_bc, scale_bc, beta_c = cols[:, 3:5], cols[:, 5:9], cols[:, 9:13]
        thr, neg_thr, abs_sum = cols[:, 13:14], cols[:, 14:15], cols[:, 15:16]

        x_in = sb("x_in", [P, QT, D])
        xt_hi = sb("xt_hi", [P, KT, D], F32R)
        xt_lo = sb("xt_lo", [P, KT, D], F32R)
        r2 = sb("r2", [P, KT, D])
        fs = sb("fs", [P, KT, D])
        cs = sb("cs", [P, KT, D])
        gs = sb("gs", [P, KT, D // 2])
        tt = sb("tt", [P, 2, D])
        res = sb("res", [P, QT, D])
        cx = sb("cx", [P, ST, D])
        fin = sb("fin", [P, ST, D])
        cz_hi = sb("cz_hi", [P, 2 * D], F32R)
        cz_lo = sb("cz_lo", [P, 2 * D], F32R)
        th_hi = sb("th_hi", [P, D], F32R)
        th_lo = sb("th_lo", [P, D], F32R)
        ph_hi = sb("ph_hi", [P, D], F32R)
        ph_lo = sb("ph_lo", [P, D], F32R)
        gt = sb("gt", [P, D])
        g_hi = sb("g_hi", [P, KT, P], F32R)
        g_lo = sb("g_lo", [P, KT, P], F32R)
        prob = sb("prob", [P, KT, D])
        fz = prob[:, 0:ST, :]
        pt_hi = sb("pt_hi", [P, KT, D], F32R)
        pt_lo = sb("pt_lo", [P, KT, D], F32R)
        rh_hi, rh_lo = pt_hi, pt_lo
        beta_w = fin[:, 1, :]
        fx_hi, fx_lo = pt_hi[:, 0:ST, :], pt_lo[:, 0:ST, :]
        a_raw = sb("a_raw", [P, QT, 6])
        a_mv = sb("a_mv", [P, QT, 2])
        t_raw = sb("t_raw", [P, 6])
        per_row = sb("per_row", [P, 16, QT])
        a_ve, a_rstd, a_nb, m_ve, m_rstd, b_ve, b_rstd, b_nb, nmax, rsum, rinv = (per_row[:, n, :] for n in range(11))
        b_sum, b_mean = (per_row[:, n, :] for n in (11, 12))
        c_ve, c_rstd, c_sum, c_mean = (per_row[:, 13 + n // 2, (n % 2) * ST:(n % 2 + 1) * ST] for n in range(4))
        t_mv = sb("t_mv", [P, 2])
        t_s = sb("t_s", [P, 6])

        Z = [stack.enter_context(nc.psum_tensor(f"z{m}", [P, D], F32)) for m in range(3)]
        W = [stack.enter_context(nc.psum_tensor(f"work{n}", [P, D], F32)) for n in range(5)]
        XT = [Z[0], Z[1], Z[2], W[4]]
        SC = [W[1], W[3], W[0], W[2]]
        Y = [W[0], W[3], W[1], W[2]]

        x_here = sem("x_here")
        res_here = [sem(f"res_here_{b}") for b in range(2)]
        ctx_here = sem("ctx_here")
        stored = sem("stored")
        w_here = [sem(f"w{m}_here") for m in "rfco"]
        q_here = sem("q_here")
        pj_here = sem("pj_here")
        small_here = sem("small_here")
        wide_here = sem("wide_here")
        ident_zero = sem("ident_zero")
        const_done = sem("const_done")
        w_hi_done = sem("w_hi_done")
        w_lo_done = sem("w_lo_done")
        col_done = sem("col_done")
        abs_done = sem("abs_done")
        abs_mean = sem("abs_mean")
        thr_done = sem("thr_done")
        below_done = sem("below_done")
        q_done = sem("q_done")
        q_t = sem("q_t")
        wq_done = sem("wq_done")
        beta_done = sem("beta_done")
        bias_mm = sem("bias_mm")
        bias_done = sem("bias_done")
        pj_t = sem("pj_t")
        pj_hi_done = sem("pj_hi_done")
        pj_lo_done = sem("pj_lo_done")
        a_mv_done = sem("a_mv_done")
        a_ve_done = sem("a_ve_done")
        a_rstd_done = sem("a_rstd_done")
        a_nb_done = sem("a_nb_done")
        xn_done = sem("xn_done")
        xt_mm = sem("xt_mm")
        xt_hi_done = sem("xt_hi_done")
        xt_lo_done = sem("xt_lo_done")
        z_mm = sem("z_mm")
        tr_done = sem("tr_done")
        tf_done = sem("tf_done")
        tc_done = sem("tc_done")
        r_done = sem("r_done")
        f_less_done = sem("f_less_done")
        f_done = sem("f_done")
        c_done = sem("c_done")
        g0_done = sem("g0_done")
        up0_t = sem("up0_t")
        up0_g = sem("up0_g")
        up0_f = sem("up0_f")
        up0_c = sem("up0_c")
        up_t = sem("up_t")
        up_g = sem("up_g")
        up_f = sem("up_f")
        up_c = sem("up_c")
        top_diff = sem("top_diff")
        top_part = sem("top_part")
        top_f = sem("top_f")
        top_c = sem("top_c")
        down_diff = sem("down_diff")
        down_t = sem("down_t")
        down_h = sem("down_h")
        down0_t = sem("down0_t")
        down0_h = sem("down0_h")
        sq_done = sem("sq_done")
        hsq_done = sem("hsq_done")
        rh_done = sem("rh_done")
        rh_hi_done = sem("rh_hi_done")
        rh_lo0_done = sem("rh_lo0_done")
        rh_lo_done = sem("rh_lo_done")
        hsq_mm = sem("hsq_mm")
        m_ve_done = sem("m_ve_done")
        m_rstd_done = sem("m_rstd_done")
        wo_mm = sem("wo_mm")
        x1_done = sem("x1_done")
        b_mean_done = sem("b_mean_done")
        b_sq_done = sem("b_sq_done")
        b_ve_done = sem("b_ve_done")
        b_rstd_done = sem("b_rstd_done")
        b_nb_done = sem("b_nb_done")
        fn_done = sem("fn_done")
        fx_hi_done = sem("fx_hi_done")
        fx_lo_done = sem("fx_lo_done")
        ctx_hi_done = sem("ctx_hi_done")
        ctx_lo_done = sem("ctx_lo_done")
        cx_done = sem("cx_done")
        g_mm = sem("g_mm")
        ph_mm = sem("ph_mm")
        th_mm = sem("th_mm")
        gt_done = sem("gt_done")
        ph_hi_done = sem("ph_hi_done")
        ph_lo_done = sem("ph_lo_done")
        th_hi_done = sem("th_hi_done")
        th_lo_done = sem("th_lo_done")
        g_t = sem("g_t")
        g_hi_done = sem("g_hi_done")
        g_lo_done = sem("g_lo_done")
        score_mm = sem("score_mm")
        nmax_done = sem("nmax_done")
        exp_done = sem("exp_done")
        rinv_done = sem("rinv_done")
        prob_done = sem("prob_done")
        prob_t = sem("prob_t")
        pt_hi_done = sem("pt_hi_done")
        pt_lo_done = sem("pt_lo_done")
        av_mm = sem("av_mm")
        t_raw_done = sem("t_raw_done")
        t_mv_done = sem("t_mv_done")
        t_mean_done = sem("t_mean_done")
        mean_mm = sem("mean_mm")
        t_dist_done = sem("t_dist_done")
        t_sec_done = sem("t_sec_done")
        sec_mm = sem("sec_mm")
        t_ve_done = sem("t_ve_done")
        t_rstd_done = sem("t_rstd_done")
        t_gam_done = sem("t_gam_done")
        t_bet_done = sem("t_bet_done")
        relu_hi_done = sem("relu_hi_done")
        relu_lo_done = sem("relu_lo_done")
        out_mm = sem("out_mm")
        x2_done = sem("x2_done")
        c_mean_done = sem("c_mean_done")
        c_sq_done = sem("c_sq_done")
        c_ve_done = sem("c_ve_done")
        c_rstd_done = sem("c_rstd_done")
        zg_done = sem("zg_done")
        fin_done = sem("fin_done")
        zg_t = sem("zg_t")
        z_hi_done = sem("z_hi_done")
        z_lo_done = sem("z_lo_done")
        ffn_mm = sem("ffn_mm")
        x3_done = sem("x3_done")

        def level(tile, start, step, less=0):
            count = (S - start + step - 1) // step - less
            return tile[:, :, :].rearrange("p e (s n) -> p (e s) n", n=S)[:, :, start:start + (count - 1) * step + 1:step]

        def products(count):
            return tt[:, :, :].rearrange("p a d -> p (a d)")[:, 0:2 * KT * count]\
                .rearrange("p (q n) -> p q n", n=count)

        def ctx_lower(eng, s):
            cut = slice(s * D, (s + 1) * D)
            eng.tensor_tensor(cz_lo[:, cut], cx[:, s, :], f32(cz_hi[:, cut]), ALU.subtract).then_inc(ctx_lo_done, 1)

        def up_nodes(l):
            step = 2 << l
            return (level(fs, step // 2 - 1, step), level(cs, step // 2 - 1, step),
                    level(fs, step - 1, step), level(cs, step - 1, step), products(S // step))

        def of_tile(nodes, e):
            return [rows[:, 2 * e:2 * e + 2, :] for rows in nodes]

        def up_ready(eng, t, l):
            if l == 1:
                eng.wait_ge(up0_f, t * KT + KT)
                eng.wait_ge(up0_c, t * KT + KT)
            else:
                eng.wait_ge(up_f, t * (TOP - 1) + (l - 1))
                eng.wait_ge(up_c, t * (TOP - 1) + (l - 1))

        def up_product_c(eng, t, l):
            fa, ca, fb, cb, product = up_nodes(l)
            up_ready(eng, t, l)
            eng.tensor_tensor(product, fb, ca, ALU.mult).then_inc(up_t, 1)

        def up_product_f(eng, t, l):
            fa, ca, fb, cb, product = up_nodes(l)
            eng.wait_ge(up_t, t * (TOP - 1) + l)
            eng.wait_ge(up_g, t * (TOP - 1) + l)
            eng.tensor_tensor(fb, fa, fb, ALU.mult).then_inc(up_f, 1)

        def up_join(eng, t, l):
            fa, ca, fb, cb, product = up_nodes(l)
            eng.wait_ge(up_t, t * (TOP - 1) + l)
            eng.wait_ge(up_g, t * (TOP - 1) + l)
            eng.tensor_tensor(cb, product, cb, ALU.subtract).then_inc(up_c, 1)

        def down_nodes(l):
            step = 2 << l
            start = step + step // 2 - 1
            return (level(fs, start, step), level(cs, start, step), level(cs, step - 1, step, less=1),
                    products(S // step - 1))

        def down_ready(eng, t, l):
            turn = LEVELS - 2 - l
            if turn == 0:
                eng.wait_ge(top_c, t * (LEVELS - TOP) + (LEVELS - TOP))
            else:
                eng.wait_ge(down_h, t * (LEVELS - 2) + turn)

        def down(eng, t, l):
            f, c, before, product = down_nodes(l)
            turn = LEVELS - 2 - l
            down_ready(eng, t, l)
            eng.tensor_tensor(product, f, before, ALU.mult).then_inc(down_t, 1)
            eng.wait_ge(down_t, t * (LEVELS - 2) + (turn + 1))
            eng.tensor_tensor(c, product, c, ALU.subtract).then_inc(down_h, 1)

        block = stack.enter_context(nc.Block())

        def store(eng, n):
            need(eng, x3_done, n * ST + ST)
            eng.dma_start(out_rows[:, bass.ds(n * ST, ST), :], fin[:, :, :]).then_inc(stored, 16)

        @block.sync
        def _(sp):
            def load_x(t):
                need(sp, xt_mm, t * KT)
                sp.dma_start(x_in[:, :, :], x_rows[:, bass.ds(t * QT, QT), :]).then_inc(x_here, 16)

            def load_res(t, b):
                n = t * 2 + (b - 2)
                if not isinstance(t, int) or t > 0:
                    need(sp, fin_done, n * ST + ST)
                    need(sp, zg_done, n * ST + ST)
                sp.dma_start(res[:, b * ST:(b + 1) * ST, :],
                             x_rows[:, bass.ds(t * QT + b * ST, ST), :]).then_inc(res_here[b], 16)

            def load_ctx(n):
                need(sp, x2_done, n * ST)
                sp.dma_start(cx[:, :, :], ctx_rows[:, bass.ds(n * ST, ST), :]).then_inc(ctx_here, 16)

            load_x(0)
            rows = lambda w: w.rearrange("(k p) n -> p k n", p=P)
            sp.dma_start(prob[:, :, :], rows(wf)).then_inc(w_here[F], 16)
            sp.dma_start(cx[:, :, :], rows(wc)[:, 0:2, :]).then_inc(w_here[C], 16)
            sp.dma_start(fin[:, :, :], rows(wc)[:, 2:4, :]).then_inc(w_here[C], 16)
            sp.dma_start(res[:, :, :], rows(wr)).then_inc(w_here[R], 16)
            sp.wait_ge(w_lo_done, KT)
            sp.dma_start(prob[:, :, :], rows(ffn_w)).then_inc(q_here, 16)
            load_x(1)
            sp.wait_ge(w_lo_done, 2 * KT)
            for n, w in enumerate((theta_w, phi_w, g_w)):
                sp.dma_start(cx[:, 0, 0:256] if n == 0 else cx[:, n // 2, (n % 2) * 256:(n % 2) * 256 + 256],
                             w).then_inc(pj_here, 16)
            sp.dma_start(fin[:, 0, 0:256].rearrange("p (o l) -> p o l", o=2), rows(out_w)).then_inc(pj_here, 16)
            sp.wait_ge(w_lo_done, 3 * KT)
            sp.dma_start(res[:, :, :], rows(wo)).then_inc(w_here[3], 16)
            for dst, src in ((gamma_bc, ffn_gamma), (bias_bc, ffn_bias)):
                sp.dma_start(dst[:, :], src.rearrange("(a d) -> a d", a=1).to_broadcast([P, D])).then_inc(wide_here, 16)
            for dst, src in ((gamma_lt, ln_gamma), (beta_lt, ln_beta)):
                sp.dma_start(dst[:, :], src).then_inc(wide_here, 16)
            sp.wait_ge(w_lo_done, 4 * KT)
            load_res(0, 0)
            load_res(0, 1)
            sp.wait_ge(pj_lo_done, 2)
            load_ctx(0)

            def step(i, load_next):
                if load_next:
                    load_x(i + 1)
                load_ctx(i * 2 - 1)
                load_res(i, 0)
                store(sp, i * 2 - 2)
                load_ctx(i * 2)
                load_res(i, 1)
                store(sp, i * 2 - 1)

            with sp.Fori(1, PAIRS - 1) as i:
                step(i, True)
            step(PAIRS - 1, False)
            load_ctx(2 * PAIRS - 1)
            store(sp, 2 * PAIRS - 2)
            store(sp, 2 * PAIRS - 1)
            sp.wait_ge(stored, 16 * B)

        @block.gpsimd
        def _(pool):
            pool.memset(ident[:, :], 0.0).then_inc(ident_zero, 1)
            pool.memset(avg[:, :], 1.0 / P).then_inc(const_done, 1)
            pool.memset(minus_half[:, :], -0.5).then_inc(const_done, 1)
            pool.wait_ge(ident_zero, 1)
            pool.affine_select(out=ident[:, :], in_=ident[:, :], compare_op=ALU.not_equal, fill=1.0,
                               base=0, pattern=[[-1, P]], channel_multiplier=1).then_inc(const_done, 1)
            pool.wait_ge(const_done, 3)

            def rsqrt(out_ap, in_ap, width, done):
                pool.tensor_tensor(out_ap, in_ap, minus_half[:, 0:width], ALU.pow).then_inc(done, 1)

            def norm_x(t):
                pool.wait_ge(a_ve_done, t + 1)
                need(pool, xn_done, t * QT)
                rsqrt(a_rstd[:, :], a_ve[:, :], QT, a_rstd_done)

            def even_g(t, e):
                pool.wait_ge(f_less_done, t * KT + (e + 1))
                pool.wait_ge(c_done, t * KT + (e + 1))
                pool.tensor_tensor(gs[:, e, :], gs[:, e, :], cs[:, e, 0:D:2], ALU.mult).then_inc(g0_done, 1)

            def up0_product_c(t, e):
                fa, ca, fb, cb, product = of_tile(up_nodes(0), e)
                pool.wait_ge(f_done, t * KT + (e + 1))
                pool.wait_ge(c_done, t * KT + (e + 1))
                need(pool, fx_lo_done, t * QT)
                pool.tensor_tensor(product, fb, ca, ALU.mult).then_inc(up0_t, 1)

            def up0_product_f(t, e):
                fa, ca, fb, cb, product = of_tile(up_nodes(0), e)
                pool.wait_ge(up0_t, t * KT + (e + 1))
                pool.wait_ge(up0_g, t * KT + (e + 1))
                pool.tensor_tensor(fb, fa, fb, ALU.mult).then_inc(up0_f, 1)

            def top_up(t, l):
                fa, ca, fb, cb, product = up_nodes(l)
                before, n = t * (LEVELS - TOP), l - TOP
                if n == 0:
                    up_ready(pool, t, TOP)
                else:
                    pool.wait_ge(top_c, before + n)
                pool.tensor_tensor(product, ca, cb, ALU.subtract).then_inc(top_diff, 1)
                if n:
                    pool.wait_ge(top_f, t * (LEVELS - TOP - 1) + n)
                pool.wait_ge(top_diff, before + (n + 1))
                pool.tensor_tensor(product, product, fb, ALU.mult).then_inc(top_part, 1)
                pool.wait_ge(top_part, before + (n + 1))
                pool.tensor_tensor(cb, cb, product, ALU.add).then_inc(top_c, 1)
                if l < LEVELS - 1:
                    pool.tensor_tensor(fb, fa, fb, ALU.mult).then_inc(top_f, 1)

            def top_down(t, l):
                f, c, before, product = down_nodes(l)
                turn = LEVELS - 2 - l
                down_ready(pool, t, l)
                pool.tensor_tensor(product, before, c, ALU.subtract).then_inc(down_diff, 1)
                pool.wait_ge(down_diff, t * (LEVELS - 1 - TOP) + (turn + 1))
                pool.tensor_tensor(product, product, f, ALU.mult).then_inc(down_t, 1)
                pool.wait_ge(down_t, t * (LEVELS - 2) + (turn + 1))
                pool.tensor_tensor(c, c, product, ALU.add).then_inc(down_h, 1)

            def top(t, first, last):
                for l in range(first, last):
                    top_up(t, l)

            def top_back(t):
                for l in range(LEVELS - 2, TOP - 1, -1):
                    top_down(t, l)
                down(pool, t, TOP - 1)

            def sum_sq(t):
                for e in range(1, KT):
                    pool.wait_ge(sq_done, t * KT + (e + 1))
                    need(pool, hsq_done, t * (KT - 1) + (e - 1))
                    pool.tensor_tensor(fs[:, 0, :], fs[:, 0, :], fs[:, e, :], ALU.add).then_inc(hsq_done, 1)

            def norm_m(t):
                pool.wait_ge(m_ve_done, t + 1)
                need(pool, x1_done, t * QT)
                rsqrt(m_rstd[:, :], m_ve[:, :], QT, m_rstd_done)

            def norm_b(n, b):
                pool.wait_ge(b_ve_done, n + 1)
                need(pool, fn_done, n * ST - ST)
                rsqrt(b_rstd[:, b * ST:(b + 1) * ST], b_ve[:, b * ST:(b + 1) * ST], ST, b_rstd_done)

            def ctx_low(n, s):
                pool.wait_ge(ctx_hi_done, n * ST + (s + 1))
                ctx_lower(pool, s)

            def ctx_plus(n, b):
                pool.wait_ge(ctx_lo_done, n * ST + ST)
                pool.wait_ge(x1_done, n * ST + ST)
                pool.tensor_tensor(cx[:, :, :], cx[:, :, :], res[:, b * ST:(b + 1) * ST, :], ALU.add)\
                    .then_inc(cx_done, 1)

            def norm_t(n):
                pool.wait_ge(t_ve_done, n + 1)
                rsqrt(t_s[:, 5:6], t_s[:, 4:5], 1, t_rstd_done)

            def norm_c(n):
                pool.wait_ge(c_ve_done, n + 1)
                need(pool, x3_done, n * ST)
                rsqrt(c_rstd, c_ve, ST, c_rstd_done)

            def fin_sum(n, b):
                pool.wait_ge(x2_done, n * ST + ST)
                need(pool, stored, n * 16)
                for s in range(ST):
                    pool.tensor_tensor(fin[:, s, :], res[:, b * ST + s, :], bias_bc[:, :], ALU.add)\
                        .then_inc(fin_done, 1)

            def back(i, b, gates, load_next):
                n = i * 2 + (b - 2)
                if b == 1:
                    ctx_low(n, 0)
                if gates and b == 1:
                    up_product_f(pool, i, 1)
                    up_join(pool, i, 1)
                if b == 0 and load_next:
                    norm_x(i + 1)
                ctx_plus(n, b)
                if gates and b == 0:
                    even_g(i, 0)
                    even_g(i, 1)
                if gates and b == 1:
                    top(i, TOP, TOP + 2)
                norm_t(n)
                if gates and b == 1:
                    top(i, TOP + 2, LEVELS)
                    top_back(i)
                if gates and b == 0:
                    for e in range(2):
                        up0_product_c(i, e)
                        up0_product_f(i, e)
                    up0_product_c(i, 2)
                    up0_product_f(i, 2)
                norm_c(n)
                if gates and b == 0:
                    even_g(i, 2)
                fin_sum(n, b)
                if gates and b == 0:
                    up0_product_c(i, 3)
                    up0_product_f(i, 3)
                    even_g(i, 3)

            def finish(t):
                pool.wait_ge(rh_hi_done, t * KT + 1)
                pool.tensor_tensor(rh_lo[:, 0, :], r2[:, 0, :], f32(rh_hi[:, 0, :]), ALU.subtract)\
                    .then_inc(rh_lo0_done, 1)
                sum_sq(t)
                norm_m(t)
                for s in range(ST):
                    ctx_low(t * 2, s)
                norm_b(t * 2, 0)
                norm_b(t * 2 + 1, 1)

            norm_x(0)
            for e in range(KT):
                if e == 2:
                    norm_x(1)
                up0_product_c(0, e)
                up0_product_f(0, e)
            for e in range(KT):
                even_g(0, e)
            top(0, TOP, LEVELS)
            top_back(0)
            finish(0)
            pool.wait_ge(bias_done, 1)

            def step(i, load_next):
                back(i, 0, True, load_next)
                back(i, 1, True, load_next)
                finish(i)

            with pool.Fori(1, PAIRS - 1) as i:
                step(i, True)
            step(PAIRS - 1, False)
            back(PAIRS, 0, False, False)
            back(PAIRS, 1, False, False)

        @block.scalar
        def _(act):
            col = lambda v: v.rearrange("(k p) -> p k", p=P)
            with nc.allow_non_contiguous_dma(reason="vectors of a few hundred elements, once"):
                for dst, src in ((theta_bc, theta_b), (phi_bc, phi_b), (g_bc, g_b), (out_bc, out_b),
                                 (scale_bc, ln_scale), (beta_c, ffn_beta)):
                    act.dma_start(dst, col(src)).then_inc(small_here, 16)

            def norm_x(t, tiles=range(QT)):
                act.wait_ge(a_nb_done, t + 1)
                for q in tiles:
                    act.activation(x_in[:, q, :], x_in[:, q, :], ACT.Identity, bias=a_nb[:, q:q + 1],
                                   scale=a_rstd[:, q:q + 1]).then_inc(xn_done, 1)

            def xt_high(t, tiles):
                need(act, z_mm, t * 3 * KT)
                for k in tiles:
                    act.wait_ge(xt_mm, t * KT + (k + 1))
                    act.activation(xt_hi[:, k, :], XT[k][:, :], ACT.Copy).then_inc(xt_hi_done, 1)

            def gate(t, m, e, tile, done):
                turn = TURN[m, e]
                act.wait_ge(z_mm, t * len(GROUPS) + (turn + 1))
                act.activation(tile[:, e, :], Z[turn % 3][:, :], ACT.Tanh, scale=0.5).then_inc(done, 1)

            def gate_r(t, e):
                need(act, rh_lo_done, t * (KT - 1))
                need(act, rh_lo0_done, t)
                gate(t, R, e, r2, tr_done)

            def gate_f(t, e):
                need(act, hsq_mm, t)
                need(act, down0_h, t * KT)
                gate(t, F, e, fs, tf_done)
                act.wait_ge(tf_done, t * KT + (e + 1))
                act.activation(gs[:, e, :], fs[:, e, 0:D:2], ACT.Copy, bias=-0.5, scale=0.5).then_inc(f_less_done, 1)
                act.wait_ge(f_less_done, t * KT + (e + 1))
                act.activation(fs[:, e, :], fs[:, e, :], ACT.Copy, bias=0.5, scale=0.5).then_inc(f_done, 1)

            def gate_c(t, e):
                need(act, rh_done, t * KT)
                need(act, sq_done, t * KT)
                gate(t, C, e, cs, tc_done)

            def rh_high(t):
                for e in range(KT):
                    act.wait_ge(down0_h, t * KT + (e + 1))
                    if e == 2 and not (isinstance(t, int) and t == 0):
                        gate_r(t, KT - 1)
                    act.activation(fs[:, e, :], cs[:, e, :], ACT.Square).then_inc(sq_done, 1)
                    act.wait_ge(rh_done, t * KT + (e + 1))
                    need(act, av_mm, t * 2)
                    act.activation(rh_hi[:, e, :], r2[:, e, :], ACT.Copy).then_inc(rh_hi_done, 1)

            def square_b(n, b):
                act.wait_ge(b_mean_done, n + 1)
                if b == 0:
                    need(act, relu_lo_done, n)
                    need(act, c_sq_done, n * ST)
                for q in range(b * ST, (b + 1) * ST):
                    need(act, b_sq_done, n * ST + q % ST)
                    act.activation(gt[:, :], res[:, q, :], ACT.Square, bias=b_mean[:, q:q + 1], scale=-1.0,
                                   accum_out=b_ve[:, q:q + 1]).then_inc(b_sq_done, 1)

            def norm_f(n, b):
                act.wait_ge(b_nb_done, n + 1)
                need(act, fx_lo_done, n * ST)
                for s in range(ST):
                    act.activation(tt[:, s, :], res[:, b * ST + s, :], ACT.Identity,
                                   bias=b_nb[:, b * ST + s:b * ST + s + 1],
                                   scale=b_rstd[:, b * ST + s:b * ST + s + 1]).then_inc(fn_done, 1)

            def fx_high(n, b):
                if b == 0:
                    act.wait_ge(wo_mm, n * (QT // 2) + QT)
                else:
                    act.wait_ge(av_mm, n)
                for s in range(ST):
                    act.wait_ge(fn_done, n * ST + (s + 1))
                    act.activation(fx_hi[:, s, :], tt[:, s, :], ACT.Copy).then_inc(fx_hi_done, 1)

            def ctx_high(n):
                act.wait_ge(ctx_here, n * 16 + 16)
                need(act, ffn_mm, n * ST)
                for s in range(ST):
                    act.activation(cz_hi[:, s * D:(s + 1) * D], cx[:, s, :], ACT.Copy).then_inc(ctx_hi_done, 1)

            def proj_high(n, b):
                act.wait_ge(g_mm, n + 1)
                need(act, relu_lo_done, n)
                need(act, c_sq_done, n * ST)
                if b == 0:
                    act.wait_ge(b_sq_done, n * ST + QT)
                act.activation(gt[:, :], W[4][:, :], ACT.Copy).then_inc(gt_done, 1)
                act.wait_ge(ph_mm, n + 1)
                act.activation(ph_hi[:, :], W[3][:, :], ACT.Identity, bias=phi_bc).then_inc(ph_hi_done, 1)
                act.wait_ge(th_mm, n + 1)
                need(act, out_mm, n * ST)
                act.activation(th_hi[:, :], W[0][:, :], ACT.Identity, bias=theta_bc).then_inc(th_hi_done, 1)

            def g_high(n):
                act.wait_ge(g_t, n + 1)
                act.activation(g_hi[:, :, :].rearrange("p j l -> p (j l)"), W[2][:, :], ACT.Copy)\
                   .then_inc(g_hi_done, 1)

            def softmax(n):
                need(act, zg_t, n * 2)
                for k in range(KT):
                    act.wait_ge(nmax_done, n * KT + (k + 1))
                    act.activation(prob[:, k, :], SC[k][:, :], ACT.Exp, bias=nmax[:, k:k + 1],
                                   accum_out=rsum[:, k:k + 1]).then_inc(exp_done, 1)

            def pt_high(n):
                for k in range(KT):
                    act.wait_ge(prob_t, n * KT + (k + 1))
                    act.activation(pt_hi[:, k, :], W[k][:, :], ACT.Copy).then_inc(pt_hi_done, 1)

            def relu_high(n):
                act.wait_ge(t_bet_done, n + 1)
                act.activation(th_hi[:, :], gt[:, :], ACT.Relu).then_inc(relu_hi_done, 1)

            def square_c(n, b):
                act.wait_ge(relu_lo_done, n + 1)
                for s in range(ST):
                    act.wait_ge(c_mean_done, n * ST + (s + 1))
                    need(act, c_sq_done, n * ST + s)
                    act.activation(gt[:, :], res[:, b * ST + s, :], ACT.Square, bias=c_mean[:, s:s + 1], scale=-1.0,
                                   accum_out=c_ve[:, s:s + 1]).then_inc(c_sq_done, 1)

            def z_high(n):
                for c, w in enumerate((W[3], W[0])):
                    act.wait_ge(zg_t, n * 2 + (c + 1))
                    act.activation(cz_hi[:, c * D:(c + 1) * D], w[:, :], ACT.Copy).then_inc(z_hi_done, 1)

            norm_x(0, range(ST))
            act.wait_ge(w_here[F], 16)
            for k in range(KT):
                act.activation(w_hi[F][:, k, :], prob[:, k, :], ACT.Copy).then_inc(w_hi_done, 1)
            xt_high(0, range(KT))
            act.wait_ge(w_here[C], 32)
            for k in range(KT):
                act.activation(w_hi[C][:, k, :], (cx if k < 2 else fin)[:, k % 2, :], ACT.Copy)\
                   .then_inc(w_hi_done, 1)
            gate_f(0, 0)
            act.wait_ge(w_here[R], 16)
            for k in range(KT):
                act.activation(w_hi[R][:, k, :], res[:, k, :], ACT.Copy).then_inc(w_hi_done, 1)
            gate_c(0, 0)
            for e in range(1, KT):
                gate_f(0, e)
                gate_c(0, e)
            gate_r(0, 0)
            for c in range(2):
                act.wait_ge(pj_t, c + 1)
                act.activation(pj_hi[:, 2 * c:2 * c + 2, :].rearrange("p m n -> p (m n)"), W[c][:, :],
                                           ACT.Copy).then_inc(pj_hi_done, 1)
            norm_x(1)
            gate_r(0, 1)
            act.wait_ge(col_done, 1)
            act.wait_ge(w_here[3], 16)
            for k in range(KT):
                act.activation(wo_hi[:, k, :], res[:, k, :], ACT.Copy, scale=scale_bc[:, k:k + 1])\
                   .then_inc(w_hi_done, 1)
            gate_r(0, 2)
            gate_r(0, 3)
            for k in range(KT):
                act.wait_ge(q_t, k + 1)
                act.activation(wq[:, k, :], W[k][:, :], ACT.Copy).then_inc(wq_done, 1)

            def finish(t, load_next):
                rh_high(t)
                ctx_high(t * 2)
                if load_next:
                    xt_high(t + 1, range(0, 2))
                square_b(t * 2, 0)
                if load_next:
                    xt_high(t + 1, range(2, KT))
                norm_f(t * 2, 0)
                fx_high(t * 2, 0)
                square_b(t * 2 + 1, 1)

            finish(0, True)

            def back(i, b, gates, load_next):
                n = i * 2 + (b - 2)
                first, second = gates and b == 0, gates and b == 1
                if first:
                    gate_f(i, 0)
                    gate_c(i, 0)
                if second and load_next:
                    norm_x(i + 1)
                if b:
                    ctx_high(n)
                proj_high(n, b)
                if b == 0:
                    norm_f(n + 1, 1)
                g_high(n)
                softmax(n)
                if first:
                    gate_f(i, 1)
                if second:
                    gate_r(i, 0)
                pt_high(n)
                if first:
                    gate_c(i, 1)
                if b == 0:
                    fx_high(n + 1, 1)
                if first:
                    gate_f(i, 2)
                if second:
                    gate_r(i, 1)
                relu_high(n)
                if first:
                    gate_c(i, 2)
                    gate_f(i, 3)
                if second:
                    gate_r(i, 2)
                square_c(n, b)
                z_high(n)
                if first:
                    gate_c(i, 3)

            def step(i, load_next):
                back(i, 0, True, load_next)
                back(i, 1, True, load_next)
                finish(i, load_next)

            with act.Fori(1, PAIRS - 1) as i:
                step(i, True)
            step(PAIRS - 1, False)
            back(PAIRS, 0, False, False)
            back(PAIRS, 1, False, False)

        @block.tensor
        def _(pe):
            pe.wait_ge(const_done, 3)

            def transpose_x(t):
                pe.wait_ge(xn_done, t * QT + QT)
                need(pe, r_done, t * KT)
                for k in range(KT):
                    if k == KT - 1:
                        need(pe, m_ve_done, t)
                    for q in range(QT):
                        mm = pe.transpose(XT[k][:, q * P:(q + 1) * P], x_in[:, q, k * P:(k + 1) * P], ident[:, :])
                    mm.then_inc(xt_mm, 1)

            free = (r_done, tf_done, c_done)

            def gates(t, first, count):
                for chunk in range(first, first + count):
                    turn, k = divmod(chunk, KT)
                    m, e = GROUPS[turn]
                    bank = Z[turn % 3]
                    if chunk == 0:
                        pe.wait_ge(xt_lo_done, t * KT + 1)
                    if k == 0 and turn >= 3:
                        m_last, e_last = GROUPS[turn - 3]
                        pe.wait_ge(free[m_last], t * KT + (e_last + 1))
                    if turn == 0:
                        pe.wait_ge(xt_hi_done, t * KT + (k + 1))
                    if e == 0 and isinstance(t, int) and t == 0:
                        pe.wait_ge(w_lo_done, (F, C, R).index(m) * KT + k + 1)
                    cut = slice(e * P, (e + 1) * P)
                    pe.matmul(bank[:, :], w_hi[m][:, k, cut], xt_hi[:, k, :], start=(k == 0), stop=False)
                    pe.matmul(bank[:, :], w_lo[m][:, k, cut], xt_hi[:, k, :], start=False, stop=False)
                    if turn == 0:
                        pe.wait_ge(xt_lo_done, t * KT + (k + 1))
                    mm = pe.matmul(bank[:, :], w_hi[m][:, k, cut], xt_lo[:, k, :], start=False,
                                   stop=(k == KT - 1))
                    if k == KT - 1:
                        mm.then_inc(z_mm, 1)

            def mix_part(t, tiles):
                for k in range(KT + 1):
                    if k < KT:
                        pe.wait_ge(rh_hi_done, t * KT + (k + 1))
                        for q in tiles:
                            cut = slice(q * P, (q + 1) * P)
                            pe.matmul(Y[q][:, :], rh_hi[:, k, cut], wo_hi[:, k, :], start=(k == 0), stop=False)
                            pe.matmul(Y[q][:, :], rh_hi[:, k, cut], wo_lo[:, k, :], start=False, stop=False)
                    if k == 1:
                        pe.wait_ge(rh_lo0_done, t + 1)
                    elif k:
                        pe.wait_ge(rh_lo_done, t * (KT - 1) + (k - 1))
                    for q in tiles if k else ():
                        mm = pe.matmul(Y[q][:, :], rh_lo[:, k - 1, q * P:(q + 1) * P], wo_hi[:, k - 1, :],
                                       start=False, stop=(k == KT))
                        if k == KT:
                            mm.then_inc(wo_mm, 1)

            def mix_out(t, next_x):
                if isinstance(t, int) and t == 0:
                    pe.wait_ge(w_lo_done, 4 * KT)
                mix_part(t, range(ST))
                if isinstance(t, int) and t == 0:
                    pe.wait_ge(bias_done, 1)
                pe.wait_ge(hsq_done, t * (KT - 1) + (KT - 1))
                for q in range(QT):
                    mm = pe.matmul(W[4][:, q:q + 1], fs[:, 0, q * P:(q + 1) * P], avg[:, 0:1], start=True, stop=True)
                mm.then_inc(hsq_mm, 1)
                if not isinstance(t, int) or t > 0:
                    need(pe, x3_done, t * QT)
                mix_part(t, range(ST, QT - 1))
                if next_x:
                    transpose_x(t + 1)
                mix_part(t, range(QT - 1, QT))

            def project_high(bank, m, hi):
                for s in range(ST):
                    pe.matmul(W[bank][:, :], pj_hi[:, m, s * P:(s + 1) * P], hi[s], start=(s == 0), stop=False)
                    pe.matmul(W[bank][:, :], pj_lo[:, m, s * P:(s + 1) * P], hi[s], start=False, stop=False)

            def project_low(bank, m, lo, done):
                for s in range(ST):
                    mm = pe.matmul(W[bank][:, :], pj_hi[:, m, s * P:(s + 1) * P], lo[s], start=False,
                                   stop=(s == ST - 1))
                mm.then_inc(done, 1)

            fh, fl = [[f[:, s, :] for s in range(ST)] for f in (fx_hi, fx_lo)]
            ch, cl = [[c[:, s * D:(s + 1) * D] for s in range(ST)] for c in (cz_hi, cz_lo)]

            def projections(n, b, fill, between):
                pe.wait_ge(fx_hi_done, n * ST + ST)
                if b == 0:
                    need(pe, x1_done, n * ST + 2 * ST)
                    project_high(4, 2, fh)
                project_high(3, 1, fh)
                pe.wait_ge(fx_lo_done, n * ST + ST)
                if b == 0:
                    project_low(4, 2, fl, g_mm)
                project_low(3, 1, fl, ph_mm)
                fill(between)
                pe.wait_ge(ctx_hi_done, n * ST + ST)
                project_high(0, 0, ch)
                pe.wait_ge(ctx_lo_done, n * ST + ST)
                project_low(0, 0, cl, th_mm)

            def turn_g(n, b):
                pe.wait_ge(gt_done, n + 1)
                if b:
                    need(pe, x3_done, n * ST)
                for j in range(KT):
                    mm = pe.transpose(W[2][:, j * P:(j + 1) * P], gt[:, j * P:(j + 1) * P], ident[:, :])
                mm.then_inc(g_t, 1)

            def scores(n):
                def high(k):
                    cut = slice(k * P, (k + 1) * P)
                    pe.matmul(SC[k][:, :], th_hi[:, cut], ph_hi[:, :], start=True, stop=False)
                    pe.matmul(SC[k][:, :], th_hi[:, cut], ph_lo[:, :], start=False, stop=False)

                def low(k):
                    pe.matmul(SC[k][:, :], th_lo[:, k * P:(k + 1) * P], ph_hi[:, :], start=False, stop=True)\
                      .then_inc(score_mm, 1)

                pe.wait_ge(th_hi_done, n + 1)
                pe.wait_ge(ph_lo_done, n + 1)
                high(0)
                high(1)
                pe.wait_ge(th_lo_done, n + 1)
                low(0)
                low(1)
                high(2)
                low(2)
                pe.wait_ge(g_lo_done, n + 1)
                high(3)
                low(3)

            def turn_prob(n):
                pe.wait_ge(prob_done, n * KT + KT)
                for j in range(KT):
                    for k in range(KT):
                        mm = pe.transpose(W[j][:, k * P:(k + 1) * P], prob[:, k, j * P:(j + 1) * P], ident[:, :])
                    mm.then_inc(prob_t, 1)

            def attend(n):
                for j in range(KT + 1):
                    if j < KT:
                        pe.wait_ge(pt_hi_done, n * KT + (j + 1))
                        pe.matmul(W[4][:, :], g_hi[:, j, :], pt_hi[:, j, :], start=(j == 0), stop=False)
                        pe.matmul(W[4][:, :], g_lo[:, j, :], pt_hi[:, j, :], start=False, stop=False)
                    if j:
                        pe.wait_ge(pt_lo_done, n * KT + j)
                        mm = pe.matmul(W[4][:, :], g_hi[:, j - 1, :], pt_lo[:, j - 1, :], start=False,
                                       stop=(j == KT))
                mm.then_inc(av_mm, 1)

            def mean_over(n):
                pe.wait_ge(t_mean_done, n + 1)
                pe.matmul(W[0][:, 0:1], avg[:, :], t_s[:, 0:1], start=True, stop=True).then_inc(mean_mm, 1)

            def second_over(n):
                pe.wait_ge(t_sec_done, n + 1)
                pe.matmul(W[3][:, 0:1], avg[:, :], t_s[:, 2:3], start=True, stop=True).then_inc(sec_mm, 1)

            def attn_out(n):
                cuts = [slice(o * P, (o + 1) * P) for o in range(ST)]
                pe.wait_ge(relu_hi_done, n + 1)
                for o, cut in enumerate(cuts):
                    pe.matmul(W[1 + o][:, :], pj_hi[:, 3, cut], th_hi[:, :], start=True, stop=False)
                    pe.matmul(W[1 + o][:, :], pj_lo[:, 3, cut], th_hi[:, :], start=False, stop=False)
                pe.wait_ge(relu_lo_done, n + 1)
                for o, cut in enumerate(cuts):
                    pe.matmul(W[1 + o][:, :], pj_hi[:, 3, cut], th_lo[:, :], start=False, stop=True)\
                      .then_inc(out_mm, 1)

            def turn_z(n):
                for s in range(ST):
                    pe.wait_ge(zg_done, n * ST + (s + 1))
                    for c, w in enumerate((W[3], W[0])):
                        for k in range(2):
                            at = (k * ST + s) * P
                            mm = pe.transpose(w[:, at:at + P], fz[:, s, (2 * c + k) * P:(2 * c + k + 1) * P],
                                              ident[:, :])
                        if s == ST - 1:
                            mm.then_inc(zg_t, 1)

            def feed(n):
                for c in range(2):
                    pe.wait_ge(z_hi_done, n * 2 + (c + 1))
                    for k in range(2 * c, 2 * c + 2):
                        for s in range(ST):
                            at = (k * ST + s) * P
                            pe.matmul(W[1 + s][:, :], cz_hi[:, at:at + P], wq[:, k, :], start=(k == 0), stop=False)
                pe.wait_ge(z_lo_done, n * 2 + 2)
                for s in range(ST):
                    for k in range(KT):
                        at = (k * ST + s) * P
                        mm = pe.matmul(W[1 + s][:, :], cz_lo[:, at:at + P], wq[:, k, :], start=False,
                                       stop=(k == KT - 1))
                    mm.then_inc(ffn_mm, 1)

            def keep_warm(count):
                for _ in range(count):
                    pe.matmul(Z[0][:, :], w_hi[R][:, 0, 0:P], xt_hi[:, 0, :], start=True, stop=True)

            transpose_x(0)
            gates(0, 0, 24)
            pe.wait_ge(abs_done, 1)
            pe.matmul(W[0][:, 0:1], avg[:, :], abs_sum, start=True, stop=True).then_inc(abs_mean, 1)
            gates(0, 24, 12)
            pe.wait_ge(thr_done, 2)
            pe.wait_ge(pj_here, 64)
            src = [cx[:, 0, 0:256], cx[:, 0, 256:512], cx[:, 1, 0:256], fin[:, 0, 0:256]]
            for m in range(4):
                for h in range(2):
                    at = ((m % 2) * 2 + h) * P
                    mm = pe.transpose(W[m // 2][:, at:at + P], src[m][:, h * P:(h + 1) * P], ident[:, :])
                if m % 2:
                    mm.then_inc(pj_t, 1)
            gates(0, 36, 12)
            pe.wait_ge(pj_lo_done, 2)
            pe.wait_ge(q_done, KT)
            for k in range(KT):
                for o in range(KT):
                    mm = pe.transpose(W[k][:, o * P:(o + 1) * P], prob[:, o, k * P:(k + 1) * P], ident[:, :])
                mm.then_inc(q_t, 1)
            pe.wait_ge(beta_done, KT)
            pe.wait_ge(wq_done, KT)
            for k in range(KT):
                mm = pe.matmul(W[4][:, :], beta_w[:, k * P:(k + 1) * P], f32(wq[:, k, :]), start=(k == 0),
                               stop=(k == KT - 1))
            mm.then_inc(bias_mm, 1)
            pe.wait_ge(r_done, KT)
            keep_warm(10)
            mix_out(0, True)

            FILLS = ((6, 4, 6, 0, 4, 2, 4, 2, 2, 2, 0), (1, 0, 5, 1, 2, 1, 2, 2, 0, 1, 1))
            WARM = ((13, 6, 14, 0, 6, 0, 10, 6, 0, 0, 0), (0, 0, 8, 0, 0, 5, 3, 12, 0, 1, 0))
            assert sum(FILLS[0]) + sum(FILLS[1]) == 12 * KT

            def back(i, b, with_gates):
                n = i * 2 + (b - 2)
                at = [sum(FILLS[0]) * b]
                fills = (FILLS if with_gates else WARM)[b]

                def fill(count):
                    if with_gates:
                        gates(i, at[0], count)
                        at[0] += count
                    else:
                        keep_warm(count)

                fill(fills[0])
                projections(n, b, fill, fills[9])
                turn_g(n, b)
                fill(fills[1])
                scores(n)
                fill(fills[2])
                turn_prob(n)
                fill(fills[3])
                attend(n)
                fill(fills[4])
                mean_over(n)
                fill(fills[5])
                second_over(n)
                fill(fills[6])
                attn_out(n)
                fill(fills[7])
                if b == 0:
                    pe.wait_ge(fx_lo_done, (n + 1) * ST + ST)
                    project_high(4, 2, fh)
                    project_low(4, 2, fl, g_mm)
                turn_z(n)
                fill(fills[8])
                feed(n)
                fill(fills[10])

            def step(i, load_next):
                back(i, 0, True)
                back(i, 1, True)
                mix_out(i, load_next)

            with pe.Fori(1, PAIRS - 1) as i:
                step(i, True)
            step(PAIRS - 1, False)
            back(PAIRS, 0, False)
            back(PAIRS, 1, False)

        @block.vector
        def _(dve):
            def stats(raw, mv, tile, count, mv_done, first):
                for q in range(count):
                    dve.bn_stats(raw[:, q, :], tile(q))
                dve.drain()
                for q in range(count):
                    dve.bn_aggr(mv[:, q, :], raw[:, q, :]).then_inc(mv_done, 1)
                dve.wait_ge(mv_done, first + count)

            def variance(ve, mv, ve_done, mul, add):
                dve.tensor_scalar(ve, mv[:, :, 1], mul, add, ALU.mult, ALU.add).then_inc(ve_done, 1)

            def stats_x(t):
                dve.wait_ge(x_here, t * 16 + 16)
                stats(a_raw, a_mv, lambda q: x_in[:, q, :], QT, a_mv_done, t * QT)
                variance(a_ve, a_mv, a_ve_done, 1.0, EPS)

            def shift_x(t):
                dve.wait_ge(a_rstd_done, t + 1)
                dve.scalar_tensor_tensor(out=a_nb[:, :], in0=a_mv[:, :, 0], scalar=-1.0, in1=a_rstd[:, :],
                                         op0=ALU.mult, op1=ALU.mult).then_inc(a_nb_done, 1)

            def xt_low(t, tiles):
                for k in tiles:
                    dve.wait_ge(xt_hi_done, t * KT + (k + 1))
                    dve.tensor_tensor(xt_lo[:, k, :], XT[k][:, :], f32(xt_hi[:, k, :]), ALU.subtract)\
                       .then_inc(xt_lo_done, 1)

            def gate(t, m, e, tile, tanh_done, done):
                dve.wait_ge(tanh_done, t * KT + (e + 1))
                dve.scalar_tensor_tensor(out=tile[:, e, :], in0=tile[:, e, :], scalar=1.0,
                                         in1=Z[TURN[m, e] % 3][:, :], op0=ALU.add, op1=ALU.mult).then_inc(done, 1)

            def gate_r(t, e):
                gate(t, R, e, r2, tr_done, r_done)

            def gate_c(t, e):
                gate(t, C, e, cs, tc_done, c_done)

            def up0_left(t, e):
                fa, ca, fb, cb, product = of_tile(up_nodes(0), e)
                dve.wait_ge(f_done, t * KT + (e + 1))
                dve.wait_ge(c_done, t * KT + (e + 1))
                dve.scalar_tensor_tensor(out=cb, in0=fb, scalar=-1.0, in1=cb, op0=ALU.add, op1=ALU.mult)\
                   .then_inc(up0_g, 1)

            def up0_join(t, e):
                fa, ca, fb, cb, product = of_tile(up_nodes(0), e)
                dve.wait_ge(up0_t, t * KT + (e + 1))
                dve.wait_ge(up0_g, t * KT + (e + 1))
                dve.tensor_tensor(cb, product, cb, ALU.subtract).then_inc(up0_c, 1)

            def up_left(t, l):
                step = 2 << l
                f, c = level(fs, step - 1, step // 2), level(cs, step - 1, step // 2)
                dve.wait_ge(up_t, t * (TOP - 1) + l)
                dve.scalar_tensor_tensor(out=c, in0=f, scalar=-1.0, in1=c, op0=ALU.add, op1=ALU.mult)\
                   .then_inc(up_g, 1)

            def up(t, l):
                up_product_c(dve, t, l)
                up_left(t, l)
                if l > 1:
                    up_product_f(dve, t, l)
                up_join(dve, t, l)

            def even_product(t, e):
                f, c, before, product = of_tile(down_nodes(0), e)
                dve.wait_ge(down_h, t * (LEVELS - 2) + (LEVELS - 2))
                dve.tensor_tensor(product, f, before, ALU.mult).then_inc(down0_t, 1)

            def even_join(t, e):
                f, c, before, product = of_tile(down_nodes(0), e)
                g = gs[:, e, :].rearrange("p (s n) -> p s n", n=S // 2)[:, :, 1:]
                dve.wait_ge(down0_t, t * KT + (e + 1))
                dve.wait_ge(g0_done, t * KT + KT)
                dve.tensor_tensor(c, product, g, ALU.subtract).then_inc(down0_h, 1)

            def rh_product(t, e):
                dve.wait_ge(down0_h, t * KT + (e + 1))
                dve.wait_ge(r_done, t * KT + (e + 1))
                dve.tensor_tensor(r2[:, e, :], r2[:, e, :], cs[:, e, :], ALU.mult).then_inc(rh_done, 1)

            def rh_low(t, e):
                dve.wait_ge(rh_hi_done, t * KT + (e + 1))
                dve.tensor_tensor(rh_lo[:, e, :], r2[:, e, :], f32(rh_hi[:, e, :]), ALU.subtract)\
                   .then_inc(rh_lo_done, 1)

            def mix(t):
                even_product(t, 0)
                even_product(t, 1)
                even_join(t, 0)
                even_join(t, 1)
                rh_product(t, 0)
                even_product(t, 2)
                rh_product(t, 1)
                even_product(t, 3)
                even_join(t, 2)
                even_join(t, 3)
                rh_product(t, 2)
                if not (isinstance(t, int) and t == 0):
                    gate_r(t, KT - 1)
                rh_low(t, 1)
                rh_product(t, 3)
                rh_low(t, 2)
                rh_low(t, 3)

            def residual_1(t, b):
                dve.wait_ge(m_rstd_done, t + 1)
                dve.wait_ge(res_here[b], t * 16 + 16)
                for q in range(b * ST, (b + 1) * ST):
                    dve.wait_ge(wo_mm, t * QT + (q + 1))
                    dve.scalar_tensor_tensor(out=res[:, q, :], in0=Y[q][:, :], scalar=m_rstd[:, q:q + 1],
                                             in1=res[:, q, :], op0=ALU.mult, op1=ALU.add,
                                             accum_out=b_sum[:, q:q + 1]).then_inc(x1_done, 1)
                part = slice(b * ST, (b + 1) * ST)
                dve.wait_ge(x1_done, t * QT + (b * ST + ST))
                dve.tensor_scalar(b_mean[:, part], b_sum[:, part], 1.0 / D, None, ALU.mult).then_inc(b_mean_done, 1)

            def variance_b(n, b):
                part = slice(b * ST, (b + 1) * ST)
                dve.wait_ge(b_sq_done, n * ST + ST)
                dve.tensor_scalar(b_ve[:, part], b_ve[:, part], 1.0 / D, EPS, ALU.mult, ALU.add)\
                   .then_inc(b_ve_done, 1)

            def shift_b(n, b):
                part = slice(b * ST, (b + 1) * ST)
                dve.wait_ge(b_rstd_done, n + 1)
                dve.scalar_tensor_tensor(out=b_nb[:, part], in0=b_mean[:, part], scalar=-1.0, in1=b_rstd[:, part],
                                         op0=ALU.mult, op1=ALU.mult).then_inc(b_nb_done, 1)

            def fx_low(n, rows):
                for s in rows:
                    dve.wait_ge(fx_hi_done, n * ST + (s + 1))
                    dve.tensor_tensor(fx_lo[:, s, :], tt[:, s, :], f32(fx_hi[:, s, :]), ALU.subtract)\
                       .then_inc(fx_lo_done, 1)

            def finish(t, load_next, last=None):
                mix(t)
                if last is None:
                    dve.wait_ge(bias_mm, 1)
                    dve.wait_ge(wide_here, 16 * 4)
                    dve.tensor_tensor(bias_bc[:, :], W[4][:, :], bias_bc[:, :], ALU.add).then_inc(bias_done, 1)
                else:
                    residual_3(last)
                dve.wait_ge(hsq_mm, t + 1)
                dve.tensor_scalar(m_ve[:, :], W[4][:, 0:QT], P / (4 * D), EPS, ALU.mult, ALU.add)\
                   .then_inc(m_ve_done, 1)
                residual_1(t, 0)
                if load_next:
                    xt_low(t + 1, range(0, 2))
                variance_b(t * 2, 0)
                if load_next:
                    xt_low(t + 1, range(2, 3))
                shift_b(t * 2, 0)
                if load_next:
                    xt_low(t + 1, range(3, 4))
                residual_1(t, 1)
                fx_low(t * 2, range(ST))
                variance_b(t * 2 + 1, 1)

            def phi_low(n):
                dve.wait_ge(ph_hi_done, n + 1)
                dve.scalar_tensor_tensor(out=ph_lo[:, :], in0=W[3][:, :], scalar=phi_bc, in1=f32(ph_hi[:, :]),
                                         op0=ALU.add, op1=ALU.subtract).then_inc(ph_lo_done, 1)

            def theta_low(n):
                dve.wait_ge(th_hi_done, n + 1)
                dve.scalar_tensor_tensor(out=th_lo[:, :], in0=W[0][:, :], scalar=theta_bc, in1=f32(th_hi[:, :]),
                                         op0=ALU.add, op1=ALU.subtract).then_inc(th_lo_done, 1)

            def g_low(n):
                dve.wait_ge(g_hi_done, n + 1)
                dve.tensor_tensor(g_lo[:, :, :].rearrange("p j l -> p (j l)"), W[2][:, :],
                                  f32(g_hi[:, :, :]).rearrange("p j l -> p (j l)"), ALU.subtract)\
                   .then_inc(g_lo_done, 1)

            def row_max(n, k):
                dve.wait_ge(score_mm, n * KT + (k + 1))
                dve.tensor_reduce(nmax[:, k:k + 1], SC[k][:, :], AX.X, ALU.max, negate=True).then_inc(nmax_done, 1)

            def row_norm(n, k):
                dve.wait_ge(exp_done, n * KT + (k + 1))
                dve.reciprocal(rinv[:, k:k + 1], rsum[:, k:k + 1]).then_inc(rinv_done, 1)

            def row_scale(n, k):
                dve.wait_ge(rinv_done, n * KT + (k + 1))
                dve.tensor_scalar(prob[:, k, :], prob[:, k, :], rinv[:, k:k + 1], None, ALU.mult)\
                   .then_inc(prob_done, 1)

            def softmax(n):
                row_max(n, 0)
                row_max(n, 1)
                row_max(n, 2)
                row_norm(n, 0)
                row_max(n, 3)
                row_norm(n, 1)
                row_scale(n, 0)
                row_scale(n, 1)
                row_norm(n, 2)
                row_scale(n, 2)
                row_norm(n, 3)
                row_scale(n, 3)

            def pt_low(n, tiles=range(KT)):
                for k in tiles:
                    dve.wait_ge(pt_hi_done, n * KT + (k + 1))
                    dve.tensor_tensor(pt_lo[:, k, :], W[k][:, :], f32(pt_hi[:, k, :]), ALU.subtract)\
                       .then_inc(pt_lo_done, 1)

            def t_mean(n):
                dve.wait_ge(av_mm, n + 1)
                dve.bn_stats(t_raw[:, :], W[4][:, :]).then_inc(t_raw_done, 1)
                dve.wait_ge(t_raw_done, n + 1)
                dve.memset(t_s[:, 1:2], 0.0)
                dve.bn_aggr(t_mv[:, :], t_raw[:, :]).then_inc(t_mv_done, 1)
                dve.wait_ge(t_mv_done, n + 1)
                dve.tensor_scalar(t_s[:, 0:1], t_mv[:, 0:1], g_bc, None, ALU.add).then_inc(t_mean_done, 1)

            def t_second(n):
                dve.wait_ge(mean_mm, n + 1)
                dve.tensor_scalar(t_s[:, 1:2], t_s[:, 0:1], W[0][:, 0:1], None, ALU.subtract).then_inc(t_dist_done, 1)
                dve.tensor_scalar(t_s[:, 3:4], g_bc, W[0][:, 0:1], None, ALU.subtract).then_inc(t_dist_done, 1)
                dve.wait_ge(t_dist_done, n * 2 + 2)
                dve.scalar_tensor_tensor(out=t_s[:, 2:3], in0=t_s[:, 1:2], scalar=t_s[:, 1:2], in1=t_mv[:, 1:2],
                                         op0=ALU.mult, op1=ALU.add).then_inc(t_sec_done, 1)
                dve.scalar_tensor_tensor(out=gt[:, :], in0=W[4][:, :], scalar=t_s[:, 3:4], in1=gamma_lt[:, :],
                                         op0=ALU.add, op1=ALU.mult).then_inc(t_gam_done, 1)

            def t_var(n):
                dve.wait_ge(sec_mm, n + 1)
                dve.tensor_scalar(t_s[:, 4:5], W[3][:, 0:1], EPS, None, ALU.add).then_inc(t_ve_done, 1)

            def t_norm(n):
                dve.wait_ge(t_rstd_done, n + 1)
                dve.wait_ge(t_gam_done, n + 1)
                dve.scalar_tensor_tensor(out=gt[:, :], in0=gt[:, :], scalar=t_s[:, 5:6], in1=beta_lt[:, :],
                                         op0=ALU.mult, op1=ALU.add).then_inc(t_bet_done, 1)

            def relu_low(n):
                dve.wait_ge(relu_hi_done, n + 1)
                dve.scalar_tensor_tensor(out=th_lo[:, :], in0=gt[:, :], scalar=0.0, in1=f32(th_hi[:, :]),
                                         op0=ALU.max, op1=ALU.subtract).then_inc(relu_lo_done, 1)

            def residual_2(n, b):
                dve.wait_ge(cx_done, n + 1)
                for o in range(ST):
                    dve.wait_ge(out_mm, n * ST + (o + 1))
                    dve.scalar_tensor_tensor(out=res[:, b * ST + o, :], in0=W[1 + o][:, :],
                                             scalar=out_bc[:, o:o + 1], in1=cx[:, o, :],
                                             op0=ALU.add, op1=ALU.add, accum_out=c_sum[:, o:o + 1])\
                       .then_inc(x2_done, 1)

            def stats_c(n, b):
                for s in range(ST):
                    dve.wait_ge(x2_done, n * ST + (s + 1))
                    dve.tensor_scalar(c_mean[:, s:s + 1], c_sum[:, s:s + 1], 1.0 / D, None, ALU.mult)\
                       .then_inc(c_mean_done, 1)
                for s in range(ST):
                    dve.wait_ge(c_mean_done, n * ST + (s + 1))
                    dve.scalar_tensor_tensor(out=fz[:, s, :], in0=res[:, b * ST + s, :], scalar=c_mean[:, s:s + 1],
                                             in1=gamma_bc[:, :], op0=ALU.subtract, op1=ALU.mult)\
                       .then_inc(zg_done, 1)

            def variance_c(n):
                dve.wait_ge(c_sq_done, n * ST + ST)
                dve.tensor_scalar(c_ve, c_ve, (1.0 + EPS) / D, EPS * EPS, ALU.mult, ALU.add).then_inc(c_ve_done, 1)

            def z_low(n):
                for c, w in enumerate((W[3], W[0])):
                    dve.wait_ge(z_hi_done, n * 2 + (c + 1))
                    dve.tensor_tensor(cz_lo[:, c * D:(c + 1) * D], w[:, :], f32(cz_hi[:, c * D:(c + 1) * D]),
                                      ALU.subtract).then_inc(z_lo_done, 1)

            def residual_3(n):
                dve.wait_ge(fin_done, n * ST + ST)
                dve.wait_ge(c_rstd_done, n + 1)
                for s in range(ST):
                    dve.wait_ge(ffn_mm, n * ST + (s + 1))
                    dve.scalar_tensor_tensor(out=fin[:, s, :], in0=W[1 + s][:, :], scalar=c_rstd[:, s:s + 1],
                                             in1=fin[:, s, :], op0=ALU.mult, op1=ALU.add).then_inc(x3_done, 1)

            stats_x(0)
            shift_x(0)
            dve.wait_ge(a_nb_done, 1)
            for q in range(ST, QT):
                dve.tensor_scalar(x_in[:, q, :], x_in[:, q, :], a_rstd[:, q:q + 1], a_nb[:, q:q + 1],
                                  ALU.mult, ALU.add).then_inc(xn_done, 1)
            for k in range(KT):
                dve.wait_ge(w_hi_done, k + 1)
                dve.tensor_tensor(w_lo[F][:, k, :], prob[:, k, :], f32(w_hi[F][:, k, :]), ALU.subtract)\
                   .then_inc(w_lo_done, 1)
            xt_low(0, range(KT))
            for k in range(KT):
                dve.wait_ge(w_hi_done, KT + k + 1)
                dve.tensor_tensor(w_lo[C][:, k, :], (cx if k < 2 else fin)[:, k % 2, :], f32(w_hi[C][:, k, :]),
                                  ALU.subtract).then_inc(w_lo_done, 1)
            for k in range(KT):
                dve.wait_ge(w_hi_done, 2 * KT + k + 1)
                dve.tensor_tensor(w_lo[R][:, k, :], res[:, k, :], f32(w_hi[R][:, k, :]), ALU.subtract)\
                   .then_inc(w_lo_done, 1)
            gate_c(0, 0)
            up0_left(0, 0)
            dve.wait_ge(small_here, 16 * 6)
            dve.tensor_scalar(scale_bc, scale_bc, 0.25, None, ALU.mult).then_inc(col_done, 1)
            stats_x(1)
            gate_c(0, 1)
            up0_left(0, 1)
            dve.wait_ge(q_here, 16)
            dve.tensor_reduce(abs_sum, prob[:, :, :], AX.XY, ALU.add, apply_absolute_value=True).then_inc(abs_done, 1)
            shift_x(1)
            up0_join(0, 0)
            gate_c(0, 2)
            up0_left(0, 2)
            up0_join(0, 1)
            dve.wait_ge(abs_mean, 1)
            half = 0.5 / (D * D // P)
            dve.tensor_scalar(thr, W[0][:, 0:1], half, 0.5 * Q_EPS, ALU.mult, ALU.add).then_inc(thr_done, 1)
            dve.tensor_scalar(neg_thr, W[0][:, 0:1], -half, -0.5 * Q_EPS, ALU.mult, ALU.add).then_inc(thr_done, 1)
            dve.wait_ge(thr_done, 2)

            def ternary(o):
                need(dve, q_done, o)
                dve.tensor_scalar(gt[:, :], prob[:, o, :], neg_thr, None, ALU.is_lt).then_inc(below_done, 1)
                dve.wait_ge(below_done, o + 1)
                dve.scalar_tensor_tensor(out=prob[:, o, :], in0=prob[:, o, :], scalar=thr, in1=gt[:, :],
                                         op0=ALU.is_gt, op1=ALU.subtract).then_inc(q_done, 1)

            ternary(0)
            ternary(1)
            up0_join(0, 2)
            gate_c(0, 3)
            up0_left(0, 3)
            ternary(2)
            up0_join(0, 3)
            up_product_c(dve, 0, 1)
            up_left(0, 1)
            up_product_f(dve, 0, 1)
            up_join(dve, 0, 1)
            gate_r(0, 0)
            up(0, 2)
            up(0, 3)
            ternary(3)
            for c in range(2):
                dve.wait_ge(pj_hi_done, c + 1)
                dve.tensor_tensor(pj_lo[:, 2 * c:2 * c + 2, :].rearrange("p m n -> p (m n)"), W[c][:, :],
                                  f32(pj_hi[:, 2 * c:2 * c + 2, :]).rearrange("p m n -> p (m n)"), ALU.subtract)\
                   .then_inc(pj_lo_done, 1)
            dve.wait_ge(const_done, 3)
            for k in range(KT):
                dve.tensor_scalar(beta_w[:, k * P:(k + 1) * P], avg[:, :], beta_c[:, k:k + 1], float(P),
                                  ALU.mult, ALU.mult).then_inc(beta_done, 1)
            gate_r(0, 1)
            gate_r(0, 2)
            for k in range(KT):
                dve.wait_ge(w_hi_done, 3 * KT + k + 1)
                dve.scalar_tensor_tensor(out=wo_lo[:, k, :], in0=res[:, k, :], scalar=scale_bc[:, k:k + 1],
                                         in1=f32(wo_hi[:, k, :]), op0=ALU.mult, op1=ALU.subtract)\
                   .then_inc(w_lo_done, 1)
            gate_r(0, 3)
            down(dve, 0, 2)
            down(dve, 0, 1)
            finish(0, True)

            def back(i, b, gates, load_next):
                n = i * 2 + (b - 2)
                first, second = gates and b == 0, gates and b == 1
                if first:
                    if load_next:
                        stats_x(i + 1)
                        shift_x(i + 1)
                    gate_c(i, 0)
                if b == 0:
                    shift_b(n + 1, 1)
                if b:
                    residual_3(n - 1)
                    dve.wait_ge(ctx_hi_done, n * ST + ST)
                    ctx_lower(dve, 1)
                if second:
                    up0_join(i, 3)
                    up_product_c(dve, i, 1)
                phi_low(n)
                if second:
                    up_left(i, 1)
                theta_low(n)
                g_low(n)
                if first:
                    up0_left(i, 0)
                softmax(n)
                if second:
                    up_product_c(dve, i, 2)
                    up_left(i, 2)
                    pt_low(n, [0])
                    up_product_f(dve, i, 2)
                    pt_low(n, [1])
                    up_join(dve, i, 2)
                    pt_low(n, [2])
                    up_product_c(dve, i, 3)
                    pt_low(n, [3])
                    up_left(i, 3)
                    up_product_f(dve, i, 3)
                    up_join(dve, i, 3)
                else:
                    pt_low(n)
                if first:
                    gate_c(i, 1)
                    up0_left(i, 1)
                t_mean(n)
                t_second(n)
                t_var(n)
                if second:
                    gate_r(i, 0)
                if b == 0:
                    fx_low(n + 1, [0])
                t_norm(n)
                if b == 0:
                    fx_low(n + 1, [1])
                if second:
                    gate_r(i, 1)
                relu_low(n)
                if second:
                    gate_r(i, 2)
                if first:
                    gate_c(i, 2)
                residual_2(n, b)
                stats_c(n, b)
                if first:
                    up0_left(i, 2)
                    up0_join(i, 0)
                    up0_join(i, 1)
                    up0_join(i, 2)
                if second:
                    down(dve, i, 2)
                variance_c(n)
                z_low(n)
                if first:
                    gate_c(i, 3)
                    up0_left(i, 3)
                if second:
                    down(dve, i, 1)

            def step(i, load_next):
                back(i, 0, True, load_next)
                back(i, 1, True, load_next)
                finish(i, load_next, i * 2 - 1)

            with dve.Fori(1, PAIRS - 1) as i:
                step(i, True)
            step(PAIRS - 1, False)
            back(PAIRS, 0, False, False)
            back(PAIRS, 1, False, False)
            residual_3(2 * PAIRS - 1)


_INS = ['x', 'ctx_2048', 'L0_attn_Wr', 'L0_attn_Wf', 'L0_attn_Wc', 'L0_attn_Wo', 'L0_attn_ln_scale',
        'L0_xattn_theta_w', 'L0_xattn_theta_b', 'L0_xattn_phi_w', 'L0_xattn_phi_b', 'L0_xattn_g_w',
        'L0_xattn_g_b', 'L0_xattn_ln_gamma', 'L0_xattn_ln_beta', 'L0_xattn_out_w', 'L0_xattn_out_b',
        'L0_ffn_weight', 'L0_ffn_bias', 'L0_ffn_ln_gamma', 'L0_ffn_ln_beta']
_OUT = ((16, 256, 512), 'float32')


def kernel(**inputs):
    import numpy as _np
    import concourse.bacc as _bacc
    from concourse import mybir as _mybir
    from concourse.bass_utils import run_bass_kernel_spmd as _run

    nc = _bacc.Bacc("TRN2", target_bir_lowering=False, num_devices=1)
    arrays, args = {}, []
    for name in _INS:
        a = _np.ascontiguousarray(inputs[name])
        arrays[f"in_{name}_dram"] = a
        args.append(nc.dram_tensor(f"in_{name}_dram", a.shape, _mybir.dt.from_np(a.dtype), kind="ExternalInput").ap())
    shape, dtype = _OUT
    args.append(nc.dram_tensor("out_0_dram", shape, _mybir.dt.from_np(_np.dtype(dtype)), kind="ExternalOutput").ap())
    build(nc, *args)
    r = _run(nc, [arrays], core_ids=[0])
    return r.results[0]["out_0_dram"]
```
